# Optimizing a Trainium2 kernel written in Bass

```python
import numpy as np
import jax
import jax.numpy as jnp

def _softmax(x, axis=-1):
    return jax.nn.softmax(x, axis=axis)

def _gelu(x):
    return jax.nn.gelu(x, approximate=True)

def _silu(x):
    return jax.nn.silu(x)

def _sigmoid(x):
    return jax.nn.sigmoid(x)

def _layernorm(x, axis=-1, eps=1e-05):
    m = jnp.mean(x, axis=axis, keepdims=True)
    v = jnp.var(x, axis=axis, keepdims=True)
    return (x - m) / jnp.sqrt(v + eps)

def _scatter_add(tgt, idx, src, axis=0):
    return tgt.at[idx].add(src)

def _segment_sum(src, seg, n):
    return jax.ops.segment_sum(src, seg, n)
kernel_name = 'mk_conv_attn_hybrid_d2_conv_nchw512_r2_e1adaa'

def setup_inputs(seed: int=0):
    np.random.seed(seed)
    _w = jnp.asarray

    def _rec_inputs():
        import jax
        import jax.numpy as jnp
        _gk = jax.random.key(seed)
        x = 7.22e-05 + 1 * jax.random.normal(jax.random.fold_in(_gk, 1), (4, 256, 32, 32), jnp.float32)
        return x
    x = _rec_inputs()

    def _L0_conv_setup():
        import jax, jax.numpy as jnp
        import numpy as np
        B, C, H, W = (4, 256, 32, 32)
        IC = C // 2
        EPS = 1e-05

        def _conv1x1(x, w, b=None):
            y = jnp.einsum('bchw,oc->bohw', x, w)
            if b is not None:
                y = y + b[None, :, None, None]
            return y
        key = jax.random.key(seed)
        ks = jax.random.split(key, 20)
        rn = lambda i, sh, s=0.02: jax.random.normal(ks[i], sh, jnp.float32) * s
        return {'xA': jax.random.normal(ks[0], (B, C, H, W), jnp.float32), 'wk': rn(1, (IC, C)), 'bk': rn(2, (IC,)), 'wv': rn(3, (IC, C)), 'bv': rn(4, (IC,)), 'wq': rn(5, (IC, C)), 'bq': rn(6, (IC,)), 'wwg': rn(7, (IC, IC)), 'bn1_g': jnp.ones((IC,), jnp.float32), 'bn1_b': rn(8, (IC,)), 'bn1_m': rn(9, (IC,)), 'bn1_v': jax.random.uniform(ks[10], (IC,), jnp.float32, 0.5, 1.5), 'wout': rn(11, (C, IC)), 'bout': rn(12, (C,)), 'bn2_g': jnp.ones((C,), jnp.float32), 'bn2_b': rn(13, (C,)), 'bn2_m': rn(14, (C,)), 'bn2_v': jax.random.uniform(ks[15], (C,), jnp.float32, 0.5, 1.5)}
    _L0_conv_all = _L0_conv_setup()
    _L0_conv_in = {k: v for k, v in _L0_conv_all.items() if k in ('wk', 'bk', 'wv', 'bv', 'wq', 'bq', 'wwg', 'bn1_g', 'bn1_b', 'bn1_m', 'bn1_v', 'wout', 'bout', 'bn2_g', 'bn2_b', 'bn2_m', 'bn2_v')}
    del _L0_conv_all

    def _L1_attn_setup():
        import jax, jax.numpy as jnp
        import numpy as np
        DIM = 256
        HEADS = 8
        B, N = (4, 1024)
        key = jax.random.key(seed)
        k1, k2, k3 = jax.random.split(key, 3)
        x = jax.random.normal(k1, (B, N, DIM), dtype=jnp.float32)
        w_qkv = jax.random.normal(k2, (DIM, 3 * DIM), dtype=jnp.float32) * DIM ** (-0.5)
        w_out = jax.random.normal(k3, (DIM, DIM), dtype=jnp.float32) * DIM ** (-0.5)
        b_out = jnp.zeros((DIM,), dtype=jnp.float32)
        return {'x': x, 'w_qkv': w_qkv, 'w_out': w_out, 'b_out': b_out}
    _L1_attn_all = _L1_attn_setup()
    _L1_attn_in = {k: v for k, v in _L1_attn_all.items() if k in ('w_qkv', 'w_out', 'b_out')}
    del _L1_attn_all

    def _L1_ffn_setup():
        import jax, jax.numpy as jnp
        import numpy as np
        NUM_EXPERTS = 8
        TOP_K = 2
        key = jax.random.key(seed)
        ks = jax.random.split(key, 6)
        d, h, E = (256, 1024, NUM_EXPERTS)
        s = 0.02
        return {'x': jax.random.normal(ks[0], (4, 2048, d), dtype=jnp.float32), 'Wr': jax.random.normal(ks[1], (d, E), dtype=jnp.float32) * s, 'W1': jax.random.normal(ks[2], (E, d, h), dtype=jnp.float32) * s, 'b1': jax.random.normal(ks[3], (E, h), dtype=jnp.float32) * s, 'W2': jax.random.normal(ks[4], (E, h, d), dtype=jnp.float32) * s, 'b2': jax.random.normal(ks[5], (E, d), dtype=jnp.float32) * s}
    _L1_ffn_all = _L1_ffn_setup()
    _L1_ffn_in = {k: v for k, v in _L1_ffn_all.items() if k in ('Wr', 'W1', 'b1', 'W2', 'b2')}
    del _L1_ffn_all
    return {'x': x, 'L0_conv_wk': _L0_conv_in['wk'], 'L0_conv_bk': _L0_conv_in['bk'], 'L0_conv_wv': _L0_conv_in['wv'], 'L0_conv_bv': _L0_conv_in['bv'], 'L0_conv_wq': _L0_conv_in['wq'], 'L0_conv_bq': _L0_conv_in['bq'], 'L0_conv_wwg': _L0_conv_in['wwg'], 'L0_conv_bn1_g': _L0_conv_in['bn1_g'], 'L0_conv_bn1_b': _L0_conv_in['bn1_b'], 'L0_conv_bn1_m': _L0_conv_in['bn1_m'], 'L0_conv_bn1_v': _L0_conv_in['bn1_v'], 'L0_conv_wout': _L0_conv_in['wout'], 'L0_conv_bout': _L0_conv_in['bout'], 'L0_conv_bn2_g': _L0_conv_in['bn2_g'], 'L0_conv_bn2_b': _L0_conv_in['bn2_b'], 'L0_conv_bn2_m': _L0_conv_in['bn2_m'], 'L0_conv_bn2_v': _L0_conv_in['bn2_v'], 'L1_attn_w_qkv': _L1_attn_in['w_qkv'], 'L1_attn_w_out': _L1_attn_in['w_out'], 'L1_attn_b_out': _L1_attn_in['b_out'], 'L1_ffn_Wr': _L1_ffn_in['Wr'], 'L1_ffn_W1': _L1_ffn_in['W1'], 'L1_ffn_b1': _L1_ffn_in['b1'], 'L1_ffn_W2': _L1_ffn_in['W2'], 'L1_ffn_b2': _L1_ffn_in['b2']}

def reference(x, L0_conv_wk, L0_conv_bk, L0_conv_wv, L0_conv_bv, L0_conv_wq, L0_conv_bq, L0_conv_wwg, L0_conv_bn1_g, L0_conv_bn1_b, L0_conv_bn1_m, L0_conv_bn1_v, L0_conv_wout, L0_conv_bout, L0_conv_bn2_g, L0_conv_bn2_b, L0_conv_bn2_m, L0_conv_bn2_v, L1_attn_w_qkv, L1_attn_w_out, L1_attn_b_out, L1_ffn_Wr, L1_ffn_W1, L1_ffn_b1, L1_ffn_W2, L1_ffn_b2):
    import jax
    import jax.numpy as jnp

    def _L0_conv_ref(xA, wk, bk, wv, bv, wq, bq, wwg, bn1_g, bn1_b, bn1_m, bn1_v, wout, bout, bn2_g, bn2_b, bn2_m, bn2_v):
        import jax, jax.numpy as jnp
        import numpy as np
        B, C, H, W = (4, 256, 32, 32)
        IC = C // 2
        EPS = 1e-05

        def _conv1x1(x, w, b=None):
            y = jnp.einsum('bchw,oc->bohw', x, w)
            if b is not None:
                y = y + b[None, :, None, None]
            return y
        b, c, h, w = xA.shape
        n = h * w
        k = _conv1x1(xA, wk, bk).reshape(b, IC, n)
        v = _conv1x1(xA, wv, bv).reshape(b, IC, n)
        q = _conv1x1(xA, wq, bq).reshape(b, IC, n)
        attn = jax.nn.softmax(jnp.einsum('bcn,bcm->bnm', v, q), axis=2)
        av = jnp.einsum('bcn,bnm->bcm', k, attn)
        avw = jnp.einsum('oc,bcn->bon', wwg, av)
        scale1 = bn1_g / jnp.sqrt(bn1_v + EPS)
        avw = (avw - bn1_m[None, :, None]) * scale1[None, :, None] + bn1_b[None, :, None]
        avw = avw.reshape(b, IC, h, w)
        o = _conv1x1(avw, wout, bout)
        scale2 = bn2_g / jnp.sqrt(bn2_v + EPS)
        o = (o - bn2_m[None, :, None, None]) * scale2[None, :, None, None] + bn2_b[None, :, None, None]
        return jax.nn.relu(o + xA)

    def _L1_attn_ref(x, w_qkv, w_out, b_out):
        import jax, jax.numpy as jnp
        import numpy as np
        DIM = 256
        HEADS = 8
        B, N = (4, 1024)
        b, n, dim = x.shape
        h = HEADS
        d = dim // h
        scale = dim ** (-0.5)
        qkv = x @ w_qkv
        qkv = qkv.reshape(b, n, 3, h, d).transpose(2, 0, 3, 1, 4)
        q, k, v = (qkv[0], qkv[1], qkv[2])
        dots = jnp.einsum('bhid,bhjd->bhij', q, k) * scale
        attn = jax.nn.softmax(dots, axis=-1)
        out = jnp.einsum('bhij,bhjd->bhid', attn, v)
        out = out.transpose(0, 2, 1, 3).reshape(b, n, dim)
        return out @ w_out + b_out

    def _L1_ffn_ref(x, Wr, W1, b1, W2, b2):
        import jax, jax.numpy as jnp
        import numpy as np
        NUM_EXPERTS = 8
        TOP_K = 2
        B, S, D = x.shape
        E = Wr.shape[1]
        flat = x.reshape(B * S, D)
        logits = flat @ Wr
        top_vals, top_idx = jax.lax.top_k(logits, TOP_K)
        top_w = jax.nn.softmax(top_vals, axis=-1)
        N = flat.shape[0]
        gates = jnp.zeros((N, E), dtype=flat.dtype).at[jnp.arange(N)[:, None], top_idx].add(top_w)
        out = jnp.zeros_like(flat)
        for e in range(E):
            hdn = jax.nn.gelu(flat @ W1[e] + b1[e], approximate=False)
            y = hdn @ W2[e] + b2[e]
            out = out + gates[:, e:e + 1] * y
        return out.reshape(B, S, D)

    def _gn(v, G=32, eps=1e-05):
        B_, C_, H_, W_ = v.shape
        g = v.reshape(B_, G, C_ // G, H_, W_)
        m = jnp.mean(g, axis=(2, 3, 4), keepdims=True)
        s = jnp.var(g, axis=(2, 3, 4), keepdims=True)
        return ((g - m) / jnp.sqrt(s + eps)).reshape(v.shape)

    def _ln_c(v, eps=1e-06):
        m = jnp.mean(v, axis=1, keepdims=True)
        s = jnp.var(v, axis=1, keepdims=True)
        return (v - m) / jnp.sqrt(s + eps)

    def _ln_t(v, eps=1e-05):
        m = jnp.mean(v, axis=-1, keepdims=True)
        s = jnp.var(v, axis=-1, keepdims=True)
        return (v - m) / jnp.sqrt(s + eps)

    def _to_tokens(v):
        B_, C_, H_, W_ = v.shape
        return v.reshape(B_, C_, H_ * W_).transpose(0, 2, 1)

    def _from_tokens(t, like):
        B_, C_, H_, W_ = like.shape
        return t.transpose(0, 2, 1).reshape(B_, C_, H_, W_)
    x = _L0_conv_ref(x, L0_conv_wk, L0_conv_bk, L0_conv_wv, L0_conv_bv, L0_conv_wq, L0_conv_bq, L0_conv_wwg, L0_conv_bn1_g, L0_conv_bn1_b, L0_conv_bn1_m, L0_conv_bn1_v, L0_conv_wout, L0_conv_bout, L0_conv_bn2_g, L0_conv_bn2_b, L0_conv_bn2_m, L0_conv_bn2_v)
    t = _to_tokens(x)
    t = t + _L1_attn_ref(_ln_t(t), L1_attn_w_qkv, L1_attn_w_out, L1_attn_b_out)
    t = t + _L1_ffn_ref(_ln_t(t), L1_ffn_Wr, L1_ffn_W1, L1_ffn_b1, L1_ffn_W2, L1_ffn_b2)
    x = _from_tokens(t, x)
    return x

_drawn_inputs = setup_inputs


def setup_inputs(seed=0):
    import zlib

    import numpy as np

    out = dict(_drawn_inputs(seed))
    spreads = {'L0_conv_bn1_g': (1.0, 0.6), 'L0_conv_bn2_g': (1.0, 0.6), 'L1_attn_b_out': (0.0, 0.1)}
    factors = {'L0_conv_wk': 8.0,
     'L0_conv_bk': 8.0,
     'L0_conv_wv': 8.0,
     'L0_conv_bv': 8.0,
     'L0_conv_wq': 8.0,
     'L0_conv_bq': 64.0,
     'L0_conv_wwg': 8.0,
     'L0_conv_bn1_b': 4.557,
     'L0_conv_bn1_m': 3.99,
     'L0_conv_bn1_v': 8.0,
     'L0_conv_wout': 4.014,
     'L0_conv_bn2_v': 5.229,
     'L1_ffn_b1': 7.943,
     'L1_ffn_b2': 2.81,
     'L0_conv_bout': 5.237,
     'L0_conv_bn2_b': 3.449,
     'L0_conv_bn2_m': 4.976}
    for name, (base, spread) in spreads.items():
        noise = np.random.default_rng([zlib.crc32(name.encode()), seed]).standard_normal(out[name].shape)
        drawn = base * np.exp(spread * noise) if base else spread * noise
        out[name] = jnp.asarray(drawn.astype(out[name].dtype))
    for name, factor in factors.items():
        out[name] = (out[name] * factor).astype(out[name].dtype)
    return out
```

```python
from contextlib import ExitStack

import concourse.bass as bass
from concourse import mybir

F32 = mybir.dt.float32
F16 = mybir.dt.float16
I32 = mybir.dt.int32
ALU = mybir.AluOpType
ACT = mybir.ActivationFunctionType
X_AXIS = mybir.AxisListType.X

P = 128
B, C, N = 4, 256, 1024
CC = C // P
NT = N // P
HALF = 512
IC = 128
HEADS, D = 8, 32
GH = 4
GROUPS = HEADS // GH
QK_ROWS = 3 * D
E, HID = 8, 1024
HC = HID // P
TT = 256
TILES = (2 * B * N) // TT + E - 1
REGION = B * N + TT
TABLE = TILES + 1
LOADS = 26
WSCALE = 64.0
MSCALE = 64.0
WE = 8192
BIG = 3.0e38
EPS = 1e-5


LOAD_GROUP = 16 * 10
MAX_FROM, MAX_EACH = 4, 3
MAX_AT = [[n for n in range(32) if MAX_FROM + n // MAX_EACH == st] for st in range(16)]

FREE = 1
PLACES = ("tk_made st_res1 pv_made fT_made st_v st_res0 rT_kept_v listed " 
          "hs_kept st_out0 st_out1 f_kept qhi_kept qlo_kept vt_kept_a vt_kept_v idx_kept " 
          "nrm_kept y_kept f_out st_q0 st_q1 y_made st_y0 st_y1")


def hybrid_block(nc, x, wk, bk, wv, bv, wq, bq, wwg, bn1_g, bn1_b, bn1_m, bn1_v, wout, bout,
                 bn2_g, bn2_b, bn2_m, bn2_v, w_qkv, w_out, b_out, wr, w1, b1, w2, b2, out):
    ctx = ExitStack()

    def sem(name):
        return ctx.enter_context(nc.semaphore(name))

    def scratch(name, shape, dt):
        return nc.dram_tensor(name, shape, dt, kind="Internal").ap()

    q_hi_d, q_lo_d = scratch("q_hi_d", (B * C, N), F16), scratch("q_lo_d", (B * C, N), F16)
    k_hi_d, k_lo_d = scratch("k_hi_d", (B * C, N), F16), scratch("k_lo_d", (B * C, N), F16)
    v_d = scratch("v_d", (B * N, C), F32)
    res0_d = scratch("res0_d", (B * N, C), F32)
    res1_d = scratch("res1_d", (B * N, C), F32)
    list_d = scratch("list_d", (E * REGION, 2 * C), F16)
    y_d = scratch("y_d", (TILES * TT, C), F32)
    last_d = scratch("last_d", (P, WE), F16)

    with ctx:
        def sb(name, shape, dt):
            return ctx.enter_context(nc.sbuf_tensor(name, shape, dt))

        WB = sb("WB", [P, E, WE], F16)
        WORK = sb("WORK", [P, 17664], F32)
        PP = [ctx.enter_context(nc.psum_tensor(f"PP{i}", [P, 2 * HALF], F32)) for i in range(4)]

        identf = sb("identf", [P, P], F32)
        ident16 = sb("ident16", [P, P], F16)
        below16 = sb("below16", [P, P], F16)
        ones16 = sb("ones16", [P, P], F16)
        onesf = sb("onesf", [P, D], F32)
        wr16 = sb("wr16", [P, CC, 2, E], F16)
        b1c = sb("b1c", [P, E, HC], F32)
        vec = sb("vec", [P, 32], F32)
        small = sb("small", [P, 8, 8], F32)
        bst = sb("bst", [P, NT, 6], F32)
        mv = sb("mv", [P, NT, 2], F32)
        nmax = sb("nmax", [P, NT], F32)
        rsum = sb("rsum", [P, NT], F32)
        rinv = sb("rinv", [P, NT], F32)
        mxp = sb("mxp", [P, 16, 2], F32)
        mx = sb("mx", [P, 2, 16], F32)
        nmr = sb("nmr", [16, P], F16)
        w8 = sb("w8", [P, E], F32)
        ebase = sb("ebase", [P, E], F32)
        pick1 = sb("pick1", [P, B * NT, E], F32)
        pick2 = sb("pick2", [P, B * NT, E], F32)
        rank = sb("rank", [P, B * NT, E], F32)
        gate1 = sb("gate1", [P, B * NT], F32)
        gate2 = sb("gate2", [P, B * NT], F32)
        idx = sb("idx", [P, 2, NT], I32)
        cum16 = sb("cum16", [P, NT + 1, E], F16)
        pick16 = sb("pick16", [P, NT, E], F16)
        rt = sb("rt", [P, 7, NT, E], F32)
        rs = sb("rs", [P, 6, NT], F32)

        def word_view(a, n):
            return WORK[:, a:a + n]

        o = [0]

        def take(n):
            o[0] += n
            assert o[0] <= 17664
            return word_view(o[0] - n, n)

        X = take(2048).rearrange("p (c n) -> p c n", c=CC)
        QV = take(2048)
        q_sb, v_sb = QV[:, 0:N], QV[:, N:2 * N]
        lnT = QV.rearrange("p (c n) -> p c n", c=CC)
        kT = take(1024)
        PA = take(3072)
        prob = [PA[:, i * N:(i + 1) * N] for i in range(3)]
        y1 = PA[:, 0:N]
        VT = PA[:, 0:2048].rearrange("p (t c) -> p t c", t=NT)
        tok = take(2048).rearrange("p (t c) -> p t c", t=NT)
        QS = take(2048)
        ln = QS.rearrange("p (t c) -> p t c", t=NT)
        qs = QS.bitcast(F16).rearrange("p (u s n) -> p u s n", u=2, s=2)
        kTs = take(384).rearrange("p (u o) -> p u o", u=3)
        stage = take(2048).rearrange("p (u n) -> p u n", u=2)
        wqkv_sb = take(1536).rearrange("p (c n) -> p c n", c=CC)
        wqT = take(256).rearrange("p (c n) -> p c n", c=CC)
        wvT = take(256).rearrange("p (c n) -> p c n", c=CC)
        kwT = take(256).rearrange("p (c n) -> p c n", c=CC)
        woT = take(256).rearrange("p (c n) -> p c n", c=CC)
        kb = take(128)
        bob = take(256)
        wq_raw, wv_raw, wk_raw = tok[:, 0, :], tok[:, 1, :], tok[:, 2, :]
        wo_raw = tok[:, 3, :].rearrange("p (c n) -> p c n", c=CC)
        wwg_raw, wwgT, bkr = tok[:, 4, 0:128], tok[:, 4, 128:256], tok[:, 5, 0:128]
        b1_raw = tok[0:E * HC, 7, 0:P]
        wr_raw = tok[:, 6, 0:16].rearrange("p (c e) -> p c e", c=CC)

        o[0] = 0
        QP = take(4096).bitcast(F16).rearrange("p (u f h n) -> p u f h n", u=2, f=2, h=GH)
        KP = take(4096).bitcast(F16).rearrange("p (u h n) -> p u h n", u=2, h=GH)
        VV = take(2048).rearrange("p (u j d) -> p u j d", u=2, j=NT)
        OS = take(2048).rearrange("p (g n) -> p g n", g=GROUPS)
        rin = take(512)
        t1 = take(2048).rearrange("p (t c) -> p t c", t=NT)
        rows = take(2048).bitcast(F16).rearrange("p (t s c) -> p t s c", t=NT, s=2)
        wo_sb = take(512).rearrange("p (c n) -> p c n", c=CC)
        LASTW = WB[:, E - 1, :]
        PR = LASTW.bitcast(F32).rearrange("p (u h n) -> p u h n", u=2, h=GH)
        ln32 = LASTW[:, 0:4096].bitcast(F32).rearrange("p (t c) -> p t c", t=NT)
        lnr = LASTW[:, 4096:8192].rearrange("p (t s n) -> p t s n", t=NT, s=4)

        o[0] = 0
        xs = [take(512).bitcast(F16).rearrange("p (a s c) -> p a s c", a=2, s=2) for _ in range(2)]
        xT = [take(512).bitcast(F16).rearrange("p (s n) -> p s n", s=4) for _ in range(2)]
        hid = [take(2048).rearrange("p (k n) -> p k n", k=HC) for _ in range(2)]
        hs = [take(2048).bitcast(F16).rearrange("p (s k n) -> p s k n", s=2, k=HC) for _ in range(2)]
        ysb = [take(512).rearrange("p (a c) -> p a c", a=2) for _ in range(2)]
        b2b = take(2048).rearrange("p (e c) -> p e c", e=E)
        zero = take(512).bitcast(F16).rearrange("p (a c) -> p a c", a=2)
        TB = take(2048)
        cnt, lists = TB[:, 0:8], TB[:, 8:16]
        incl, start = TB[:, 16:24], TB[:, 24:32]
        thr = TB[:, 32:48]
        seq, seqc = TB[:, 48:88], TB[:, 88:128]
        te, tk = TB[:, 128:168], TB[:, 168:208]
        one8 = TB[:, 208:216]
        cmp = TB[:, 256:256 + TABLE * E].rearrange("p (s e) -> p s e", s=TABLE)
        big = TB[:, 640:640 + 256].rearrange("p (t e) -> p t e", e=E)
        big2 = TB[:, 896:896 + 256].rearrange("p (t e) -> p t e", e=E)
        tile_e = TB[:, 1152:1152 + TABLE].bitcast(I32)
        tile_row = TB[:, 1192:1192 + TABLE].bitcast(I32)
        zrow = TB[:, 1232:1240].bitcast(I32)
        zrowf = TB[:, 1240:1248]
        slot = TB[:, 1248:1312].bitcast(I32).rearrange("p (k t) -> p k t", k=2)
        slotf = TB[:, 1312:1376].rearrange("p (k t) -> p k t", k=2)
        slot_now = TB[:, 1376:1392].bitcast(I32).rearrange("p (k t) -> p k t", k=2)
        o[0] = 0
        yg = [take(2048).rearrange("p (k t c) -> p k t c", k=2, t=4) for _ in range(2)]
        tf = [take(1024).rearrange("p (t c) -> p t c", t=4) for _ in range(2)]
        ob = [take(1024).rearrange("p (c n) -> p c n", c=CC) for _ in range(2)]

        def hidden_bank(k):
            return PP[k // 2 % 2][:, (k % 2) * HALF:(k % 2) * HALF + TT]

        def turned_bank(u):
            return PP[3][:, u * HALF:(u + 1) * HALF].bitcast(F16)

        S = {}

        def s(name):
            if name not in S:
                S[name] = sem(name)
            return S[name]

        for name in ("ld_w ld_x pool_const pe_prep dve_prep act_prep mv_prep "
                     "q_made v_made k_made q_kept v_kept k_kept sc_made max_kept exp_kept ks_kept "
                     "av_made y1_kept cv_made cv_kept x1_kept tk_made tk_kept_a tk_kept_v stat_kept "
                     "sd_kept ln_kept lnT_made lnT_kept_a lnT_kept_v qk_made qhi_kept qlo_kept vt_made "
                     "vt_kept_a vt_kept_v res0_kept st_res0 st_v st_q0 st_q1 "
                     "ld_stage0 ld_stage1 scaled split_hi split_lo st_last wts_split "
                     "ld_g0 ld_g1 ld_nm00 ld_nm01 ld_nm10 ld_nm11 st_made e_kept pv_made nrm_kept "
                     "c_made c_kept nm_kept nmT_made nmr_kept ld_wo ld_res0 pr_made stat1_kept "
                     "sd1_kept ln1_kept hi_kept rows_kept rT_made rT_kept_a rT_kept_v lg_made pick_kept "
                     "gexp_kept rk_made idx_kept st_list st_res1 phase_b cnt_made table_kept zero_kept "
                     "ld_last ld_b2 st_zero ld_xs0 ld_xs1 xT_made xT_kept h_made h_kept hs_kept "
                     "y_made y_kept st_y0 st_y1 slot_kept idx_now ld_y0 ld_y1 ld_t0 ld_t1 f_kept "
                     "fT_made f_out st_out0 st_out1 kone_kept scatter_on gather_on listed").split():
            s(name)

        block = ctx.enter_context(nc.Block())

        BQ, BV, BK, G1, BB1, M1, V1, S1, BE1 = range(9)
        BO, G2, BB2, M2, V2, S2, BE2 = (10 + 2 * i for i in range(7))

        @block.sync
        def _(sp):
            for name in PLACES.split():
                sp.sem_inc(s(name), FREE)
            col = lambda a: a.rearrange("(p o) -> p o", o=1)
            n_w = 0
            for dst, src in ((wq_raw, wq), (wv_raw, wv), (wk_raw, wk),
                             (wo_raw, wout.rearrange("(c p) i -> p c i", p=P)), (wwg_raw, wwg),
                             (wqkv_sb, w_qkv.rearrange("(c p) n -> p c n", p=P)),
                             (wr_raw, wr.rearrange("(c p) e -> p c e", p=P)),
                             (bob, b_out.rearrange("(o c) -> o c", o=1).broadcast_to((P, C))),
                             (b1_raw, b1.rearrange("e (k p) -> (e k) p", p=P)),
                             (vec[:, BQ:BQ + 1], col(bq)), (vec[:, BV:BV + 1], col(bv)),
                             (vec[:, BK:BK + 1], col(bk)), (vec[:, G1:G1 + 1], col(bn1_g)),
                             (vec[:, BB1:BB1 + 1], col(bn1_b)), (vec[:, M1:M1 + 1], col(bn1_m)),
                             (vec[:, V1:V1 + 1], col(bn1_v)),
                             *((vec[:, at + c:at + c + 1], col(src[c * P:(c + 1) * P]))
                               for at, src in ((BO, bout), (G2, bn2_g), (BB2, bn2_b), (M2, bn2_m), (V2, bn2_v))
                               for c in range(CC))):
                sp.dma_start(dst, src).then_inc(s("ld_w"), 16)
                n_w += 1
            assert n_w == LOADS
            xv = x.rearrange("b (c p) h w -> b p c (h w)", p=P)
            qk_d = ((q_hi_d, q_lo_d), (k_hi_d, k_lo_d))
            with sp.Fori(0, B) as b:
                sp.wait_ge(s("tk_made"), FREE + b * 2)
                sp.dma_start(X, xv[bass.ds(b, 1)].rearrange("o p c n -> p (o c) n")).then_inc(s("ld_x"), 16)
                sp.wait_ge(s("res0_kept"), b + 1)
                sp.dma_start(res0_d[bass.ds(b * N, N), :].rearrange("(t p) c -> p t c", p=P), tok)\
                  .then_inc(s("st_res0"), 16)
                for u in range(4):
                    sp.wait_ge(s("qlo_kept"), FREE + b * 4 + (u + 1))
                    for k in range(2):
                        dst = qk_d[u // 2][k][bass.ds(b * C + (u % 2) * P, P), :]
                        sp.dma_start(dst, qs[:, u % 2, k, :]).then_inc(s(f"st_q{u % 2}"), 16)
                sp.wait_ge(s("vt_kept_a"), FREE + b + 1)
                sp.wait_ge(s("vt_kept_v"), FREE + b + 1)
                sp.dma_start(v_d[bass.ds(b * N, N), :].rearrange("(t p) c -> p t c", p=P), VT)\
                  .then_inc(s("st_v"), 16)
            sp.wait_ge(s("st_res0"), FREE + 16 * B)
            sp.wait_ge(s("st_q0"), FREE + 64 * B)
            sp.wait_ge(s("st_q1"), FREE + 64 * B)
            sp.wait_ge(s("st_v"), FREE + 16 * B)
            sp.wait_ge(s("vt_made"), 2 * B)
            sp.wait_ge(s("split_lo"), 32)
            sp.dma_start(wo_sb, w_out.rearrange("(c p) n -> p c n", p=P)).then_inc(s("ld_wo"), 16)

            def load_group(b, g, par):
                ld = s(f"ld_g{par}")
                row = b * C + g * P
                for r, src in enumerate((q_hi_d, q_hi_d, q_lo_d)):
                    part = src[bass.ds(row, P), :].rearrange("(h d) (f n) -> d h f n", d=D, f=2)
                    for f in range(2):
                        sp.dma_start(QP[r * D:(r + 1) * D, par, f], part[:, :, f, :]).then_inc(ld, 16)
                for r, src in enumerate((k_hi_d, k_lo_d, k_hi_d)):
                    part = src[bass.ds(row, P), :].rearrange("(h d) n -> d h n", d=D)
                    sp.dma_start(KP[r * D:(r + 1) * D, par], part).then_inc(ld, 16)
                sp.dma_start(VV[:, par], v_d[bass.ds(b * N, N), g * P:(g + 1) * P]
                             .rearrange("(j p) d -> p j d", p=P)).then_inc(ld, 16)

            def store_max(par, f, b_next):
                sp.wait_ge(s("nmr_kept"), b_next)
                sp.dma_start(QP[QK_ROWS:QK_ROWS + 1, par, f].rearrange("o h n -> o (h n)"),
                             nmr[:, :]).then_inc(s(f"ld_nm{par}{f}"), 16)

            load_group(0, 0, 0)
            store_max(0, 0, 1)
            store_max(0, 1, 2)
            with sp.Fori(0, B) as b:
                sp.wait_ge(s("st_res1"), FREE + b * 16)
                sp.dma_start(t1, res0_d[bass.ds(b * N, N), :].rearrange("(t p) c -> p t c", p=P))\
                  .then_inc(s("ld_res0"), 16)
                for g in range(GROUPS):
                    sp.wait_ge(s("pv_made"), FREE + b * 32 + g * 16)
                    if g == 0:
                        load_group(b, 1, 1)
                    else:
                        load_group((b + 1) % B, 0, 0)
                    for f in range(2):
                        store_max(1 - g, f, b * 4 + (2 * g + f + 3))
                sp.wait_ge(s("ln1_kept"), b + 1)
                sp.dma_start(res1_d[bass.ds(b * N, N), :].rearrange("(t p) c -> p t c", p=P), t1)\
                  .then_inc(s("st_res1"), 16)
            sp.wait_ge(s("st_res1"), FREE + 16 * B)

            sp.wait_ge(s("st_last"), 16)
            sp.wait_ge(s("phase_b"), 1)
            sp.dma_start(LASTW, last_d[:, :]).then_inc(s("ld_last"), 16)
            sp.dma_start(b2b, b2.rearrange("(o e) c -> o e c", o=1).broadcast_to((P, E, C)))\
              .then_inc(s("ld_b2"), 16)
            sp.wait_ge(s("table_kept"), 1)
            sp.wait_ge(s("zero_kept"), 1)
            for e in range(E):
                r = sp.value_load(zrow[0:1, e:e + 1], min_val=0, max_val=E * REGION - TT)
                sp.dma_start(list_d[bass.ds(r, TT), :].rearrange("(a p) c -> p a c", p=P), zero)\
                  .then_inc(s("st_zero"), 16)
            sp.wait_ge(s("st_zero"), 16 * E)
            sp.wait_ge(s("st_list"), 16 * 2 * NT * B)

            def load_rows(t, u, n_before):
                r = sp.value_load(tile_row[0:1, t], min_val=0, max_val=E * REGION - TT)
                sp.dma_start(xs[u], list_d[bass.ds(r, TT), :].rearrange("(a p) (s c) -> p a s c", p=P, s=2))\
                  .then_inc(s(f"ld_xs{u}"), 16)

            load_rows(slice(0, 1), 0, 0)
            load_rows(slice(1, 2), 1, 0)
            with sp.Fori(0, (TILES - 1) // 2) as i:
                for u in range(2):
                    sp.wait_ge(s("xT_made"), i * 2 + (u + 1))
                    if u == 0:
                        load_rows(bass.ds(i * 2 + 2, 1), u, None)
                    else:
                        load_rows(bass.ds(i * 2 + 3, 1), u, None)
                    sp.wait_ge(s("y_kept"), FREE + i * 2 + (u + 1))
                    sp.dma_start(y_d[bass.ds(i * (2 * TT) + u * TT, TT), :]
                                 .rearrange("(a p) c -> p a c", p=P), ysb[u]).then_inc(s(f"st_y{u}"), 16)
            sp.wait_ge(s("y_kept"), FREE + TILES)
            sp.dma_start(y_d[(TILES - 1) * TT:TILES * TT, :].rearrange("(a p) c -> p a c", p=P), ysb[0])\
              .then_inc(s("st_y0"), 16)

            ov = out.rearrange("b (c p) h w -> b p c (h w)", p=P)
            with sp.Fori(0, B) as b:
                for f in range(2):
                    sp.wait_ge(s("fT_made"), FREE + b * 2)
                    sp.dma_start(tf[f], res1_d[bass.ds(b * N + f * HALF, HALF), :]
                                 .rearrange("(t p) c -> p t c", p=P)).then_inc(s(f"ld_t{f}"), 16)
                for f in range(2):
                    sp.wait_ge(s("f_out"), FREE + b * 2 + (f + 1))
                    sp.dma_start(ov[bass.ds(b, 1), :, :, f * HALF:(f + 1) * HALF]
                                 .rearrange("o p c n -> p (o c) n"), ob[f]).then_inc(s(f"st_out{f}"), 16)
            sp.wait_ge(s("st_out0"), FREE + 16 * B)
            sp.wait_ge(s("st_out1"), FREE + 16 * B)

        @block.gpsimd
        def _(pool):
            def one_where(m, op, base):
                pool.affine_select(out=m[:, :], in_=m[:, :], compare_op=op, fill=1.0, base=base,
                                   pattern=[[-1, P]], channel_multiplier=1)
            for m in (identf, ident16, below16):
                pool.memset(m[:, :], 0.0)
            pool.memset(ones16[:, :], 1.0)
            pool.memset(onesf[:, :], 1.0)
            pool.drain()
            one_where(identf, ALU.not_equal, 0)
            one_where(ident16, ALU.not_equal, 0)
            one_where(below16, ALU.is_ge, 0)
            for e in range(E):
                pool.memset(w8[:, e:e + 1], float(E - e))
                pool.memset(ebase[:, e:e + 1], float(REGION * e))
            pool.drain()
            pool.sem_inc(s("pool_const"), 1)

            parts = []
            for e in [E - 1] + list(range(E - 1)):
                for c in range(CC):
                    parts.append((e, w1[e].rearrange("(c p) n -> p c n", p=P)[:, c, :], c * HID, CC * HID))
                for c in range(2):
                    src = w2[e].rearrange("(k p) n -> p k n", p=P)[:, c * 4:c * 4 + 4, :]
                    parts.append((e, src, 2 * CC * HID + c * HID, HC * C))

            def load_part(i):
                dst = stage[:, i % 2, :]
                if parts[i][2] >= 2 * CC * HID:
                    dst = dst.rearrange("p (k n) -> p k n", k=4)
                pool.dma_start(dst, parts[i][1]).then_inc(s(f"ld_stage{i % 2}"), 16)

            load_part(0)
            load_part(1)
            for i, (e, _, at, gap) in enumerate(parts):
                hi, lo = WB[:, e, at:at + HID], WB[:, e, at + gap:at + gap + HID]
                w = stage[:, i % 2, :]
                pool.wait_ge(s(f"ld_stage{i % 2}"), 16 * (i // 2 + 1))
                pool.tensor_scalar(w, w, WSCALE, None, ALU.mult).then_inc(s("scaled"), 1)
                pool.wait_ge(s("scaled"), i + 1)
                pool.tensor_copy(hi, w).then_inc(s("split_hi"), 1)
                pool.wait_ge(s("split_hi"), i + 1)
                pool.tensor_tensor(lo, w, hi, ALU.subtract).then_inc(s("split_lo"), 1)
                pool.wait_ge(s("split_lo"), i + 1)
                if i + 2 < len(parts):
                    load_part(i + 2)
                if i == 3:
                    pool.dma_start(last_d[:, :], LASTW).then_inc(s("st_last"), 16)

            with pool.Fori(0, B) as b:
                pool.wait_ge(s("idx_kept"), FREE + b + 1)
                pool.sem_inc(s("scatter_on"), 1)
                for t in range(NT):
                    for k in range(2):
                        pool.indirect_dma_start(
                            list_d[:, :], bass.IndirectOffsetOnAxis(ap=idx[:, k, t:t + 1], axis=0),
                            rows[:, t].rearrange("p s c -> p (s c)"), None).then_inc(s("st_list"), 16)
                pool.wait_ge(s("st_list"), (b + 1) * (16 * 2 * NT))
                pool.sem_inc(s("listed"), 1)

            pool.wait_ge(s("phase_b"), 1)
            pool.wait_ge(s("st_res1"), FREE + 16 * B)
            pool.wait_ge(s("st_list"), 16 * 2 * NT * B)
            for k in range(B * N // TT):
                pool.memset(thr[:, k:k + 1], float(TT * k))
            pool.iota(seq.bitcast(I32), pattern=[[1, TABLE]], base=0, channel_multiplier=0)
            pool.memset(one8, 1.0)
            pool.memset(zero, 0.0)
            pool.drain()
            pool.sem_inc(s("zero_kept"), 1)

            pool.wait_ge(s("slot_kept"), 1)
            pool.wait_ge(s("st_y0"), FREE + 16 * ((TILES + 1) // 2))
            pool.wait_ge(s("st_y1"), FREE + 16 * (TILES // 2))
            with pool.Fori(0, B) as b:
                pool.wait_ge(s("idx_now"), b + 1)
                for f in range(2):
                    pool.wait_ge(s("f_kept"), FREE + b * 2)
                    pool.sem_inc(s("gather_on"), 1)
                    for t in range(4):
                        for k in range(2):
                            pool.indirect_dma_start(
                                yg[f][:, k, t], None, y_d[:, :],
                                bass.IndirectOffsetOnAxis(ap=slot_now[:, k, 4 * f + t:4 * f + t + 1], axis=0))\
                                .then_inc(s(f"ld_y{f}"), 16)

        @block.scalar
        def _(act):
            act.wait_ge(s("dve_prep"), 1)
            act.activation(vec[:, 24:27], vec[:, 24:27], ACT.Sqrt).then_inc(s("act_prep"), 1)
            act.wait_ge(s("dve_prep"), 2)
            with act.Fori(0, B) as b:
                act.wait_ge(s("q_made"), b + 1)
                act.activation(q_sb, PP[0][:, :], ACT.Identity, bias=vec[:, BQ:BQ + 1]).then_inc(s("q_kept"), 1)
                act.wait_ge(s("st_v"), FREE + b * 16)
                for i in range(NT):
                    act.wait_ge(s("max_kept"), b * NT + (i + 1))
                    if i >= 3:
                        act.wait_ge(s("av_made"), b * NT + (i - 2))
                    act.activation(prob[i % 3], PP[i % 3][:, :], ACT.Exp, bias=nmax[:, i:i + 1],
                                   accum_out=rsum[:, i:i + 1]).then_inc(s("exp_kept"), 1)
                for c in range(CC):
                    act.wait_ge(s("cv_kept"), b * 2 + (c + 1))
                    act.activation(X[:, c], X[:, c], ACT.Relu, bias=vec[:, BE2 + c:BE2 + c + 1])\
                       .then_inc(s("x1_kept"), 1)
                act.wait_ge(s("tk_made"), FREE + b * 2 + 1)
                act.wait_ge(s("st_res0"), FREE + b * 16)
                act.activation(tok[:, 0:4], PP[2][:, :].rearrange("p (t c) -> p t c", t=4), ACT.Copy)\
                   .then_inc(s("tk_kept_a"), 1)
                act.wait_ge(s("stat_kept"), b + 1)
                act.activation(small[:, 2], small[:, 1], ACT.Sqrt).then_inc(s("sd_kept"), 1)
                act.wait_ge(s("lnT_made"), b * 2 + 1)
                act.activation(lnT[:, 0], PP[0][:, :], ACT.Copy).then_inc(s("lnT_kept_a"), 1)
                for u in range(4):
                    act.wait_ge(s("qk_made"), b * 4 + (u + 1))
                    if u >= 2:
                        act.wait_ge(s(f"st_q{u % 2}"), FREE + b * 64 + 32)
                    act.activation(qs[:, u % 2, 0], PP[(u + 2) % 4][:, :], ACT.Copy,
                                   scale=C ** -0.5 if u < 2 else 1.0).then_inc(s("qhi_kept"), 1)
                act.wait_ge(s("vt_made"), b * 2 + 1)
                act.activation(VT[:, 0:4], PP[2][:, :].rearrange("p (t c) -> p t c", t=4), ACT.Copy)\
                   .then_inc(s("vt_kept_a"), 1)

            with act.Fori(0, B) as b:
                act.wait_ge(s("rT_kept_v"), FREE + b)
                for g in range(GROUPS):
                    for st in range(16):
                        if st < 2:
                            act.wait_ge(s("pv_made"), FREE + b * 32 + g * 16)
                        else:
                            act.wait_ge(s("pv_made"), FREE + b * 32 + (g * 16 + st - 1))
                        for pr in range(2):
                            act.wait_ge(s("st_made"), b * 64 + (g * 32 + st * 2 + pr + 1))
                            act.activation(PR[:, st % 2, 2 * pr:2 * pr + 2], PP[pr][:, :]
                                           .rearrange("p (h n) -> p h n", h=2), ACT.Exp).then_inc(s("e_kept"), 1)
                act.wait_ge(s("stat1_kept"), b + 1)
                act.activation(small[:, 2], small[:, 1], ACT.Sqrt).then_inc(s("sd1_kept"), 1)
                act.wait_ge(s("ln1_kept"), b + 1)
                act.wait_ge(s("listed"), FREE + b)
                act.activation(rows[:, :, 0, :], ln32, ACT.Copy).then_inc(s("hi_kept"), 1)
                act.wait_ge(s("rT_made"), b * 2 + 1)
                act.activation(lnr[:, 0:4], PP[2][:, :].bitcast(F16).rearrange("p (t s n) -> p t s n", t=4, s=4),
                               ACT.Copy).then_inc(s("rT_kept_a"), 1)
                act.wait_ge(s("pick_kept"), b + 1)
                act.activation(rs[:, 2], rs[:, 2], ACT.Exp, scale=1.0 / WSCALE).then_inc(s("gexp_kept"), 1)

            act.wait_ge(s("table_kept"), 1)

            def gelus(t, u, at):
                e = act.value_load(tile_e[0:1, at], min_val=0, max_val=E - 1)
                for k in range(HC):
                    act.wait_ge(s("h_made"), t * HC + (k + 1))
                    act.activation(hid[u][:, k], hidden_bank(k), ACT.Gelu,
                                   bias=b1c[:, bass.ds(e, 1), k], scale=1.0 / WSCALE)\
                       .then_inc(s("h_kept"), 1)

            gelus(0, 0, slice(0, 1))
            with act.Fori(0, (TILES - 1) // 2) as i:
                for u in (1, 0):
                    act.wait_ge(s("hs_kept"), FREE + i * 8 + (0 if u else 4))
                    gelus(i * 2 + (1 if u else 2), u, bass.ds(i * 2 + (1 if u else 2), 1))

            with act.Fori(0, B) as b:
                for f in range(2):
                    act.wait_ge(s("fT_made"), FREE + b * 2 + (f + 1))
                    act.wait_ge(s(f"st_out{f}"), FREE + b * 16)
                    act.activation(ob[f], PP[f][:, :].rearrange("p (c n) -> p c n", c=CC), ACT.Copy)\
                       .then_inc(s("f_out"), 1)

        @block.tensor
        def _(pe):
            def product(dst, pairs, sem_name=None):
                for n, (lhsT, rhs) in enumerate(pairs):
                    mm = pe.matmul(dst, lhsT, rhs, start=(n == 0), stop=(n == len(pairs) - 1))
                if sem_name:
                    mm.then_inc(s(sem_name), 1)

            pe.wait_ge(s("pool_const"), 1)
            pe.wait_ge(s("ld_w"), 16 * LOADS)
            for c in range(CC):
                cols = slice(c * P, (c + 1) * P)
                pe.transpose(PP[0][:, c * P:(c + 1) * P], wq_raw[:, cols], identf[:, :])
                pe.transpose(PP[0][:, 256 + c * P:256 + (c + 1) * P], wv_raw[:, cols], identf[:, :])
                pe.transpose(PP[0][:, 512 + c * P:512 + (c + 1) * P], wo_raw[:, c], identf[:, :])
            pe.transpose(PP[0][:, 896:896 + E * HC], b1_raw, identf[0:E * HC, 0:E * HC])
            pe.transpose(PP[0][:, 768:896], wwg_raw, identf[:, :]).then_inc(s("pe_prep"), 1)
            pe.wait_ge(s("dve_prep"), 1)
            for c in range(CC):
                product(PP[1][:, c * P:(c + 1) * P], [(wk_raw[:, c * P:(c + 1) * P], wwgT)])
            product(PP[1][:, 512:640], [(bkr, wwgT)], "pe_prep")
            pe.wait_ge(s("dve_prep"), 2)

            with pe.Fori(0, B) as b:
                def halves(dst, w, src, sem_name):
                    for h in range(2):
                        n = slice(h * HALF, (h + 1) * HALF)
                        product(dst[:, n], [(w(c), src[:, c, n]) for c in range(CC)],
                                sem_name if h else None)

                pe.wait_ge(s("ld_x"), b * 16 + 16)
                pe.wait_ge(s("qhi_kept"), FREE + b * 4)
                pe.wait_ge(s("qlo_kept"), FREE + b * 4)
                halves(PP[0], lambda c: wqT[:, c], X, "q_made")
                halves(PP[1], lambda c: wvT[:, c], X, "v_made")
                pe.wait_ge(s("vt_kept_a"), FREE + b)
                for t in range(NT):
                    n = slice(t * P, (t + 1) * P)
                    product(PP[2][:, n], [(X[:, c, n], kwT[:, c]) for c in range(CC)],
                            "k_made" if t == NT - 1 else None)

                def scores(i):
                    if i == 0:
                        pe.wait_ge(s("q_kept"), b + 1)
                        pe.wait_ge(s("v_kept"), b + 1)
                    elif i == 2:
                        pe.wait_ge(s("k_kept"), b + 1)
                    elif i >= 3:
                        pe.wait_ge(s("exp_kept"), b * NT + (i - 2))
                    for h in range(2):
                        product(PP[i % 3][:, h * HALF:(h + 1) * HALF],
                                [(v_sb[:, i * P:(i + 1) * P], q_sb[:, h * HALF:(h + 1) * HALF])],
                                "sc_made" if h else None)

                def weigh(i):
                    pe.wait_ge(s("exp_kept"), b * NT + (i + 1))
                    pe.wait_ge(s("ks_kept"), b * NT + (i + 1))
                    if i == 0:
                        pe.wait_ge(s("vt_kept_v"), FREE + b)
                    for h in range(2):
                        mm = pe.matmul(PP[3][:, h * HALF:(h + 1) * HALF], kTs[:, i % 3],
                                       prob[i % 3][:, h * HALF:(h + 1) * HALF],
                                       start=(i == 0), stop=(i == NT - 1))
                    mm.then_inc(s("av_made"), 1)

                scores(0)
                scores(1)
                for i in range(NT):
                    if i + 2 < NT:
                        scores(i + 2)
                    weigh(i)
                for c in range(CC):
                    for h in range(2):
                        pe.wait_ge(s("y1_kept"), b * 2 + (h + 1))
                        product(PP[c][:, h * HALF:(h + 1) * HALF], [(woT[:, c], y1[:, h * HALF:(h + 1) * HALF])],
                                "cv_made" if h else None)
                for t in range(NT):
                    for c in range(CC):
                        if t == 0:
                            pe.wait_ge(s("x1_kept"), b * 2 + (c + 1))
                        mm = pe.transpose(PP[2 + t // 4][:, (t % 4) * C + c * P:(t % 4) * C + (c + 1) * P],
                                          X[:, c, t * P:(t + 1) * P], identf[:, :])
                    if t % 4 == 3:
                        mm.then_inc(s("tk_made"), 1)
                for c in range(CC):
                    for t in range(NT):
                        pe.wait_ge(s("ln_kept"), b * NT + (t + 1)) if c == 0 else None
                        mm = pe.transpose(PP[c][:, t * P:(t + 1) * P], ln[:, t, c * P:(c + 1) * P], identf[:, :])
                    mm.then_inc(s("lnT_made"), 1)
                pe.wait_ge(s("lnT_kept_a"), b + 1)
                pe.wait_ge(s("lnT_kept_v"), b + 1)
                for u in range(4):
                    halves(PP[(u + 2) % 4], lambda c: wqkv_sb[:, c, u * P:(u + 1) * P], lnT, "qk_made")
                for t in range(NT):
                    if t % 4 == 0:
                        pe.wait_ge(s("qhi_kept"), FREE + b * 4 + (t // 4 + 1))
                        pe.wait_ge(s("qlo_kept"), FREE + b * 4 + (t // 4 + 1))
                    product(PP[2 + t // 4][:, (t % 4) * C:(t % 4 + 1) * C],
                            [(lnT[:, c, t * P:(t + 1) * P], wqkv_sb[:, c, 2 * C:3 * C]) for c in range(CC)],
                            "vt_made" if t % 4 == 3 else None)

            def max_pair(n, par, base):
                f, h, i = n // 16, n // 4 % 4, n % 4
                for k in range(2):
                    at = 2 * n + k
                    if not isinstance(base, int) or at >= 2:
                        pe.wait_ge(s("c_kept"), base + (at - 1))
                    mm = pe.matmul(PP[3][:, k * HALF:(k + 1) * HALF],
                                   QP[0:QK_ROWS, par, f, h, i * P:(i + 1) * P],
                                   KP[0:QK_ROWS, par, h, k * HALF:(k + 1) * HALF], start=True, stop=True)
                    mm.then_inc(s("c_made"), 1)

            def max_row(f, n_half):
                pe.wait_ge(s("nm_kept"), n_half)
                pe.transpose(PP[3][0:16, 0:P], mx[:, f], identf[:, :]).then_inc(s("nmT_made"), 1)

            pe.wait_ge(s("ld_g0"), LOAD_GROUP)
            for n in range(32):
                if n == 16:
                    max_row(0, 1)
                    pe.wait_ge(s("nmr_kept"), 1)
                max_pair(n, 0, 0)
            max_row(1, 2)

            with pe.Fori(0, B) as b:
                pe.wait_ge(s("idx_kept"), FREE + b)
                for g in range(GROUPS):
                    def weigh_heads(st):
                        f, j = st // 8, st % 8
                        pe.wait_ge(s("e_kept"), b * 64 + (g * 32 + st * 2 + 2))
                        if j == 0:
                            pe.wait_ge(s("nrm_kept"), FREE + b * 4 + (g * 2 + f))
                        for h in range(GH):
                            pe.matmul(PP[2][h * D:(h + 1) * D, 0:HALF], VV[:, g, j, h * D:(h + 1) * D],
                                      PR[:, st % 2, h], start=(j == 0), stop=(j == 7))
                        for h in range(GH):
                            mm = pe.matmul(PP[2][h * D:(h + 1) * D, HALF:2 * HALF], onesf[:, :],
                                           PR[:, st % 2, h], start=(j == 0), stop=(j == 7))
                        mm.then_inc(s("pv_made"), 1)

                    for st in range(16):
                        f, j = st // 8, st % 8
                        if st == 0:
                            pe.wait_ge(s(f"ld_g{g}"), b * LOAD_GROUP + LOAD_GROUP)
                            pe.wait_ge(s("kone_kept"), 1)
                        if j == 0:
                            pe.wait_ge(s(f"ld_nm{g}{f}"), b * 16 + 16)
                        for pr in range(2):
                            if g or st:
                                pe.wait_ge(s("e_kept"), b * 64 + (g * 32 + st * 2 + pr - 1))
                            for h in (2 * pr, 2 * pr + 1):
                                mm = pe.matmul(PP[pr][:, (h % 2) * HALF:(h % 2 + 1) * HALF],
                                               KP[0:QK_ROWS + 1, g, h, j * P:(j + 1) * P],
                                               QP[0:QK_ROWS + 1, g, f, h, :], start=True, stop=True)
                            mm.then_inc(s("st_made"), 1)
                        if st:
                            weigh_heads(st - 1)
                        for n in MAX_AT[st]:
                            if n == 0:
                                pe.wait_ge(s(f"ld_g{1 - g}"), b * LOAD_GROUP + LOAD_GROUP * (g + 1))
                            if n == 16:
                                max_row(0, b * 4 + (2 * g + 3))
                                pe.wait_ge(s("nmr_kept"), b * 4 + (2 * g + 3))
                            max_pair(n, 1 - g, b * 128 + 64 * (g + 1))
                    weigh_heads(15)
                    max_row(1, b * 4 + (2 * g + 4))
                pe.wait_ge(s("nrm_kept"), FREE + b * 4 + 4)
                pe.wait_ge(s("ld_wo"), 16)
                for t in range(NT):
                    product(PP[t // 4][:, (t % 4) * C:(t % 4 + 1) * C],
                            [(OS[:, c, t * P:(t + 1) * P], wo_sb[:, c]) for c in range(CC)],
                            "pr_made" if t % 4 == 3 else None)
                pe.wait_ge(s("rows_kept"), b + 1)
                pe.wait_ge(s("nmr_kept"), b * 4 + 6)
                for t in range(NT):
                    for q in range(4):
                        at = (t % 4) * 512 + q * P
                        mm = pe.transpose(PP[2 + t // 4][:, :].bitcast(F16)[:, at:at + P],
                                          rows[:, t, q // 2, (q % 2) * P:(q % 2 + 1) * P], ident16[:, :])
                    if t % 4 == 3:
                        mm.then_inc(s("rT_made"), 1)
                for t in range(NT):
                    if t == 0:
                        pe.wait_ge(s("rT_kept_a"), b + 1)
                    if t == 4:
                        pe.wait_ge(s("rT_kept_v"), FREE + b + 1)
                    product(PP[0][:, t * 2 * E:(t + 1) * 2 * E],
                            [(lnr[:, t, q], wr16[:, q % 2].rearrange("p s e -> p (s e)")) for q in range(4)],
                            "lg_made" if t == NT - 1 else None)
                pe.wait_ge(s("pick_kept"), b + 1)
                product(PP[1][:, 0:NT * E], [(below16[:, :], pick16[:, :, :].rearrange("p t e -> p (t e)")),
                                             (ones16[:, :], cum16[:, 0:NT, :].rearrange("p t e -> p (t e)"))],
                        "rk_made")

            pe.wait_ge(s("idx_kept"), FREE + B)
            product(PP[0][:, 0:E], [(ones16[:, :], cum16[:, 0, :])], "cnt_made")
            pe.wait_ge(s("table_kept"), 1)
            pe.wait_ge(s("ld_last"), 16)

            def expert(at):
                return pe.value_load(tile_e[0:1, at], min_val=0, max_val=E - 1)

            def weights(e, off, n):
                return WB[:, bass.ds(e, 1), off:off + n].rearrange("p o n -> p (o n)")

            def turn(t, u, n_load):
                pe.wait_ge(s(f"ld_xs{u}"), n_load)
                if not (isinstance(t, int) and t < 2):
                    pe.wait_ge(s("xT_kept"), t - 1)
                for q in range(4):
                    for a in range(2):
                        at = q * TT + a * P
                        mm = pe.transpose(turned_bank(u)[:, at:at + P],
                                          xs[u][:, a, q // 2, (q % 2) * P:(q % 2 + 1) * P], ident16[:, :])
                mm.then_inc(s("xT_made"), 1)

            MEET = ((0, 0), (0, 1), (1, 0))

            def first(t, u, e):
                pe.wait_ge(s("xT_kept"), t + 1)
                for k in range(HC):
                    if not (isinstance(t, int) and k < 4):
                        pe.wait_ge(s("h_kept"), t * HC + (k - 3))
                    product(hidden_bank(k),
                            [(weights(e, (w * CC + c) * HID + k * P, P), xT[u][:, d * CC + c])
                             for w, d in MEET for c in range(CC)], "h_made")

            def second(t, u, e):
                pe.wait_ge(s("hs_kept"), FREE + t * 4 + 4)
                for a in range(2):
                    product(PP[2][:, u * HALF + a * C:u * HALF + (a + 1) * C],
                            [(hs[u][:, d, k, a * P:(a + 1) * P], weights(e, 2 * CC * HID + (w * HC + k) * C, C))
                             for w, d in MEET for k in range(HC)], "y_made" if a else None)

            turn(0, 0, 16)
            first(0, 0, expert(slice(0, 1)))
            turn(1, 1, 16)
            with pe.Fori(0, (TILES - 1) // 2) as i:
                e0 = expert(bass.ds(i * 2, 1))
                e1 = expert(bass.ds(i * 2 + 1, 1))
                e2 = expert(bass.ds(i * 2 + 2, 1))
                first(i * 2 + 1, 1, e1)
                turn(i * 2 + 2, 0, i * 16 + 32)
                pe.wait_ge(s("y_kept"), FREE + i * 2)
                second(i * 2, 0, e0)
                first(i * 2 + 2, 0, e2)
                turn(i * 2 + 3, 1, i * 16 + 32)
                pe.wait_ge(s("y_kept"), FREE + i * 2)
                second(i * 2 + 1, 1, e1)
            pe.wait_ge(s("y_kept"), FREE + TILES - 2)
            second(TILES - 1, 0, expert(slice(TILES - 1, TILES)))

            with pe.Fori(0, B) as b:
                for f in range(2):
                    pe.wait_ge(s("f_kept"), FREE + b * 2 + (f + 1))
                    pe.wait_ge(s("f_out"), FREE + b * 2)
                    for c in range(CC):
                        for t in range(4):
                            mm = pe.transpose(PP[f][:, c * HALF + t * P:c * HALF + (t + 1) * P],
                                              tf[f][:, t, c * P:(c + 1) * P], identf[:, :])
                    mm.then_inc(s("fT_made"), 1)

        @block.vector
        def _(dve):
            def per_tile(a):
                return a.unsqueeze(2).broadcast_to((P, a.shape[1], E))

            def per_expert(a, n):
                return a.unsqueeze(1).broadcast_to((P, n, E))

            dve.wait_ge(s("pe_prep"), 1)
            dve.wait_ge(s("ld_w"), 16 * LOADS)
            for dst, at in ((wqT, 0), (wvT, 256), (woT, 512)):
                dve.tensor_copy(dst, PP[0][:, at:at + 256].rearrange("p (c n) -> p c n", c=CC))
            dve.tensor_copy(b1c[:, :, :], PP[0][:, 896:896 + E * HC].rearrange("p (e k) -> p e k", e=E))
            dve.tensor_copy(wwgT, PP[0][:, 768:896])
            dve.tensor_scalar(bkr, identf[:, :], 0.0, vec[:, BK:BK + 1], ALU.mult, ALU.add)
            dve.tensor_scalar(vec[:, 24:25], vec[:, V1:V1 + 1], EPS, None, ALU.add)
            dve.tensor_scalar(vec[:, 25:27], vec[:, V2:V2 + 2], EPS, None, ALU.add)
            dve.tensor_scalar(wr16[:, :, 0, :], wr_raw, WSCALE, None, ALU.mult)
            dve.memset(cum16[:, 0, :], 0.0)
            dve.drain()
            dve.scalar_tensor_tensor(out=wr16[:, :, 1, :], in0=wr_raw, scalar=WSCALE, in1=wr16[:, :, 0, :],
                                     op0=ALU.mult, op1=ALU.subtract).then_inc(s("dve_prep"), 1)
            dve.wait_ge(s("act_prep"), 1)
            dve.reciprocal(vec[:, 27:30], vec[:, 24:27])
            dve.drain()
            dve.tensor_tensor(vec[:, S1:S1 + 1], vec[:, 27:28], vec[:, G1:G1 + 1], ALU.mult)
            dve.tensor_tensor(vec[:, S2:S2 + 2], vec[:, 28:30], vec[:, G2:G2 + 2], ALU.mult)
            dve.tensor_tensor(vec[:, BO:BO + 2], vec[:, BO:BO + 2], vec[:, M2:M2 + 2], ALU.subtract)
            dve.drain()
            dve.tensor_tensor(vec[:, M1:M1 + 1], vec[:, M1:M1 + 1], vec[:, S1:S1 + 1], ALU.mult)
            dve.tensor_tensor(vec[:, BO:BO + 2], vec[:, BO:BO + 2], vec[:, S2:S2 + 2], ALU.mult)
            dve.drain()
            dve.tensor_tensor(vec[:, BE1:BE1 + 1], vec[:, BB1:BB1 + 1], vec[:, M1:M1 + 1], ALU.subtract)
            dve.tensor_tensor(vec[:, BE2:BE2 + 2], vec[:, BO:BO + 2], vec[:, BB2:BB2 + 2], ALU.add)
            dve.wait_ge(s("pe_prep"), 2)
            dve.tensor_copy(kwT, PP[1][:, 0:256].rearrange("p (c n) -> p c n", c=CC))
            dve.tensor_copy(kb, PP[1][:, 512:640])
            dve.drain()
            dve.sem_inc(s("dve_prep"), 1)

            def statistics(src, out_sem):
                for t in range(NT):
                    dve.bn_stats(bst[:, t], src[:, t])
                dve.drain()
                for t in range(NT):
                    dve.bn_aggr(mv[:, t], bst[:, t])
                dve.drain()
                dve.tensor_scalar(small[:, 1], mv[:, :, 1], EPS, None, ALU.add).then_inc(s(out_sem), 1)

            with dve.Fori(0, B) as b:
                dve.wait_ge(s("v_made"), b + 1)
                dve.tensor_scalar(v_sb, PP[1][:, :], vec[:, BV:BV + 1], None, ALU.add).then_inc(s("v_kept"), 1)
                dve.wait_ge(s("k_made"), b + 1)
                dve.tensor_tensor(kT.rearrange("p (t o) -> p t o", t=NT), PP[2][:, :]
                                  .rearrange("p (t o) -> p t o", t=NT),
                                  kb.unsqueeze(1).broadcast_to((P, NT, P)), ALU.add).then_inc(s("k_kept"), 1)

                def scale_keys(i):
                    dve.wait_ge(s("exp_kept"), b * NT + (i + 1))
                    dve.reciprocal(rinv[:, i:i + 1], rsum[:, i:i + 1])
                    dve.drain()
                    if i >= 3:
                        dve.wait_ge(s("av_made"), b * NT + (i - 2))
                    dve.tensor_scalar(kTs[:, i % 3], kT[:, i * P:(i + 1) * P], rinv[:, i:i + 1], None,
                                      ALU.mult).then_inc(s("ks_kept"), 1)

                for i in range(NT):
                    dve.wait_ge(s("sc_made"), b * NT + (i + 1))
                    dve.tensor_reduce(nmax[:, i:i + 1], PP[i % 3][:, :], X_AXIS, ALU.max, negate=True)\
                       .then_inc(s("max_kept"), 1)
                    if i:
                        scale_keys(i - 1)
                scale_keys(NT - 1)
                dve.wait_ge(s("av_made"), b * NT + NT)
                for h in range(2):
                    n = slice(h * HALF, (h + 1) * HALF)
                    dve.tensor_scalar(y1[:, n], PP[3][:, n], vec[:, S1:S1 + 1], vec[:, BE1:BE1 + 1],
                                      ALU.mult, ALU.add).then_inc(s("y1_kept"), 1)
                for c in range(CC):
                    dve.wait_ge(s("cv_made"), b * 2 + (c + 1))
                    dve.scalar_tensor_tensor(out=X[:, c], in0=PP[c][:, :], scalar=vec[:, S2 + c:S2 + c + 1],
                                             in1=X[:, c], op0=ALU.mult, op1=ALU.add).then_inc(s("cv_kept"), 1)
                dve.wait_ge(s("tk_made"), FREE + b * 2 + 2)
                dve.wait_ge(s("st_res0"), FREE + b * 16)
                dve.tensor_copy(tok[:, 4:8], PP[3][:, :].rearrange("p (t c) -> p t c", t=4))\
                   .then_inc(s("tk_kept_v"), 1)
                dve.drain()
                dve.wait_ge(s("tk_kept_a"), b + 1)
                statistics(tok, "stat_kept")
                dve.wait_ge(s("sd_kept"), b + 1)
                dve.reciprocal(small[:, 3], small[:, 2])
                dve.drain()
                dve.wait_ge(s("st_q0"), FREE + b * 64)
                dve.wait_ge(s("st_q1"), FREE + b * 64)
                for t in range(NT):
                    dve.tensor_scalar(ln[:, t], tok[:, t], mv[:, t, 0:1], small[:, 3, t:t + 1],
                                      ALU.subtract, ALU.mult).then_inc(s("ln_kept"), 1)
                dve.wait_ge(s("ln_kept"), b * NT + NT)
                dve.tensor_tensor(tok, tok, bob.unsqueeze(1).broadcast_to((P, NT, C)), ALU.add)\
                   .then_inc(s("res0_kept"), 1)
                dve.wait_ge(s("lnT_made"), b * 2 + 2)
                dve.tensor_copy(lnT[:, 1], PP[1][:, :]).then_inc(s("lnT_kept_v"), 1)
                for u in range(4):
                    dve.wait_ge(s("qhi_kept"), FREE + b * 4 + (u + 1))
                    dve.scalar_tensor_tensor(out=qs[:, u % 2, 1], in0=PP[(u + 2) % 4][:, :],
                                             scalar=C ** -0.5 if u < 2 else 1.0, in1=qs[:, u % 2, 0],
                                             op0=ALU.mult, op1=ALU.subtract).then_inc(s("qlo_kept"), 1)
                dve.wait_ge(s("vt_made"), b * 2 + 2)
                dve.tensor_copy(VT[:, 4:8], PP[3][:, :].rearrange("p (t c) -> p t c", t=4))\
                   .then_inc(s("vt_kept_v"), 1)

            for name, n in (("st_v", 16), ("st_q0", 64), ("st_q1", 64), ("st_res0", 16)):
                dve.wait_ge(s(name), FREE + n * B)
            dve.memset(KP[QK_ROWS:QK_ROWS + 1], MSCALE).then_inc(s("kone_kept"), 1)

            def reduce_pair(n, base):
                for k in range(2):
                    dve.wait_ge(s("c_made"), base + (2 * n + k + 1))
                    dve.tensor_reduce(mxp[:, n % 16, k:k + 1], PP[3][:, k * HALF:(k + 1) * HALF], X_AXIS,
                                      ALU.max).then_inc(s("c_kept"), 1)

            def join_halves(f, sem_row, n_row, n_half):
                dve.drain()
                dve.tensor_reduce(mx[:, f], mxp[:, :, :], X_AXIS, ALU.max, negate=True)
                dve.drain()
                dve.tensor_scalar(mx[:, f], mx[:, f], 1.0 / MSCALE, None, ALU.mult).then_inc(s("nm_kept"), 1)
                dve.wait_ge(s("nmT_made"), n_half)
                if sem_row:
                    dve.wait_ge(s(sem_row), n_row)
                dve.tensor_copy(nmr[:, :], PP[3][0:16, 0:P]).then_inc(s("nmr_kept"), 1)

            for n in range(32):
                reduce_pair(n, 0)
                if n == 15:
                    join_halves(0, None, 0, 1)
            join_halves(1, "ld_nm00", 16, 2)

            with dve.Fori(0, B) as b:
                for g in range(GROUPS):
                    def normalise(f):
                        dve.wait_ge(s("pv_made"), FREE + b * 32 + (g * 16 + 8 * f + 8))
                        dve.reciprocal(rin, PP[2][:, HALF:2 * HALF])
                        dve.drain()
                        dve.tensor_tensor(OS[:, g, f * HALF:(f + 1) * HALF], PP[2][:, 0:HALF], rin, ALU.mult)\
                           .then_inc(s("nrm_kept"), 1)

                    for st in range(16):
                        if st == 8:
                            normalise(0)
                        for n in MAX_AT[st]:
                            reduce_pair(n, b * 128 + 64 * (g + 1))
                            if n == 15:
                                join_halves(0, f"ld_nm{g}1", b * 16 + 16, b * 4 + (2 * g + 3))
                    normalise(1)
                    join_halves(1, f"ld_nm{1 - g}0", b * 16 + 16 * (g + 1), b * 4 + (2 * g + 4))
                dve.wait_ge(s("ld_res0"), b * 16 + 16)
                for h in range(2):
                    dve.wait_ge(s("pr_made"), b * 2 + (h + 1))
                    dve.tensor_tensor(t1[:, 4 * h:4 * h + 4], PP[h][:, :].rearrange("p (t c) -> p t c", t=4),
                                      t1[:, 4 * h:4 * h + 4], ALU.add)
                dve.drain()
                statistics(t1, "stat1_kept")
                dve.wait_ge(s("sd1_kept"), b + 1)
                dve.reciprocal(small[:, 3], small[:, 2])
                dve.drain()
                for t in range(NT):
                    dve.tensor_scalar(ln32[:, t], t1[:, t], mv[:, t, 0:1], small[:, 3, t:t + 1],
                                      ALU.subtract, ALU.mult)
                dve.drain()
                dve.sem_inc(s("ln1_kept"), 1)
                dve.wait_ge(s("hi_kept"), b + 1)
                dve.tensor_tensor(rows[:, :, 1, :], ln32, rows[:, :, 0, :], ALU.subtract)\
                   .then_inc(s("rows_kept"), 1)
                dve.wait_ge(s("rT_made"), b * 2 + 2)
                dve.tensor_copy(lnr[:, 4:8], PP[3][:, :].bitcast(F16).rearrange("p (t s n) -> p t s n", t=4, s=4))\
                   .then_inc(s("rT_kept_v"), 1)
                logit, oh1, oh2, val, rest, rk, tmp = [rt[:, i] for i in range(7)]
                dve.wait_ge(s("lg_made"), b + 1)
                dve.tensor_copy(tmp, PP[0][:, 0:NT * 2 * E].rearrange("p (t s e) -> p t s e", t=NT, s=2)[:, :, 1])
                dve.drain()
                dve.tensor_tensor(logit, PP[0][:, 0:NT * 2 * E]
                                  .rearrange("p (t s e) -> p t s e", t=NT, s=2)[:, :, 0], tmp, ALU.add)
                dve.drain()

                def largest(src, top, one_hot):
                    dve.tensor_reduce(top, src, X_AXIS, ALU.max)
                    dve.drain()
                    dve.tensor_tensor(val, src, per_tile(top), ALU.is_equal)
                    dve.drain()
                    dve.tensor_tensor(val, val, per_expert(w8[:, :], NT), ALU.mult)
                    dve.drain()
                    dve.tensor_reduce(rs[:, 3], val, X_AXIS, ALU.max)
                    dve.drain()
                    dve.tensor_tensor(one_hot, per_expert(w8[:, :], NT), per_tile(rs[:, 3]), ALU.is_equal)
                    dve.drain()

                largest(logit, rs[:, 0], oh1)
                dve.scalar_tensor_tensor(out=rest, in0=oh1, scalar=-BIG, in1=logit, op0=ALU.mult, op1=ALU.add)
                dve.drain()
                largest(rest, rs[:, 1], oh2)
                dve.tensor_tensor(rs[:, 2], rs[:, 1], rs[:, 0], ALU.subtract)
                dve.tensor_tensor(pick16[:, :, :], oh1, oh2, ALU.add)
                dve.drain()
                for t in range(NT):
                    dve.tensor_tensor(cum16[:, t + 1], cum16[:, t], pick16[:, t], ALU.add)
                    dve.drain()
                dve.sem_inc(s("pick_kept"), 1)
                dve.tensor_copy(pick1[:, bass.ds(b * NT, NT), :], oh1)
                dve.tensor_copy(pick2[:, bass.ds(b * NT, NT), :], oh2)
                dve.wait_ge(s("gexp_kept"), b + 1)
                dve.tensor_scalar(rs[:, 3], rs[:, 2], 1.0, None, ALU.add)
                dve.drain()
                dve.reciprocal(rs[:, 4], rs[:, 3])
                dve.drain()
                dve.tensor_copy(gate1[:, bass.ds(b * NT, NT)], rs[:, 4])
                dve.tensor_tensor(gate2[:, bass.ds(b * NT, NT)], rs[:, 4], rs[:, 2], ALU.mult)
                dve.wait_ge(s("rk_made"), b + 1)
                dve.tensor_copy(rk, PP[1][:, 0:NT * E].rearrange("p (t e) -> p t e", e=E))
                dve.tensor_copy(cum16[:, 0], cum16[:, NT])
                dve.drain()
                dve.tensor_tensor(val, rk, per_expert(ebase[:, :], NT), ALU.add)
                dve.tensor_copy(rank[:, bass.ds(b * NT, NT), :], rk)
                dve.drain()
                dve.tensor_tensor(tmp, val, oh1, ALU.mult)
                dve.tensor_tensor(rest, val, oh2, ALU.mult)
                dve.drain()
                dve.tensor_reduce(rs[:, 0], tmp, X_AXIS, ALU.add)
                dve.tensor_reduce(rs[:, 1], rest, X_AXIS, ALU.add)
                dve.drain()
                dve.wait_ge(s("listed"), FREE + b)
                dve.tensor_copy(idx[:, :, :], rs[:, 0:2]).then_inc(s("idx_kept"), 1)
            dve.wait_ge(s("idx_kept"), FREE + B)
            dve.sem_inc(s("phase_b"), 1)

            dve.wait_ge(s("zero_kept"), 1)
            dve.wait_ge(s("cnt_made"), 1)
            dve.wait_ge(s("ld_b2"), 16)
            dve.tensor_copy(cnt, PP[0][:, 0:E])
            dve.tensor_copy(seqc, seq.bitcast(I32))
            dve.drain()
            over = cmp[:, 0:B * N // TT]
            dve.tensor_tensor(over, per_expert(cnt, B * N // TT), per_tile(thr), ALU.is_gt)
            dve.tensor_tensor(zrowf, cnt, ebase[:, :], ALU.add)
            dve.drain()
            dve.tensor_reduce(lists, over.rearrange("p k e -> p e k"), X_AXIS, ALU.add)
            dve.tensor_copy(zrow, zrowf)
            dve.drain()
            dve.tensor_tensor_scan(incl, one8, lists, 0.0, ALU.mult, ALU.add)
            dve.drain()
            dve.tensor_tensor(start, incl, lists, ALU.subtract)
            dve.tensor_scalar(seq, incl[:, E - 1:E].broadcast_to((P, TABLE)), -1.0, None, ALU.add)
            dve.drain()
            dve.tensor_tensor(seqc, seqc, seq, ALU.min)
            dve.drain()
            dve.tensor_tensor(cmp, per_expert(incl, TABLE), per_tile(seqc), ALU.is_le)
            dve.drain()
            dve.tensor_reduce(te, cmp, X_AXIS, ALU.add)
            dve.drain()
            dve.tensor_tensor(cmp, cmp, per_expert(lists, TABLE), ALU.mult)
            dve.drain()
            dve.tensor_reduce(tk, cmp, X_AXIS, ALU.add)
            dve.drain()
            dve.tensor_tensor(tk, seqc, tk, ALU.subtract)
            dve.tensor_copy(tile_e, te)
            dve.drain()
            dve.tensor_scalar(tk, tk, float(TT), None, ALU.mult)
            dve.drain()
            dve.scalar_tensor_tensor(out=tk, in0=te, scalar=float(REGION), in1=tk, op0=ALU.mult, op1=ALU.add)
            dve.drain()
            dve.tensor_copy(tile_row, tk)
            dve.drain()
            dve.sem_inc(s("table_kept"), 1)
            dve.tensor_scalar(start, start, float(TT), None, ALU.mult)
            dve.drain()
            dve.tensor_tensor(big, rank[:, :, :], per_expert(start, B * NT), ALU.add)
            dve.drain()
            for k, pick in enumerate((pick1, pick2)):
                dve.tensor_tensor(big2, big, pick[:, :, :], ALU.mult)
                dve.drain()
                dve.tensor_reduce(slotf[:, k], big2, X_AXIS, ALU.add)
                dve.drain()
            dve.tensor_copy(slot, slotf)
            dve.drain()
            dve.sem_inc(s("slot_kept"), 1)

            def keep_turned(t, u):
                dve.wait_ge(s("xT_made"), t + 1)
                dve.tensor_copy(xT[u].rearrange("p s n -> p (s n)"), turned_bank(u)).then_inc(s("xT_kept"), 1)

            def split_hidden(t, u):
                for j in range(HC // 2):
                    dve.wait_ge(s("h_kept"), t * HC + (2 * j + 2))
                    k = slice(2 * j, 2 * j + 2)
                    dve.tensor_copy(hs[u][:, 0, k], hid[u][:, k])
                    dve.drain()
                    dve.tensor_tensor(hs[u][:, 1, k], hid[u][:, k], hs[u][:, 0, k], ALU.subtract)\
                       .then_inc(s("hs_kept"), 1)

            def keep_output(t, u, n_store, e):
                dve.wait_ge(s("y_made"), FREE + t + 1)
                if n_store is not None:
                    dve.wait_ge(s(f"st_y{u}"), FREE + n_store)
                dve.scalar_tensor_tensor(
                    out=ysb[u], in0=PP[2][:, u * HALF:(u + 1) * HALF].rearrange("p (a c) -> p a c", a=2),
                    scalar=1.0 / WSCALE, in1=b2b[:, bass.ds(e, 1), :].broadcast_to((P, 2, C)),
                    op0=ALU.mult, op1=ALU.add).then_inc(s("y_kept"), 1)

            def expert(at):
                return dve.value_load(tile_e[0:1, at], min_val=0, max_val=E - 1)

            keep_turned(0, 0)
            split_hidden(0, 0)
            keep_turned(1, 1)
            with dve.Fori(0, (TILES - 1) // 2) as i:
                e0 = expert(bass.ds(i * 2, 1))
                e1 = expert(bass.ds(i * 2 + 1, 1))
                dve.wait_ge(s("y_made"), FREE + i * 2)
                split_hidden(i * 2 + 1, 1)
                keep_turned(i * 2 + 2, 0)
                keep_output(i * 2, 0, i * 16, e0)
                dve.wait_ge(s("y_made"), FREE + i * 2 + 1)
                split_hidden(i * 2 + 2, 0)
                keep_turned(i * 2 + 3, 1)
                keep_output(i * 2 + 1, 1, i * 16, e1)
            keep_output(TILES - 1, 0, 16 * (TILES // 2), expert(slice(TILES - 1, TILES)))

            with dve.Fori(0, B) as b:
                dve.tensor_copy(slot_now, slot[:, :, bass.ds(b * NT, NT)]).then_inc(s("idx_now"), 1)
                dve.tensor_copy(rs[:, 0], gate1[:, bass.ds(b * NT, NT)])
                dve.tensor_copy(rs[:, 1], gate2[:, bass.ds(b * NT, NT)])
                dve.drain()
                for f in range(2):
                    dve.wait_ge(s(f"ld_y{f}"), b * 128 + 128)
                    dve.wait_ge(s(f"ld_t{f}"), b * 16 + 16)
                    for k in range(2):
                        for t in range(4):
                            last = dve.scalar_tensor_tensor(
                                out=tf[f][:, t], in0=yg[f][:, k, t], scalar=rs[:, k, 4 * f + t:4 * f + t + 1],
                                in1=tf[f][:, t], op0=ALU.mult, op1=ALU.add)
                        if k == 0:
                            dve.drain()
                    last.then_inc(s("f_kept"), 1)
                dve.drain()


_INS = ["x", "L0_conv_wk", "L0_conv_bk", "L0_conv_wv", "L0_conv_bv", "L0_conv_wq", "L0_conv_bq",
        "L0_conv_wwg", "L0_conv_bn1_g", "L0_conv_bn1_b", "L0_conv_bn1_m", "L0_conv_bn1_v",
        "L0_conv_wout", "L0_conv_bout", "L0_conv_bn2_g", "L0_conv_bn2_b", "L0_conv_bn2_m",
        "L0_conv_bn2_v", "L1_attn_w_qkv", "L1_attn_w_out", "L1_attn_b_out", "L1_ffn_Wr",
        "L1_ffn_W1", "L1_ffn_b1", "L1_ffn_W2", "L1_ffn_b2"]
_OUTS = [((4, 256, 32, 32), "float32")]


def kernel(**inputs):
    import numpy as _np
    import concourse.bacc as _bacc
    from concourse import mybir as _mybir
    from concourse.bass_utils import run_bass_kernel_spmd as _run

    nc = _bacc.Bacc("TRN2", target_bir_lowering=False, num_devices=1)
    arrays, args = {}, []
    for name in _INS:
        a = _np.ascontiguousarray(inputs[name])
        arrays[f"in_{name}_dram"] = a
        args.append(nc.dram_tensor(f"in_{name}_dram", a.shape, _mybir.dt.from_np(a.dtype), kind="ExternalInput").ap())
    for i, (shape, dtype) in enumerate(_OUTS):
        dt = _mybir.dt.from_np(_np.dtype(dtype))
        args.append(nc.dram_tensor(f"out_{i}_dram", shape, dt, kind="ExternalOutput").ap())
    hybrid_block(nc, *args)
    r = _run(nc, [arrays], core_ids=[0])
    return r.results[0]["out_0_dram"]
```

```python
from contextlib import ExitStack

import concourse.bass as bass
from concourse import mybir

F32 = mybir.dt.float32
F16 = mybir.dt.float16
I32 = mybir.dt.int32
ALU = mybir.AluOpType
ACT = mybir.ActivationFunctionType
X_AXIS = mybir.AxisListType.X

P = 128
B, C, N = 4, 256, 1024
CC = C // P
NT = N // P
HALF = 512
IC = 128
HEADS, D = 8, 32
GH = 4
GROUPS = HEADS // GH
QK_ROWS = 3 * D
E, HID = 8, 1024
HC = HID // P
TT = 256
TILES = (2 * B * N) // TT + E - 1
REGION = B * N + TT
TABLE = TILES + 1
LOADS = 26
WSCALE = 64.0
MSCALE = 64.0
WE = 8192
BIG = 3.0e38
EPS = 1e-5


LOAD_GROUP = 16 * 10
MAX_AT = [[((st >= 4), int(st < 4 or st >= 12), (st - (4 if 4 <= st < 12 else 12)) % 16 * 2 + n)
           for n in range(2)] for st in range(16)]
ROW_AT = (4, 12)
PROJECT_AT, STATS_AT, SD_AT, RSTD_AT, NORM_AT, HIGH_AT = (0, 4, 7, 8), (6, 13), 13, 14, (14, 15, 16, 17), (16, 18)
TURN_AT, LOGIT_AT, PICK_AT, GATE_AT, RANK_AT = (18, 20, 22, 23), 24, (24, 26, 28, 29), 30, 30
ROW_USES = 48 + 1
INVERT_AT = (1, 2, 3, 5)
GROUP_USES = 2 * (32 + 1)
TAIL_USES = 4 + 4 + 2

FREE = 1
PLACES = ("tk_made st_res1 pv_made fT_made st_v st_res0 rT_kept_v listed " 
          "hs_kept st_out0 st_out1 f_kept qhi_kept qlo_kept vt_kept_a vt_kept_v idx_kept " 
          "nrm_kept sum_kept y_kept f_out st_q0 st_q1 y_made st_y0 st_y1")


def hybrid_block(nc, x, wk, bk, wv, bv, wq, bq, wwg, bn1_g, bn1_b, bn1_m, bn1_v, wout, bout,
                 bn2_g, bn2_b, bn2_m, bn2_v, w_qkv, w_out, b_out, wr, w1, b1, w2, b2, out):
    ctx = ExitStack()

    def sem(name):
        return ctx.enter_context(nc.semaphore(name))

    def scratch(name, shape, dt):
        return nc.dram_tensor(name, shape, dt, kind="Internal").ap()

    q_hi_d, q_lo_d = scratch("q_hi_d", (B * C, N), F16), scratch("q_lo_d", (B * C, N), F16)
    k_hi_d, k_lo_d = scratch("k_hi_d", (B * C, N), F16), scratch("k_lo_d", (B * C, N), F16)
    v_d = scratch("v_d", (B * N, C), F32)
    res0_d = scratch("res0_d", (B * N, C), F32)
    res1_d = scratch("res1_d", (B * N, C), F32)
    list_d = scratch("list_d", (E * REGION, 2 * C), F16)
    y_d = scratch("y_d", (TILES * TT, C), F32)
    late_d = scratch("late_d", (P, 2 * WE), F16)

    with ctx:
        def sb(name, shape, dt):
            return ctx.enter_context(nc.sbuf_tensor(name, shape, dt))

        WB = sb("WB", [P, E, WE], F16)
        WORK = sb("WORK", [P, 17664], F32)
        PP = [ctx.enter_context(nc.psum_tensor(f"PP{i}", [P, 2 * HALF], F32)) for i in range(4)]

        identf = sb("identf", [P, P], F32)
        ident16 = sb("ident16", [P, P], F16)
        below16 = sb("below16", [P, P], F16)
        ones16 = sb("ones16", [P, P], F16)
        onesf = sb("onesf", [P, D], F32)
        wr16 = sb("wr16", [P, CC, 2, E], F16)
        b1c = sb("b1c", [P, E, HC], F32)
        vec = sb("vec", [P, 32], F32)
        small = sb("small", [P, 8, 8], F32)
        bst = sb("bst", [P, NT, 6], F32)
        mv = sb("mv", [P, NT, 2], F32)
        nmax = sb("nmax", [P, NT], F32)
        rsum = sb("rsum", [P, NT], F32)
        rinv = sb("rinv", [P, NT], F32)
        mxp = sb("mxp", [P, 16, 2], F32)
        mx = sb("mx", [P, 2, 16], F32)
        nmr = sb("nmr", [16, P], F16)
        w8 = sb("w8", [P, E], F32)
        ebase = sb("ebase", [P, E], F32)
        pick1 = sb("pick1", [P, B * NT, E], F32)
        pick2 = sb("pick2", [P, B * NT, E], F32)
        rank = sb("rank", [P, B * NT, E], F32)
        gate1 = sb("gate1", [P, B * NT], F32)
        gate2 = sb("gate2", [P, B * NT], F32)
        idx = sb("idx", [P, 2, NT], I32)
        cum16 = sb("cum16", [P, NT + 1, E], F16)
        pick16 = sb("pick16", [P, NT, E], F16)
        rt = sb("rt", [P, 7, NT, E], F32)
        rs = sb("rs", [P, 6, NT], F32)

        def word_view(a, n):
            return WORK[:, a:a + n]

        o = [0]

        def take(n):
            o[0] += n
            assert o[0] <= 17664
            return word_view(o[0] - n, n)

        X = take(2048).rearrange("p (c n) -> p c n", c=CC)
        QV = take(2048)
        q_sb, v_sb = QV[:, 0:N], QV[:, N:2 * N]
        kT = take(1024)
        PA = take(3072)
        prob = [PA[:, i * N:(i + 1) * N] for i in range(3)]
        y1 = PA[:, 0:N]
        lnT = PA[:, 0:2048].rearrange("p (c n) -> p c n", c=CC)
        tok = take(2048).rearrange("p (t c) -> p t c", t=NT)
        VT = tok
        QS = take(2048)
        ln = QS.rearrange("p (t c) -> p t c", t=NT)
        qs = QS.bitcast(F16).rearrange("p (u s n) -> p u s n", u=2, s=2)
        stage = take(2048).rearrange("p (u n) -> p u n", u=2)
        kTs = take(384).rearrange("p (u o) -> p u o", u=3)
        wqkv_sb = take(1536).rearrange("p (c n) -> p c n", c=CC)
        wqT = take(256).rearrange("p (c n) -> p c n", c=CC)
        wvT = take(256).rearrange("p (c n) -> p c n", c=CC)
        kwT = take(256).rearrange("p (c n) -> p c n", c=CC)
        woT = take(256).rearrange("p (c n) -> p c n", c=CC)
        kb = take(128)
        bob = take(256)
        wq_raw, wv_raw, wk_raw = tok[:, 0, :], tok[:, 1, :], tok[:, 2, :]
        wo_raw = tok[:, 3, :].rearrange("p (c n) -> p c n", c=CC)
        wwg_raw, wwgT, bkr = tok[:, 4, 0:128], tok[:, 4, 128:256], tok[:, 5, 0:128]
        b1_raw = tok[0:E * HC, 7, 0:P]
        wr_raw = tok[:, 6, 0:16].rearrange("p (c e) -> p c e", c=CC)

        o[0] = 0
        stacked = "p (h n) -> p h n"
        QP = take(4096).bitcast(F16).rearrange("p (u f h n) -> p u f h n", u=2, f=2, h=GH)
        VV = [take(1024).rearrange("p (j d) -> p j d", j=NT)]
        KP = [None, take(2048).bitcast(F16).rearrange(stacked, h=GH)]
        OS = take(2048).rearrange("p (g n) -> p g n", g=GROUPS)
        t1 = take(2048).rearrange("p (t c) -> p t c", t=NT)
        VV.append(take(1024).rearrange("p (j d) -> p j d", j=NT))
        KP[0] = take(2048).bitcast(F16).rearrange(stacked, h=GH)
        rin = take(512)
        wo_sb = take(512).rearrange("p (c n) -> p c n", c=CC)
        rows = take(2048).bitcast(F16).rearrange("p (t s c) -> p t s c", t=NT, s=2)
        LATEW = WB[:, E - 2:E, :].rearrange("p e n -> p (e n)")
        PR = WB[:, E - 1].bitcast(F32).rearrange("p (u h n) -> p u h n", u=2, h=GH)
        ln32 = WB[:, E - 2, 0:4096].bitcast(F32).rearrange("p (t c) -> p t c", t=NT)
        lnr = WB[:, E - 2, 4096:8192].rearrange("p (t s n) -> p t s n", t=NT, s=4)

        o[0] = 0
        xs = [take(512).bitcast(F16).rearrange("p (a s c) -> p a s c", a=2, s=2) for _ in range(2)]
        xT = [take(512).bitcast(F16).rearrange("p (s n) -> p s n", s=4) for _ in range(2)]
        hid = [take(2048).rearrange("p (k n) -> p k n", k=HC) for _ in range(2)]
        hs = [take(2048).bitcast(F16).rearrange("p (s k n) -> p s k n", s=2, k=HC) for _ in range(2)]
        ysb = [take(512).rearrange("p (a c) -> p a c", a=2) for _ in range(2)]
        b2b = take(2048).rearrange("p (e c) -> p e c", e=E)
        zero = take(512).bitcast(F16).rearrange("p (a c) -> p a c", a=2)
        TB = take(1408)
        cnt, lists = TB[:, 0:8], TB[:, 8:16]
        incl, start = TB[:, 16:24], TB[:, 24:32]
        thr = TB[:, 32:48]
        seq, seqc = TB[:, 48:88], TB[:, 88:128]
        te, tk = TB[:, 128:168], TB[:, 168:208]
        one8 = TB[:, 208:216]
        cmp = TB[:, 256:256 + TABLE * E].rearrange("p (s e) -> p s e", s=TABLE)
        big = TB[:, 640:640 + 256].rearrange("p (t e) -> p t e", e=E)
        big2 = TB[:, 896:896 + 256].rearrange("p (t e) -> p t e", e=E)
        tile_e = TB[:, 1152:1152 + TABLE].bitcast(I32)
        tile_row = TB[:, 1192:1192 + TABLE].bitcast(I32)
        zrow = TB[:, 1232:1240].bitcast(I32)
        zrowf = TB[:, 1240:1248]
        slot = TB[:, 1248:1312].bitcast(I32).rearrange("p (k t) -> p k t", k=2)
        slotf = TB[:, 1312:1376].rearrange("p (k t) -> p k t", k=2)
        slot_now = TB[:, 1376:1392].bitcast(I32).rearrange("p (k t) -> p k t", k=2)
        o[0] = 0
        yg = [take(2048).rearrange("p (k t c) -> p k t c", k=2, t=4) for _ in range(2)]
        tf = [take(1024).rearrange("p (t c) -> p t c", t=4) for _ in range(2)]
        ob = [take(1024).rearrange("p (c n) -> p c n", c=CC) for _ in range(2)]

        def parity(before):
            return before % 2 if isinstance(before, int) else ROW_USES - TAIL_USES

        def shared_bank(k):
            return PP[3][:, (k % 2) * HALF:(k % 2 + 1) * HALF]

        def hidden_bank(k):
            return PP[k // 2 % 2][:, (k % 2) * HALF:(k % 2) * HALF + TT]

        def turned_bank(u):
            return PP[3][:, u * HALF:(u + 1) * HALF].bitcast(F16)

        S = {}

        def s(name):
            if name not in S:
                S[name] = sem(name)
            return S[name]

        for name in ("ld_w ld_x0 ld_x1 x_used pool_const pe_prep dve_prep act_prep mv_prep "
                     "q_made v_made k_made q_kept v_kept k_kept sc_made max_kept exp_kept ks_kept "
                     "av_made y1_kept cv_made cv_kept x1_kept tk_made tk_kept_a tk_kept_v stat_kept "
                     "sd_kept ln_kept lnT_made lnT_kept_a lnT_kept_v qk_made qhi_kept qlo_kept vt_made "
                     "vt_kept_a vt_kept_v res0_kept st_res0 st_v st_q0 st_q1 "
                     "ld_stage0 ld_stage1 scaled split_hi split_lo st_last wts_split "
                     "ld_g0 ld_g1 sum_kept rin_kept rstd_kept ld_nm00 ld_nm01 ld_nm10 ld_nm11 st_made e_kept pv_made nrm_kept "
                     "c_made c_kept nm_kept nmT_made nmr_kept ld_wo ld_res0 pr_made stat1_kept "
                     "sd1_kept ln1_kept hi_kept rows_kept rT_made rT_kept_a rT_kept_v lg_made pick_kept "
                     "gexp_kept rk_made idx_kept st_list st_res1 phase_b cnt_made table_kept zero_kept "
                     "ld_last ld_b2 st_zero ld_xs0 ld_xs1 xT_made xT_kept h_made h_kept hs_kept "
                     "y_made y_kept st_y0 st_y1 slot_kept idx_now ld_y0 ld_y1 ld_t0 ld_t1 f_kept "
                     "fT_made f_out st_out0 st_out1 kone_kept scatter_on gather_on listed t1_free").split():
            s(name)

        block = ctx.enter_context(nc.Block())

        BQ, BV, BK, G1, BB1, M1, V1, S1, BE1 = range(9)
        BO, G2, BB2, M2, V2, S2, BE2 = (10 + 2 * i for i in range(7))

        @block.sync
        def _(sp):
            for name in PLACES.split():
                sp.sem_inc(s(name), FREE)
            col = lambda a: a.rearrange("(p o) -> p o", o=1)
            n_w = 0
            for dst, src in ((wq_raw, wq), (wv_raw, wv), (wk_raw, wk),
                             (wo_raw, wout.rearrange("(c p) i -> p c i", p=P)), (wwg_raw, wwg),
                             (wqkv_sb, w_qkv.rearrange("(c p) n -> p c n", p=P)),
                             (wr_raw, wr.rearrange("(c p) e -> p c e", p=P)),
                             (bob, b_out.rearrange("(o c) -> o c", o=1).broadcast_to((P, C))),
                             (b1_raw, b1.rearrange("e (k p) -> (e k) p", p=P)),
                             (vec[:, BQ:BQ + 1], col(bq)), (vec[:, BV:BV + 1], col(bv)),
                             (vec[:, BK:BK + 1], col(bk)), (vec[:, G1:G1 + 1], col(bn1_g)),
                             (vec[:, BB1:BB1 + 1], col(bn1_b)), (vec[:, M1:M1 + 1], col(bn1_m)),
                             (vec[:, V1:V1 + 1], col(bn1_v)),
                             *((vec[:, at + c:at + c + 1], col(src[c * P:(c + 1) * P]))
                               for at, src in ((BO, bout), (G2, bn2_g), (BB2, bn2_b), (M2, bn2_m), (V2, bn2_v))
                               for c in range(CC))):
                sp.dma_start(dst, src).then_inc(s("ld_w"), 16)
                n_w += 1
            assert n_w == LOADS
            xv = x.rearrange("b (c p) h w -> b p c (h w)", p=P)
            qk_d = ((q_hi_d, q_lo_d), (k_hi_d, k_lo_d))

            def load_x(n, c):
                sp.dma_start(X[:, c], xv[bass.ds(n, 1), :, c, :].rearrange("o p n -> p (o n)"))\
                  .then_inc(s(f"ld_x{c}"), 16)

            def load_q(b, g, par):
                for r, src in enumerate((q_hi_d, q_hi_d, q_lo_d)):
                    part = src[bass.ds(b * C + g * P, P), :].rearrange("(h d) (f n) -> d h f n", d=D, f=2)
                    for f in range(2):
                        sp.dma_start(QP[r * D:(r + 1) * D, par, f], part[:, :, f, :])\
                          .then_inc(s(f"ld_g{par}"), 16)

            def load_k(b, g, par):
                for r, src in enumerate((k_hi_d, k_lo_d, k_hi_d)):
                    part = src[bass.ds(b * C + g * P, P), :].rearrange("(h d) n -> d h n", d=D)
                    sp.dma_start(KP[par][r * D:(r + 1) * D], part).then_inc(s(f"ld_g{par}"), 16)

            def load_v(b, g, par):
                sp.dma_start(VV[par], v_d[bass.ds(b * N, N), g * P:(g + 1) * P]
                             .rearrange("(j p) d -> p j d", p=P)).then_inc(s(f"ld_g{par}"), 16)

            def load_group(b, g, par):
                load_q(b, g, par)
                load_k(b, g, par)
                load_v(b, g, par)

            def tokens(b, last):
                if not last:
                    for c in range(CC):
                        sp.wait_ge(s("x_used"), b * 2 + (c + 1))
                        load_x(b + 1, c)
                else:
                    sp.wait_ge(s("x_used"), 2 * B)
                    for name, n in (("st_v", 16), ("st_q0", 64), ("st_q1", 64)):
                        sp.wait_ge(s(name), FREE + n)
                    load_q(0, 0, 0)
                    load_v(0, 0, 0)
                sp.wait_ge(s("res0_kept"), b + 1)
                sp.dma_start(res0_d[bass.ds(b * N, N), :].rearrange("(t p) c -> p t c", p=P), tok)\
                  .then_inc(s("st_res0"), 16)
                for u in range(4):
                    sp.wait_ge(s("qlo_kept"), FREE + b * 4 + (u + 1))
                    for k in range(2):
                        dst = qk_d[u // 2][k][bass.ds(b * C + (u % 2) * P, P), :]
                        sp.dma_start(dst, qs[:, u % 2, k, :]).then_inc(s(f"st_q{u % 2}"), 16)
                    if last and u == 2:
                        sp.wait_ge(s("split_lo"), 32)
                        load_k(0, 0, 0)
                sp.wait_ge(s("vt_kept_a"), FREE + b + 1)
                sp.wait_ge(s("vt_kept_v"), FREE + b + 1)
                sp.dma_start(v_d[bass.ds(b * N, N), :].rearrange("(t p) c -> p t c", p=P), VT)\
                  .then_inc(s("st_v"), 16)

            load_x(0, 0)
            load_x(0, 1)
            with sp.Fori(0, B - 1) as b:
                tokens(b, False)
            tokens(B - 1, True)
            sp.wait_ge(s("st_res0"), FREE + 16 * B)
            sp.wait_ge(s("st_q0"), FREE + 64 * B)
            sp.wait_ge(s("st_q1"), FREE + 64 * B)
            sp.wait_ge(s("st_v"), FREE + 16 * B)
            sp.wait_ge(s("vt_made"), 2 * B)
            sp.dma_start(wo_sb, w_out.rearrange("(c p) n -> p c n", p=P)).then_inc(s("ld_wo"), 16)

            def store_max(par, f, n):
                sp.wait_ge(s("nmr_kept"), n)
                sp.dma_start(QP[QK_ROWS:QK_ROWS + 1, par, f].rearrange("o h n -> o (h n)"),
                             nmr[:, :]).then_inc(s(f"ld_nm{par}{f}"), 16)

            def store_res1(tail, n):
                sp.wait_ge(s("ln1_kept"), n * 4)
                sp.dma_start(res1_d[bass.ds(tail * N, N), :].rearrange("(t p) c -> p t c", p=P), t1)\
                  .then_inc(s("st_res1"), 16)

            def attend(b, first):
                for g in range(GROUPS):
                    sp.wait_ge(s("pv_made"), FREE + b * 32 + g * 16)
                    if g == 0:
                        load_group(b, 1, 1)
                    else:
                        load_group((b + 1) % B, 0, 0)
                        if not first:
                            store_res1(b - 1, b)
                        sp.wait_ge(s("st_res1"), FREE + b * 16)
                        sp.sem_inc(s("t1_free"), 1)
                        sp.dma_start(t1, res0_d[bass.ds(b * N, N), :].rearrange("(t p) c -> p t c", p=P))\
                          .then_inc(s("ld_res0"), 16)
                    store_max(g, 1, b * 4 + (2 * g + 2))
                    store_max(1 - g, 0, b * 4 + (2 * g + 3))

            store_max(0, 0, 1)
            attend(0, True)
            with sp.Fori(1, B) as b:
                attend(b, False)
            sp.wait_ge(s("st_last"), 16)
            sp.wait_ge(s("pv_made"), FREE + 32 * B)
            sp.dma_start(WB[:, E - 1], late_d[:, WE:2 * WE]).then_inc(s("ld_last"), 16)
            sp.dma_start(b2b, b2.rearrange("(o e) c -> o e c", o=1).broadcast_to((P, E, C)))\
              .then_inc(s("ld_b2"), 16)
            store_res1(B - 1, B)
            sp.wait_ge(s("rows_kept"), 2 * B)
            sp.wait_ge(s("pick_kept"), B)
            sp.dma_start(WB[:, E - 2], late_d[:, 0:WE]).then_inc(s("ld_last"), 16)
            sp.wait_ge(s("st_res1"), FREE + 16 * B)
            sp.wait_ge(s("ld_nm00"), 16 * (B + 1))
            for f, g in ((1, 0), (0, 1), (1, 1)):
                sp.wait_ge(s(f"ld_nm{g}{f}"), 16 * B)

            sp.wait_ge(s("phase_b"), 1)
            sp.wait_ge(s("table_kept"), 1)
            sp.wait_ge(s("zero_kept"), 1)
            for e in range(E):
                r = sp.value_load(zrow[0:1, e:e + 1], min_val=0, max_val=E * REGION - TT)
                sp.dma_start(list_d[bass.ds(r, TT), :].rearrange("(a p) c -> p a c", p=P), zero)\
                  .then_inc(s("st_zero"), 16)
            sp.wait_ge(s("st_zero"), 16 * E)
            sp.wait_ge(s("st_list"), 16 * 2 * NT * B)

            def load_rows(t, u, n_before):
                r = sp.value_load(tile_row[0:1, t], min_val=0, max_val=E * REGION - TT)
                sp.dma_start(xs[u], list_d[bass.ds(r, TT), :].rearrange("(a p) (s c) -> p a s c", p=P, s=2))\
                  .then_inc(s(f"ld_xs{u}"), 16)

            load_rows(slice(0, 1), 0, 0)
            load_rows(slice(1, 2), 1, 0)
            with sp.Fori(0, (TILES - 1) // 2) as i:
                for u in range(2):
                    sp.wait_ge(s("xT_made"), i * 2 + (u + 1))
                    if u == 0:
                        load_rows(bass.ds(i * 2 + 2, 1), u, None)
                    else:
                        load_rows(bass.ds(i * 2 + 3, 1), u, None)
                    sp.wait_ge(s("y_kept"), FREE + i * 2 + (u + 1))
                    sp.dma_start(y_d[bass.ds(i * (2 * TT) + u * TT, TT), :]
                                 .rearrange("(a p) c -> p a c", p=P), ysb[u]).then_inc(s(f"st_y{u}"), 16)
            sp.wait_ge(s("y_kept"), FREE + TILES)
            sp.dma_start(y_d[(TILES - 1) * TT:TILES * TT, :].rearrange("(a p) c -> p a c", p=P), ysb[0])\
              .then_inc(s("st_y0"), 16)

            ov = out.rearrange("b (c p) h w -> b p c (h w)", p=P)
            with sp.Fori(0, B) as b:
                for f in range(2):
                    sp.wait_ge(s("fT_made"), FREE + b * 2)
                    sp.dma_start(tf[f], res1_d[bass.ds(b * N + f * HALF, HALF), :]
                                 .rearrange("(t p) c -> p t c", p=P)).then_inc(s(f"ld_t{f}"), 16)
                for f in range(2):
                    sp.wait_ge(s("f_out"), FREE + b * 2 + (f + 1))
                    sp.dma_start(ov[bass.ds(b, 1), :, :, f * HALF:(f + 1) * HALF]
                                 .rearrange("o p c n -> p (o c) n"), ob[f]).then_inc(s(f"st_out{f}"), 16)
            sp.wait_ge(s("st_out0"), FREE + 16 * B)
            sp.wait_ge(s("st_out1"), FREE + 16 * B)

        @block.gpsimd
        def _(pool):
            def one_where(m, op, base):
                pool.affine_select(out=m[:, :], in_=m[:, :], compare_op=op, fill=1.0, base=base,
                                   pattern=[[-1, P]], channel_multiplier=1)
            for m in (identf, ident16, below16):
                pool.memset(m[:, :], 0.0)
            pool.memset(ones16[:, :], 1.0)
            pool.memset(onesf[:, :], 1.0)
            pool.drain()
            one_where(identf, ALU.not_equal, 0)
            one_where(ident16, ALU.not_equal, 0)
            one_where(below16, ALU.is_ge, 0)
            for e in range(E):
                pool.memset(w8[:, e:e + 1], float(E - e))
                pool.memset(ebase[:, e:e + 1], float(REGION * e))
            pool.drain()
            pool.sem_inc(s("pool_const"), 1)

            parts = []
            for e in [E - 2, E - 1] + list(range(E - 2)):
                for c in range(CC):
                    parts.append((e, w1[e].rearrange("(c p) n -> p c n", p=P)[:, c, :], c * HID, CC * HID))
                for c in range(2):
                    src = w2[e].rearrange("(k p) n -> p k n", p=P)[:, c * 4:c * 4 + 4, :]
                    parts.append((e, src, 2 * CC * HID + c * HID, HC * C))

            def load_part(i):
                dst = stage[:, i % 2, :]
                if parts[i][2] >= 2 * CC * HID:
                    dst = dst.rearrange("p (k n) -> p k n", k=4)
                pool.dma_start(dst, parts[i][1]).then_inc(s(f"ld_stage{i % 2}"), 16)

            load_part(0)
            load_part(1)
            for i, (e, _, at, gap) in enumerate(parts):
                hi, lo = WB[:, e, at:at + HID], WB[:, e, at + gap:at + gap + HID]
                pool.wait_ge(s("split_hi"), i + 1)
                pool.tensor_tensor(lo, stage[:, i % 2, :], hi, ALU.subtract).then_inc(s("split_lo"), 1)
                pool.wait_ge(s("split_lo"), i + 1)
                if i + 2 < len(parts):
                    load_part(i + 2)
                if i == 7:
                    pool.dma_start(late_d[:, :], LATEW).then_inc(s("st_last"), 16)

            def normalise(g, f, n):
                out_at = OS[:, g, f * HALF:(f + 1) * HALF]
                pool.wait_ge(s("rin_kept"), n + 1)
                pool.tensor_tensor(out_at, out_at, rin, ALU.mult).then_inc(s("nrm_kept"), 1)

            def tail_low(n):
                for part in range(2):
                    here = slice(part * NT // 2, (part + 1) * NT // 2)
                    pool.wait_ge(s("hi_kept"), n * 2 + (part - 1))
                    pool.tensor_tensor(rows[:, here, 1, :], ln32[:, here], rows[:, here, 0, :], ALU.subtract)\
                        .then_inc(s("rows_kept"), 1)

            def scatter(n):
                pool.wait_ge(s("idx_kept"), FREE + n)
                pool.sem_inc(s("scatter_on"), 1)
                for t in range(NT):
                    for k in range(2):
                        pool.indirect_dma_start(
                            list_d[:, :], bass.IndirectOffsetOnAxis(ap=idx[:, k, t:t + 1], axis=0),
                            rows[:, t].rearrange("p s c -> p (s c)"), None).then_inc(s("st_list"), 16)

            def scattered(n):
                pool.wait_ge(s("st_list"), n * (16 * 2 * NT))
                pool.sem_inc(s("listed"), 1)

            normalise(0, 0, 0)
            normalise(0, 1, 1)
            normalise(1, 0, 2)
            with pool.Fori(1, B) as b:
                normalise(1, 1, b * 4 - 1)
                normalise(0, 0, b * 4)
                tail_low(b)
                normalise(0, 1, b * 4 + 1)
                normalise(1, 0, b * 4 + 2)
                scatter(b)
                scattered(b)
            normalise(1, 1, B * 4 - 1)
            for k in range(B * N // TT):
                pool.memset(thr[:, k:k + 1], float(TT * k))
            pool.iota(seq.bitcast(I32), pattern=[[1, TABLE]], base=0, channel_multiplier=0)
            pool.memset(one8, 1.0)
            pool.memset(zero, 0.0)
            pool.drain()
            pool.sem_inc(s("zero_kept"), 1)
            tail_low(B)
            scatter(B)
            scattered(B)

            pool.wait_ge(s("slot_kept"), 1)
            pool.wait_ge(s("st_y0"), FREE + 16 * ((TILES + 1) // 2))
            pool.wait_ge(s("st_y1"), FREE + 16 * (TILES // 2))
            with pool.Fori(0, B) as b:
                pool.wait_ge(s("idx_now"), b + 1)
                for f in range(2):
                    pool.wait_ge(s("f_kept"), FREE + b * 2)
                    pool.sem_inc(s("gather_on"), 1)
                    for t in range(4):
                        for k in range(2):
                            pool.indirect_dma_start(
                                yg[f][:, k, t], None, y_d[:, :],
                                bass.IndirectOffsetOnAxis(ap=slot_now[:, k, 4 * f + t:4 * f + t + 1], axis=0))\
                                .then_inc(s(f"ld_y{f}"), 16)

        @block.scalar
        def _(act):
            act.wait_ge(s("dve_prep"), 1)
            act.activation(vec[:, 24:27], vec[:, 24:27], ACT.Sqrt).then_inc(s("act_prep"), 1)
            act.wait_ge(s("dve_prep"), 2)

            def keep_q(n):
                act.wait_ge(s("q_made"), n + 1)
                act.activation(q_sb, PP[0][:, :], ACT.Identity, bias=vec[:, BQ:BQ + 1]).then_inc(s("q_kept"), 1)

            def keep_v(n):
                act.wait_ge(s("v_made"), n + 1)
                act.activation(v_sb, PP[1][:, :], ACT.Identity, bias=vec[:, BV:BV + 1]).then_inc(s("v_kept"), 1)

            def split_weights(b, i):
                w = stage[:, i % 2, :]
                e = (b * 2 + (E - 2 + i // 4)) % E
                at = (i % 2) * HID + (0 if i % 4 < 2 else 2 * CC * HID)
                act.wait_ge(s(f"ld_stage{i % 2}"), 16 * (b * 4 + (i // 2 + 1)))
                hi = WB[:, bass.ds(e, 1), at:at + HID].rearrange("p o n -> p (o n)")
                act.activation(hi, w, ACT.Copy, scale=WSCALE)
                act.activation(w, w, ACT.Copy, scale=WSCALE).then_inc(s("split_hi"), 1)

            def tokens(b, last):
                for i in range(NT):
                    act.wait_ge(s("max_kept"), b * NT + (i + 1))
                    if i >= 3:
                        act.wait_ge(s("av_made"), b * NT + (i - 2))
                    act.activation(prob[i % 3], PP[i % 3][:, :], ACT.Exp, bias=nmax[:, i:i + 1],
                                   accum_out=rsum[:, i:i + 1]).then_inc(s("exp_kept"), 1)
                    if i % 2 == 0:
                        split_weights(b, i // 2)
                split_weights(b, 4)
                for c in range(CC):
                    act.wait_ge(s("cv_kept"), b * 2 + (c + 1))
                    act.activation(X[:, c], X[:, c], ACT.Relu, bias=vec[:, BE2 + c:BE2 + c + 1])\
                       .then_inc(s("x1_kept"), 1)
                act.wait_ge(s("tk_made"), FREE + b * 2 + 1)
                act.wait_ge(s("st_v"), FREE + b * 16)
                act.activation(tok[:, 0:4], PP[2][:, :].rearrange("p (t c) -> p t c", t=4), ACT.Copy)\
                   .then_inc(s("tk_kept_a"), 1)
                act.wait_ge(s("stat_kept"), b + 1)
                act.activation(small[:, 2], small[:, 1], ACT.Sqrt).then_inc(s("sd_kept"), 1)
                if not last:
                    keep_q(b + 1)
                    keep_v(b + 1)
                split_weights(b, 5)
                act.wait_ge(s("lnT_made"), b * 2 + 1)
                act.activation(lnT[:, 0], PP[0][:, :], ACT.Copy).then_inc(s("lnT_kept_a"), 1)
                for u in range(4):
                    act.wait_ge(s("qk_made"), b * 4 + (u + 1))
                    if u >= 2:
                        act.wait_ge(s(f"st_q{u % 2}"), FREE + b * 64 + 32)
                    act.activation(qs[:, u % 2, 0], PP[(u + 2) % 4][:, :], ACT.Copy,
                                   scale=C ** -0.5 if u < 2 else 1.0).then_inc(s("qhi_kept"), 1)
                    if u < 2:
                        split_weights(b, 6 + u)
                act.wait_ge(s("vt_made"), b * 2 + 1)
                act.wait_ge(s("st_res0"), FREE + b * 16 + 16)
                act.activation(VT[:, 0:4], PP[2][:, :].rearrange("p (t c) -> p t c", t=4), ACT.Copy)\
                   .then_inc(s("vt_kept_a"), 1)

            keep_q(0)
            keep_v(0)
            with act.Fori(0, B - 1) as b:
                tokens(b, False)
            tokens(B - 1, True)

            def tail_deviations(n):
                act.wait_ge(s("stat1_kept"), n)
                act.activation(small[:, 2], small[:, 1], ACT.Sqrt).then_inc(s("sd1_kept"), 1)

            def tail_norm(part, n):
                if part == 0:
                    act.wait_ge(s("rstd_kept"), n)
                for t in range(part * NT // 4, (part + 1) * NT // 4):
                    op = act.activation(ln32[:, t], t1[:, t], ACT.Identity,
                                        bias=small[:, 4, t:t + 1], scale=small[:, 3, t:t + 1])
                op.then_inc(s("ln1_kept"), 1)

            def tail_high(part, n):
                act.wait_ge(s("ln1_kept"), n * 4 + (2 * part - 2))
                if part == 0:
                    act.wait_ge(s("listed"), n)
                here = slice(part * NT // 2, (part + 1) * NT // 2)
                act.activation(rows[:, here, 0, :], ln32[:, here], ACT.Copy).then_inc(s("hi_kept"), 1)

            def keep_sums(g, f, n):
                act.wait_ge(s("pv_made"), n * 8 + (FREE + 8))
                act.wait_ge(s("nrm_kept"), FREE + n)
                act.activation(OS[:, g, f * HALF:(f + 1) * HALF], PP[2][:, 0:HALF], ACT.Copy)
                act.activation(rin, PP[2][:, HALF:2 * HALF], ACT.Copy).then_inc(s("sum_kept"), 1)

            def tail_gate(n):
                act.wait_ge(s("pick_kept"), n)
                act.activation(rs[:, 2], rs[:, 2], ACT.Exp, scale=1.0 / WSCALE).then_inc(s("gexp_kept"), 1)

            def attend(b, first):
                for g in range(GROUPS):
                    for st in range(16):
                        if not (first and g + st == 0):
                            act.wait_ge(s("pv_made"), b * 32 + (FREE + g * 16 + st - 1))
                        for pr in range(2):
                            act.wait_ge(s("st_made"), b * 64 + (g * 32 + st * 2 + pr + 1))
                            act.activation(PR[:, st % 2, 2 * pr:2 * pr + 2], PP[pr][:, :]
                                           .rearrange("p (h n) -> p h n", h=2), ACT.Exp).then_inc(s("e_kept"), 1)
                        if st % 8 == 0 and not (first and g + st == 0):
                            keep_sums(*divmod((g * 2 + st // 8 - 1) % 4, 2), b * 4 + (g * 2 + st // 8 - 1))
                        if not first and g * 16 + st == SD_AT:
                            tail_deviations(b)
                        if not first and g * 16 + st in NORM_AT:
                            tail_norm(NORM_AT.index(g * 16 + st), b)
                        if not first and g * 16 + st in HIGH_AT:
                            tail_high(HIGH_AT.index(g * 16 + st), b)
                        if not first and g * 16 + st == GATE_AT:
                            tail_gate(b)

            attend(0, True)
            with act.Fori(1, B) as b:
                attend(b, False)
            keep_sums(1, 1, 4 * B - 1)
            tail_deviations(B)
            for part in range(4):
                tail_norm(part, B)
            tail_high(0, B)
            tail_high(1, B)
            tail_gate(B)

            act.wait_ge(s("table_kept"), 1)

            def gelus(t, u, at):
                e = act.value_load(tile_e[0:1, at], min_val=0, max_val=E - 1)
                for k in range(HC):
                    act.wait_ge(s("h_made"), t * HC + (k + 1))
                    act.activation(hid[u][:, k], hidden_bank(k), ACT.Gelu,
                                   bias=b1c[:, bass.ds(e, 1), k], scale=1.0 / WSCALE)\
                       .then_inc(s("h_kept"), 1)

            gelus(0, 0, slice(0, 1))
            with act.Fori(0, (TILES - 1) // 2) as i:
                for u in (1, 0):
                    act.wait_ge(s("hs_kept"), FREE + i * 8 + (0 if u else 4))
                    gelus(i * 2 + (1 if u else 2), u, bass.ds(i * 2 + (1 if u else 2), 1))

            with act.Fori(0, B) as b:
                for f in range(2):
                    act.wait_ge(s("fT_made"), FREE + b * 2 + (f + 1))
                    act.wait_ge(s(f"st_out{f}"), FREE + b * 16)
                    act.activation(ob[f], PP[f][:, :].rearrange("p (c n) -> p c n", c=CC), ACT.Copy)\
                       .then_inc(s("f_out"), 1)

        @block.tensor
        def _(pe):
            def product(dst, pairs, sem_name=None):
                for n, (lhsT, rhs) in enumerate(pairs):
                    mm = pe.matmul(dst, lhsT, rhs, start=(n == 0), stop=(n == len(pairs) - 1))
                if sem_name:
                    mm.then_inc(s(sem_name), 1)

            pe.wait_ge(s("pool_const"), 1)
            pe.wait_ge(s("ld_w"), 16 * LOADS)
            for c in range(CC):
                cols = slice(c * P, (c + 1) * P)
                pe.transpose(PP[0][:, c * P:(c + 1) * P], wq_raw[:, cols], identf[:, :])
                pe.transpose(PP[0][:, 256 + c * P:256 + (c + 1) * P], wv_raw[:, cols], identf[:, :])
                pe.transpose(PP[0][:, 512 + c * P:512 + (c + 1) * P], wo_raw[:, c], identf[:, :])
            pe.transpose(PP[0][:, 896:896 + E * HC], b1_raw, identf[0:E * HC, 0:E * HC])
            pe.transpose(PP[0][:, 768:896], wwg_raw, identf[:, :]).then_inc(s("pe_prep"), 1)
            pe.wait_ge(s("dve_prep"), 1)
            for c in range(CC):
                product(PP[1][:, c * P:(c + 1) * P], [(wk_raw[:, c * P:(c + 1) * P], wwgT)])
            product(PP[1][:, 512:640], [(bkr, wwgT)], "pe_prep")
            pe.wait_ge(s("dve_prep"), 2)

            def halves(dst, w, src, sem_name):
                for h in range(2):
                    n = slice(h * HALF, (h + 1) * HALF)
                    product(dst[:, n], [(w(c), src[:, c, n]) for c in range(CC)],
                            sem_name if h else None)

            def project_x(n, first):
                for c in range(CC):
                    pe.wait_ge(s(f"ld_x{c}"), n * 16 + 16)
                    for dst, w, name in ((PP[0], wqT, "q_made"), (PP[1], wvT, "v_made")):
                        for h in range(2):
                            here = slice(h * HALF, (h + 1) * HALF)
                            mm = pe.matmul(dst[:, here], w[:, c], X[:, c, here],
                                           start=(c == 0), stop=(c == CC - 1))
                        if c == CC - 1:
                            mm.then_inc(s(name), 1)
                if not first:
                    pe.wait_ge(s("tk_kept_a"), n)
                for t in range(NT):
                    at = slice(t * P, (t + 1) * P)
                    product(PP[2][:, at], [(X[:, c, at], kwT[:, c]) for c in range(CC)],
                            "k_made" if t == NT - 1 else None)

            def tokens(b, last):
                def scores(i):
                    if i == 0:
                        pe.wait_ge(s("q_kept"), b + 1)
                        pe.wait_ge(s("v_kept"), b + 1)
                        pe.wait_ge(s("qhi_kept"), FREE + b * 4)
                        pe.wait_ge(s("qlo_kept"), FREE + b * 4)
                    elif i == 2:
                        pe.wait_ge(s("k_kept"), b + 1)
                        pe.wait_ge(s("vt_kept_a"), FREE + b)
                    elif i >= 3:
                        pe.wait_ge(s("exp_kept"), b * NT + (i - 2))
                    for h in range(2):
                        product(PP[i % 3][:, h * HALF:(h + 1) * HALF],
                                [(v_sb[:, i * P:(i + 1) * P], q_sb[:, h * HALF:(h + 1) * HALF])],
                                "sc_made" if h else None)

                def weigh(i):
                    pe.wait_ge(s("exp_kept"), b * NT + (i + 1))
                    pe.wait_ge(s("ks_kept"), b * NT + (i + 1))
                    if i == 0:
                        pe.wait_ge(s("vt_kept_v"), FREE + b)
                    for h in range(2):
                        mm = pe.matmul(PP[3][:, h * HALF:(h + 1) * HALF], kTs[:, i % 3],
                                       prob[i % 3][:, h * HALF:(h + 1) * HALF],
                                       start=(i == 0), stop=(i == NT - 1))
                    mm.then_inc(s("av_made"), 1)

                scores(0)
                scores(1)
                for i in range(NT):
                    if i + 2 < NT:
                        scores(i + 2)
                    weigh(i)
                for c in range(CC):
                    for h in range(2):
                        pe.wait_ge(s("y1_kept"), b * 2 + (h + 1))
                        product(PP[c][:, h * HALF:(h + 1) * HALF], [(woT[:, c], y1[:, h * HALF:(h + 1) * HALF])],
                                "cv_made" if h else None)
                for c in range(CC):
                    pe.wait_ge(s("x1_kept"), b * 2 + (c + 1))
                    for t in range(NT):
                        mm = pe.transpose(PP[2 + t // 4][:, (t % 4) * C + c * P:(t % 4) * C + (c + 1) * P],
                                          X[:, c, t * P:(t + 1) * P], identf[:, :])
                        if t % 4 == 3 and c == CC - 1:
                            mm.then_inc(s("tk_made"), 1)
                    pe.drain()
                    pe.sem_inc(s("x_used"), 1)
                if not last:
                    project_x(b + 1, False)
                    pe.wait_ge(s("q_kept"), b + 2)
                    pe.wait_ge(s("v_kept"), b + 2)
                for c in range(CC):
                    for t in range(NT):
                        pe.wait_ge(s("ln_kept"), b * NT + (t + 1)) if c == 0 else None
                        mm = pe.transpose(PP[c][:, t * P:(t + 1) * P], ln[:, t, c * P:(c + 1) * P], identf[:, :])
                    mm.then_inc(s("lnT_made"), 1)
                pe.wait_ge(s("lnT_kept_a"), b + 1)
                pe.wait_ge(s("lnT_kept_v"), b + 1)
                if not last:
                    pe.wait_ge(s("k_kept"), b + 2)
                for u in range(4):
                    halves(PP[(u + 2) % 4], lambda c: wqkv_sb[:, c, u * P:(u + 1) * P], lnT, "qk_made")
                for t in range(NT):
                    if t % 4 == 0:
                        pe.wait_ge(s("qhi_kept"), FREE + b * 4 + (t // 4 + 1))
                        pe.wait_ge(s("qlo_kept"), FREE + b * 4 + (t // 4 + 1))
                    product(PP[2 + t // 4][:, (t % 4) * C:(t % 4 + 1) * C],
                            [(lnT[:, c, t * P:(t + 1) * P], wqkv_sb[:, c, 2 * C:3 * C]) for c in range(CC)],
                            "vt_made" if t % 4 == 3 else None)

            project_x(0, True)
            with pe.Fori(0, B - 1) as b:
                tokens(b, False)
            tokens(B - 1, True)

            uses = [0]

            def next_bank(before):
                at = uses[0]
                uses[0] += 1
                if not isinstance(before, int) or before + at >= 2:
                    pe.wait_ge(s("c_kept"), before + (at - 1))
                return shared_bank(at + parity(before))

            def max_half(n, k, f, par, before):
                h, i = n // 4, n % 4
                pe.matmul(next_bank(before), QP[0:QK_ROWS, par, f, h, i * P:(i + 1) * P],
                          KP[par][0:QK_ROWS, h, k * HALF:(k + 1) * HALF],
                          start=True, stop=True).then_inc(s("c_made"), 1)

            def max_row(f, before, n):
                bank = next_bank(before)
                pe.wait_ge(s("nm_kept"), n)
                pe.transpose(bank[0:16, 0:P], mx[:, f], identf[:, :]).then_inc(s("c_made"), 1)

            def tail_project(c, before, n):
                bank = next_bank(before)
                pe.wait_ge(s("nrm_kept"), FREE + n * 4 - (1 if c < 2 else 0))
                for t in range(2):
                    tok_at = slice((2 * c + t) * P, (2 * c + t + 1) * P)
                    product(bank[:, t * C:(t + 1) * C], [(OS[:, k, tok_at], wo_sb[:, k]) for k in range(CC)],
                            "c_made" if t else None)

            def tail_turn(c, before, n):
                bank = next_bank(before).bitcast(F16)
                pe.wait_ge(s("rows_kept"), n * 2 - (1 if c < 2 else 0))
                for t in range(2):
                    for q in range(4):
                        mm = pe.transpose(bank[:, (4 * t + q) * P:(4 * t + q + 1) * P],
                                          rows[:, 2 * c + t, q // 2, (q % 2) * P:(q % 2 + 1) * P], ident16[:, :])
                mm.then_inc(s("c_made"), 1)

            def tail_logits(before):
                bank = next_bank(before)
                pe.wait_ge(s("c_kept"), before + (uses[0] - 1))
                for t in range(NT):
                    product(bank[:, t * 2 * E:(t + 1) * 2 * E],
                            [(lnr[:, t, q], wr16[:, q % 2].rearrange("p s e -> p (s e)")) for q in range(4)],
                            "c_made" if t == NT - 1 else None)

            def tail_ranks(before, n):
                bank = next_bank(before)
                pe.wait_ge(s("pick_kept"), n)
                product(bank[:, 0:NT * E], [(below16[:, :], pick16[:, :, :].rearrange("p t e -> p (t e)")),
                                            (ones16[:, :], cum16[:, 0:NT, :].rearrange("p t e -> p (t e)"))],
                        "c_made")

            def attend(b, first):
                before = ROW_USES if first else b * (2 * GROUP_USES + TAIL_USES) + (ROW_USES - TAIL_USES)
                uses[0] = 0

                def weigh_heads(g, st):
                    par, f, j = g % 2, st // 8, st % 8
                    pe.wait_ge(s("e_kept"), b * 64 + (g * 32 + st * 2 + 2))
                    if j == 0:
                        pe.wait_ge(s("sum_kept"), b * 4 + (FREE + g * 2 + f))
                    for h in range(GH):
                        pe.matmul(PP[2][h * D:(h + 1) * D, 0:HALF], VV[par][:, j, h * D:(h + 1) * D],
                                  PR[:, st % 2, h], start=(j == 0), stop=(j == 7))

                def sum_heads(st):
                    for h in range(GH):
                        mm = pe.matmul(PP[2][h * D:(h + 1) * D, HALF:2 * HALF], onesf[:, :],
                                       PR[:, st % 2, h], start=(st % 8 == 0), stop=(st % 8 == 7))
                    mm.then_inc(s("pv_made"), 1)

                for g in range(GROUPS):
                    for st in range(16):
                        f, j = st // 8, st % 8
                        if st == 0:
                            pe.wait_ge(s(f"ld_g{g}"), b * LOAD_GROUP + LOAD_GROUP)
                        if j == 0:
                            pe.wait_ge(s(f"ld_nm{g}{f}"), b * 16 + 16)
                        more, mf, _ = MAX_AT[st][0]
                        mg = (g + more) % 2
                        halves = [(n, k) for _, _, n in MAX_AT[st] for k in range(2)]
                        for pr in range(2):
                            if not (first and g + st == 0):
                                pe.wait_ge(s("e_kept"), b * 64 + (g * 32 + st * 2 + pr - 1))
                            for h in (2 * pr, 2 * pr + 1):
                                mm = pe.matmul(PP[pr][:, (h % 2) * HALF:(h % 2 + 1) * HALF],
                                               KP[g][0:QK_ROWS + 1, h, j * P:(j + 1) * P],
                                               QP[0:QK_ROWS + 1, g, f, h, :], start=True, stop=True)
                            mm.then_inc(s("st_made"), 1)
                            if st == 4 and pr == 0:
                                pe.wait_ge(s(f"ld_g{1 - g}"), b * LOAD_GROUP + LOAD_GROUP * (g + 1))
                            max_half(*halves[pr], mf, mg, before)
                        weighs = st > 0 or g > 0 or not first
                        if weighs:
                            weigh_heads(g if st else g - 1, (st - 1) % 16)
                        max_half(*halves[2], mf, mg, before)
                        if st in ROW_AT:
                            max_row(1 - f, before, b * 4 + (2 * g + f + 2))
                        if weighs:
                            sum_heads((st - 1) % 16)
                        max_half(*halves[3], mf, mg, before)
                        at = g * 16 + st
                        if not first:
                            if at in PROJECT_AT:
                                tail_project(PROJECT_AT.index(at), before, b)
                            if at in TURN_AT:
                                tail_turn(TURN_AT.index(at), before, b)
                            if at == LOGIT_AT:
                                tail_logits(before)
                            if at == RANK_AT:
                                tail_ranks(before, b)
                if not first:
                    assert uses[0] == 2 * GROUP_USES + TAIL_USES

            pe.wait_ge(s("ld_g0"), LOAD_GROUP)
            for name, n in (("vt_kept_v", 1), ("vt_kept_a", 1), ("qlo_kept", 4)):
                pe.wait_ge(s(name), FREE + n * B)
            for n in range(32):
                max_half(n // 2, n % 2, 0, 0, 0)
            max_row(0, 0, 1)
            for n in range(16):
                max_half(n // 2, n % 2, 1, 0, 0)
            pe.wait_ge(s("kone_kept"), 2)
            attend(0, True)
            with pe.Fori(1, B) as b:
                attend(b, False)
            pe.wait_ge(s("e_kept"), B * 64)
            for lhsT, at in ((VV[1][:, 7], 0), (None, HALF)):
                for h in range(GH):
                    mm = pe.matmul(PP[2][h * D:(h + 1) * D, at:at + HALF],
                                   onesf[:, :] if lhsT is None else lhsT[:, h * D:(h + 1) * D],
                                   PR[:, 1, h], start=False, stop=True)
            mm.then_inc(s("pv_made"), 1)
            before = B * (2 * GROUP_USES + TAIL_USES) + (ROW_USES - TAIL_USES)
            uses[0] = 0
            for c in range(4):
                tail_project(c, before, B)
            for c in range(4):
                tail_turn(c, before, B)
            tail_logits(before)
            tail_ranks(before, B)

            pe.wait_ge(s("idx_kept"), FREE + B)
            product(PP[0][:, 0:E], [(ones16[:, :], cum16[:, 0, :])], "cnt_made")
            pe.wait_ge(s("table_kept"), 1)
            pe.wait_ge(s("ld_last"), 32)

            def expert(at):
                return pe.value_load(tile_e[0:1, at], min_val=0, max_val=E - 1)

            def weights(e, off, n):
                return WB[:, bass.ds(e, 1), off:off + n].rearrange("p o n -> p (o n)")

            def turn(t, u, n_load):
                pe.wait_ge(s(f"ld_xs{u}"), n_load)
                if not (isinstance(t, int) and t < 2):
                    pe.wait_ge(s("xT_kept"), t - 1)
                for q in range(4):
                    for a in range(2):
                        at = q * TT + a * P
                        mm = pe.transpose(turned_bank(u)[:, at:at + P],
                                          xs[u][:, a, q // 2, (q % 2) * P:(q % 2 + 1) * P], ident16[:, :])
                mm.then_inc(s("xT_made"), 1)

            MEET = ((0, 0), (0, 1), (1, 0))

            def first(t, u, e):
                pe.wait_ge(s("xT_kept"), t + 1)
                for k in range(HC):
                    if not (isinstance(t, int) and k < 4):
                        pe.wait_ge(s("h_kept"), t * HC + (k - 3))
                    product(hidden_bank(k),
                            [(weights(e, (w * CC + c) * HID + k * P, P), xT[u][:, d * CC + c])
                             for w, d in MEET for c in range(CC)], "h_made")

            def second(t, u, e):
                pe.wait_ge(s("hs_kept"), FREE + t * 4 + 4)
                for a in range(2):
                    product(PP[2][:, u * HALF + a * C:u * HALF + (a + 1) * C],
                            [(hs[u][:, d, k, a * P:(a + 1) * P], weights(e, 2 * CC * HID + (w * HC + k) * C, C))
                             for w, d in MEET for k in range(HC)], "y_made" if a else None)

            turn(0, 0, 16)
            first(0, 0, expert(slice(0, 1)))
            turn(1, 1, 16)
            with pe.Fori(0, (TILES - 1) // 2) as i:
                e0 = expert(bass.ds(i * 2, 1))
                e1 = expert(bass.ds(i * 2 + 1, 1))
                e2 = expert(bass.ds(i * 2 + 2, 1))
                first(i * 2 + 1, 1, e1)
                turn(i * 2 + 2, 0, i * 16 + 32)
                pe.wait_ge(s("y_kept"), FREE + i * 2)
                second(i * 2, 0, e0)
                first(i * 2 + 2, 0, e2)
                turn(i * 2 + 3, 1, i * 16 + 32)
                pe.wait_ge(s("y_kept"), FREE + i * 2)
                second(i * 2 + 1, 1, e1)
            pe.wait_ge(s("y_kept"), FREE + TILES - 2)
            second(TILES - 1, 0, expert(slice(TILES - 1, TILES)))

            with pe.Fori(0, B) as b:
                for f in range(2):
                    pe.wait_ge(s("f_kept"), FREE + b * 2 + (f + 1))
                    pe.wait_ge(s("f_out"), FREE + b * 2)
                    for c in range(CC):
                        for t in range(4):
                            mm = pe.transpose(PP[f][:, c * HALF + t * P:c * HALF + (t + 1) * P],
                                              tf[f][:, t, c * P:(c + 1) * P], identf[:, :])
                    mm.then_inc(s("fT_made"), 1)

        @block.vector
        def _(dve):
            def per_tile(a):
                return a.unsqueeze(2).broadcast_to((P, a.shape[1], E))

            def per_expert(a, n):
                return a.unsqueeze(1).broadcast_to((P, n, E))

            dve.wait_ge(s("pe_prep"), 1)
            dve.wait_ge(s("ld_w"), 16 * LOADS)
            for dst, at in ((wqT, 0), (wvT, 256), (woT, 512)):
                dve.tensor_copy(dst, PP[0][:, at:at + 256].rearrange("p (c n) -> p c n", c=CC))
            dve.tensor_copy(b1c[:, :, :], PP[0][:, 896:896 + E * HC].rearrange("p (e k) -> p e k", e=E))
            dve.tensor_copy(wwgT, PP[0][:, 768:896])
            dve.tensor_scalar(bkr, identf[:, :], 0.0, vec[:, BK:BK + 1], ALU.mult, ALU.add)
            dve.tensor_scalar(vec[:, 24:25], vec[:, V1:V1 + 1], EPS, None, ALU.add)
            dve.tensor_scalar(vec[:, 25:27], vec[:, V2:V2 + 2], EPS, None, ALU.add)
            dve.tensor_scalar(wr16[:, :, 0, :], wr_raw, WSCALE, None, ALU.mult)
            dve.memset(cum16[:, 0, :], 0.0)
            dve.drain()
            dve.scalar_tensor_tensor(out=wr16[:, :, 1, :], in0=wr_raw, scalar=WSCALE, in1=wr16[:, :, 0, :],
                                     op0=ALU.mult, op1=ALU.subtract).then_inc(s("dve_prep"), 1)
            dve.wait_ge(s("act_prep"), 1)
            dve.reciprocal(vec[:, 27:30], vec[:, 24:27])
            dve.drain()
            dve.tensor_tensor(vec[:, S1:S1 + 1], vec[:, 27:28], vec[:, G1:G1 + 1], ALU.mult)
            dve.tensor_tensor(vec[:, S2:S2 + 2], vec[:, 28:30], vec[:, G2:G2 + 2], ALU.mult)
            dve.tensor_tensor(vec[:, BO:BO + 2], vec[:, BO:BO + 2], vec[:, M2:M2 + 2], ALU.subtract)
            dve.drain()
            dve.tensor_tensor(vec[:, M1:M1 + 1], vec[:, M1:M1 + 1], vec[:, S1:S1 + 1], ALU.mult)
            dve.tensor_tensor(vec[:, BO:BO + 2], vec[:, BO:BO + 2], vec[:, S2:S2 + 2], ALU.mult)
            dve.drain()
            dve.tensor_tensor(vec[:, BE1:BE1 + 1], vec[:, BB1:BB1 + 1], vec[:, M1:M1 + 1], ALU.subtract)
            dve.tensor_tensor(vec[:, BE2:BE2 + 2], vec[:, BO:BO + 2], vec[:, BB2:BB2 + 2], ALU.add)
            dve.wait_ge(s("pe_prep"), 2)
            dve.tensor_copy(kwT, PP[1][:, 0:256].rearrange("p (c n) -> p c n", c=CC))
            dve.tensor_copy(kb, PP[1][:, 512:640])
            dve.drain()
            dve.sem_inc(s("dve_prep"), 1)

            def statistics(src, out_sem):
                for t in range(NT):
                    dve.bn_stats(bst[:, t], src[:, t])
                dve.drain()
                deviations(out_sem)

            def deviations(out_sem):
                for t in range(NT):
                    dve.bn_aggr(mv[:, t], bst[:, t])
                dve.drain()
                dve.tensor_scalar(small[:, 1], mv[:, :, 1], EPS, None, ALU.add).then_inc(s(out_sem), 1)

            def part_statistics(part):
                dve.drain()
                for t in range(part * NT // 2, (part + 1) * NT // 2):
                    dve.bn_stats(bst[:, t], t1[:, t])
                if part == 1:
                    dve.drain()
                    deviations("stat1_kept")

            def keep_k(n):
                dve.wait_ge(s("k_made"), n + 1)
                dve.tensor_tensor(kT.rearrange("p (t o) -> p t o", t=NT), PP[2][:, :]
                                  .rearrange("p (t o) -> p t o", t=NT),
                                  kb.unsqueeze(1).broadcast_to((P, NT, P)), ALU.add).then_inc(s("k_kept"), 1)

            def tokens(b, last):
                def scale_keys(i):
                    dve.wait_ge(s("exp_kept"), b * NT + (i + 1))
                    dve.reciprocal(rinv[:, i:i + 1], rsum[:, i:i + 1])
                    dve.drain()
                    if i >= 3:
                        dve.wait_ge(s("av_made"), b * NT + (i - 2))
                    dve.tensor_scalar(kTs[:, i % 3], kT[:, i * P:(i + 1) * P], rinv[:, i:i + 1], None,
                                      ALU.mult).then_inc(s("ks_kept"), 1)

                for i in range(NT):
                    dve.wait_ge(s("sc_made"), b * NT + (i + 1))
                    dve.tensor_reduce(nmax[:, i:i + 1], PP[i % 3][:, :], X_AXIS, ALU.max, negate=True)\
                       .then_inc(s("max_kept"), 1)
                    if i:
                        scale_keys(i - 1)
                scale_keys(NT - 1)
                dve.wait_ge(s("av_made"), b * NT + NT)
                for h in range(2):
                    n = slice(h * HALF, (h + 1) * HALF)
                    dve.tensor_scalar(y1[:, n], PP[3][:, n], vec[:, S1:S1 + 1], vec[:, BE1:BE1 + 1],
                                      ALU.mult, ALU.add).then_inc(s("y1_kept"), 1)
                for c in range(CC):
                    dve.wait_ge(s("cv_made"), b * 2 + (c + 1))
                    dve.scalar_tensor_tensor(out=X[:, c], in0=PP[c][:, :], scalar=vec[:, S2 + c:S2 + c + 1],
                                             in1=X[:, c], op0=ALU.mult, op1=ALU.add).then_inc(s("cv_kept"), 1)
                dve.wait_ge(s("tk_made"), FREE + b * 2 + 2)
                dve.wait_ge(s("st_v"), FREE + b * 16)
                dve.tensor_copy(tok[:, 4:8], PP[3][:, :].rearrange("p (t c) -> p t c", t=4))\
                   .then_inc(s("tk_kept_v"), 1)
                dve.drain()
                dve.wait_ge(s("tk_kept_a"), b + 1)
                statistics(tok, "stat_kept")
                dve.wait_ge(s("sd_kept"), b + 1)
                dve.reciprocal(small[:, 3], small[:, 2])
                dve.drain()
                dve.wait_ge(s("st_q0"), FREE + b * 64)
                dve.wait_ge(s("st_q1"), FREE + b * 64)
                for t in range(NT):
                    dve.tensor_scalar(ln[:, t], tok[:, t], mv[:, t, 0:1], small[:, 3, t:t + 1],
                                      ALU.subtract, ALU.mult).then_inc(s("ln_kept"), 1)
                if not last:
                    keep_k(b + 1)
                dve.wait_ge(s("lnT_made"), b * 2 + 2)
                dve.tensor_copy(lnT[:, 1], PP[1][:, :]).then_inc(s("lnT_kept_v"), 1)
                dve.wait_ge(s("ln_kept"), b * NT + NT)
                dve.tensor_tensor(tok, tok, bob.unsqueeze(1).broadcast_to((P, NT, C)), ALU.add)\
                   .then_inc(s("res0_kept"), 1)
                for u in range(4):
                    dve.wait_ge(s("qhi_kept"), FREE + b * 4 + (u + 1))
                    dve.scalar_tensor_tensor(out=qs[:, u % 2, 1], in0=PP[(u + 2) % 4][:, :],
                                             scalar=C ** -0.5 if u < 2 else 1.0, in1=qs[:, u % 2, 0],
                                             op0=ALU.mult, op1=ALU.subtract).then_inc(s("qlo_kept"), 1)
                dve.wait_ge(s("vt_made"), b * 2 + 2)
                dve.wait_ge(s("st_res0"), FREE + b * 16 + 16)
                dve.tensor_copy(VT[:, 4:8], PP[3][:, :].rearrange("p (t c) -> p t c", t=4))\
                   .then_inc(s("vt_kept_v"), 1)

            keep_k(0)
            with dve.Fori(0, B - 1) as b:
                tokens(b, False)
            tokens(B - 1, True)

            for name, n in (("st_v", 16), ("st_q0", 64), ("st_q1", 64), ("st_res0", 16)):
                dve.wait_ge(s(name), FREE + n * B)
            dve.wait_ge(s("split_lo"), 32)
            for par in range(2):
                dve.memset(KP[par][QK_ROWS:QK_ROWS + 1], MSCALE).then_inc(s("kone_kept"), 1)

            uses = [0]

            def bank_made(before):
                at = uses[0]
                uses[0] += 1
                dve.wait_ge(s("c_made"), before + (at + 1))
                return shared_bank(at + parity(before))

            def reduce_half(n, k, before):
                dve.tensor_reduce(mxp[:, n, k:k + 1], bank_made(before), X_AXIS, ALU.max)\
                   .then_inc(s("c_kept"), 1)

            def join_halves(f):
                dve.drain()
                dve.tensor_reduce(mx[:, f], mxp[:, :, :], X_AXIS, ALU.max, negate=True)
                dve.drain()
                dve.tensor_scalar(mx[:, f], mx[:, f], 1.0 / MSCALE, None, ALU.mult).then_inc(s("nm_kept"), 1)

            def keep_row(before, moved, n):
                bank = bank_made(before)
                if moved:
                    dve.wait_ge(s(moved), n)
                dve.tensor_copy(nmr[:, :], bank[0:16, 0:P]).then_inc(s("c_kept"), 1)
                dve.drain()
                dve.sem_inc(s("nmr_kept"), 1)

            logit, oh1, oh2, val, rest, rk, tmp = [rt[:, i] for i in range(7)]

            def tail_project(c, before, n):
                bank = bank_made(before)
                if c == 0:
                    dve.wait_ge(s("ld_res0"), n * 16)
                dve.tensor_tensor(t1[:, 2 * c:2 * c + 2], bank.rearrange("p (t c) -> p t c", t=2),
                                  t1[:, 2 * c:2 * c + 2], ALU.add).then_inc(s("c_kept"), 1)

            def tail_rstd(n):
                dve.wait_ge(s("sd1_kept"), n)
                dve.reciprocal(small[:, 3], small[:, 2])
                dve.drain()
                dve.scalar_tensor_tensor(out=small[:, 4], in0=mv[:, :, 0], scalar=-1.0, in1=small[:, 3],
                                         op0=ALU.mult, op1=ALU.mult).then_inc(s("rstd_kept"), 1)

            def tail_turn(c, before):
                dve.tensor_copy(lnr[:, 2 * c:2 * c + 2], bank_made(before).bitcast(F16)
                                .rearrange("p (t s n) -> p t s n", t=2, s=4)).then_inc(s("c_kept"), 1)

            def tail_logits(before):
                bank = bank_made(before)[:, 0:NT * 2 * E].rearrange("p (t s e) -> p t s e", t=NT, s=2)
                dve.tensor_copy(tmp, bank[:, :, 1])
                dve.drain()
                dve.tensor_tensor(logit, bank[:, :, 0], tmp, ALU.add).then_inc(s("c_kept"), 1)

            def largest(src, top):
                dve.drain()
                dve.tensor_reduce(top, src, X_AXIS, ALU.max)
                dve.drain()
                dve.tensor_tensor(val, src, per_tile(top), ALU.is_equal)
                dve.drain()
                dve.tensor_tensor(val, val, per_expert(w8[:, :], NT), ALU.mult)

            def mark(one_hot):
                dve.drain()
                dve.tensor_reduce(rs[:, 3], val, X_AXIS, ALU.max)
                dve.drain()
                dve.tensor_tensor(one_hot, per_expert(w8[:, :], NT), per_tile(rs[:, 3]), ALU.is_equal)
                dve.drain()

            def tail_pick(part):
                if part == 0:
                    largest(logit, rs[:, 0])
                elif part == 1:
                    mark(oh1)
                    dve.scalar_tensor_tensor(out=rest, in0=oh1, scalar=-BIG, in1=logit, op0=ALU.mult, op1=ALU.add)
                elif part == 2:
                    largest(rest, rs[:, 1])
                else:
                    mark(oh2)
                    dve.tensor_tensor(rs[:, 2], rs[:, 1], rs[:, 0], ALU.subtract)
                    dve.tensor_tensor(pick16[:, :, :], oh1, oh2, ALU.add)
                    dve.drain()
                    for t in range(NT):
                        dve.tensor_tensor(cum16[:, t + 1], cum16[:, t], pick16[:, t], ALU.add)
                        dve.drain()
                    dve.sem_inc(s("pick_kept"), 1)

            def tail_places(before, tail, n):
                here = bass.ds(tail * NT, NT)
                dve.tensor_copy(pick1[:, here, :], oh1)
                dve.tensor_copy(pick2[:, here, :], oh2)
                dve.wait_ge(s("gexp_kept"), n)
                dve.tensor_scalar(rs[:, 3], rs[:, 2], 1.0, None, ALU.add)
                dve.drain()
                dve.reciprocal(rs[:, 4], rs[:, 3])
                dve.drain()
                dve.tensor_copy(gate1[:, here], rs[:, 4])
                dve.tensor_tensor(gate2[:, here], rs[:, 4], rs[:, 2], ALU.mult)
                bank = bank_made(before)
                dve.tensor_copy(rk, bank[:, 0:NT * E].rearrange("p (t e) -> p t e", e=E)).then_inc(s("c_kept"), 1)
                dve.tensor_copy(cum16[:, 0], cum16[:, NT])
                dve.drain()
                dve.tensor_tensor(val, rk, per_expert(ebase[:, :], NT), ALU.add)
                dve.tensor_copy(rank[:, here, :], rk)
                dve.drain()
                dve.tensor_tensor(tmp, val, oh1, ALU.mult)
                dve.tensor_tensor(rest, val, oh2, ALU.mult)
                dve.drain()
                dve.tensor_reduce(rs[:, 0], tmp, X_AXIS, ALU.add)
                dve.tensor_reduce(rs[:, 1], rest, X_AXIS, ALU.add)
                dve.drain()
                dve.wait_ge(s("listed"), n)
                dve.tensor_copy(idx[:, :, :], rs[:, 0:2]).then_inc(s("idx_kept"), 1)
                dve.drain()

            def invert_sums(part, n):
                if part == 0:
                    dve.wait_ge(s("sum_kept"), FREE + (n + 1))
                here = slice(part * P, (part + 1) * P)
                op = dve.reciprocal(rin[:, here], rin[:, here])
                if part == 3:
                    op.then_inc(s("rin_kept"), 1)

            def attend(b, first):
                before = ROW_USES if first else b * (2 * GROUP_USES + TAIL_USES) + (ROW_USES - TAIL_USES)
                uses[0] = 0
                for g in range(GROUPS):
                    for st in range(16):
                        f, j = st // 8, st % 8
                        halves = [(n, k) for _, _, n in MAX_AT[st] for k in range(2)]
                        reduce_half(*halves[0], before)
                        reduce_half(*halves[1], before)
                        if j in INVERT_AT and (not first or g * 2 + f > 0):
                            invert_sums(INVERT_AT.index(j), b * 4 + (g * 2 + f - 1))
                        reduce_half(*halves[2], before)
                        if st in ROW_AT:
                            keep_row(before, f"ld_nm{g}{f}", b * 16 + 16)
                        reduce_half(*halves[3], before)
                        if j == 3:
                            join_halves(1 - f)
                        at = g * 16 + st
                        if not first:
                            if at in PROJECT_AT:
                                tail_project(PROJECT_AT.index(at), before, b)
                            if at in STATS_AT:
                                part_statistics(STATS_AT.index(at))
                            if at == RSTD_AT:
                                tail_rstd(b)
                            if at in TURN_AT:
                                tail_turn(TURN_AT.index(at), before)
                            if at == LOGIT_AT:
                                tail_logits(before)
                            if at in PICK_AT:
                                tail_pick(PICK_AT.index(at))
                            if at == RANK_AT:
                                tail_places(before, b - 1, b)

            for n in range(32):
                reduce_half(n // 2, n % 2, 0)
            join_halves(0)
            keep_row(0, None, 0)
            for n in range(16):
                reduce_half(n // 2, n % 2, 0)
            attend(0, True)
            with dve.Fori(1, B) as b:
                attend(b, False)
            for part in range(4):
                invert_sums(part, 4 * B - 1)
            before = B * (2 * GROUP_USES + TAIL_USES) + (ROW_USES - TAIL_USES)
            uses[0] = 0
            for c in range(4):
                tail_project(c, before, B)
            part_statistics(0)
            part_statistics(1)
            tail_rstd(B)
            for c in range(4):
                tail_turn(c, before)
            tail_logits(before)
            for part in range(4):
                tail_pick(part)
            tail_places(before, B - 1, B)
            dve.wait_ge(s("idx_kept"), FREE + B)
            dve.sem_inc(s("phase_b"), 1)

            dve.wait_ge(s("zero_kept"), 1)
            dve.wait_ge(s("cnt_made"), 1)
            dve.wait_ge(s("ld_b2"), 16)
            dve.tensor_copy(cnt, PP[0][:, 0:E])
            dve.tensor_copy(seqc, seq.bitcast(I32))
            dve.drain()
            over = cmp[:, 0:B * N // TT]
            dve.tensor_tensor(over, per_expert(cnt, B * N // TT), per_tile(thr), ALU.is_gt)
            dve.tensor_tensor(zrowf, cnt, ebase[:, :], ALU.add)
            dve.drain()
            dve.tensor_reduce(lists, over.rearrange("p k e -> p e k"), X_AXIS, ALU.add)
            dve.tensor_copy(zrow, zrowf)
            dve.drain()
            dve.tensor_tensor_scan(incl, one8, lists, 0.0, ALU.mult, ALU.add)
            dve.drain()
            dve.tensor_tensor(start, incl, lists, ALU.subtract)
            dve.tensor_scalar(seq, incl[:, E - 1:E].broadcast_to((P, TABLE)), -1.0, None, ALU.add)
            dve.drain()
            dve.tensor_tensor(seqc, seqc, seq, ALU.min)
            dve.drain()
            dve.tensor_tensor(cmp, per_expert(incl, TABLE), per_tile(seqc), ALU.is_le)
            dve.drain()
            dve.tensor_reduce(te, cmp, X_AXIS, ALU.add)
            dve.drain()
            dve.tensor_tensor(cmp, cmp, per_expert(lists, TABLE), ALU.mult)
            dve.drain()
            dve.tensor_reduce(tk, cmp, X_AXIS, ALU.add)
            dve.drain()
            dve.tensor_tensor(tk, seqc, tk, ALU.subtract)
            dve.tensor_copy(tile_e, te)
            dve.drain()
            dve.tensor_scalar(tk, tk, float(TT), None, ALU.mult)
            dve.drain()
            dve.scalar_tensor_tensor(out=tk, in0=te, scalar=float(REGION), in1=tk, op0=ALU.mult, op1=ALU.add)
            dve.drain()
            dve.tensor_copy(tile_row, tk)
            dve.drain()
            dve.sem_inc(s("table_kept"), 1)
            dve.tensor_scalar(start, start, float(TT), None, ALU.mult)
            dve.drain()
            dve.tensor_tensor(big, rank[:, :, :], per_expert(start, B * NT), ALU.add)
            dve.drain()
            for k, pick in enumerate((pick1, pick2)):
                dve.tensor_tensor(big2, big, pick[:, :, :], ALU.mult)
                dve.drain()
                dve.tensor_reduce(slotf[:, k], big2, X_AXIS, ALU.add)
                dve.drain()
            dve.tensor_copy(slot, slotf)
            dve.drain()
            dve.sem_inc(s("slot_kept"), 1)

            def keep_turned(t, u):
                dve.wait_ge(s("xT_made"), t + 1)
                dve.tensor_copy(xT[u].rearrange("p s n -> p (s n)"), turned_bank(u)).then_inc(s("xT_kept"), 1)

            def split_hidden(t, u):
                for j in range(HC // 2):
                    dve.wait_ge(s("h_kept"), t * HC + (2 * j + 2))
                    k = slice(2 * j, 2 * j + 2)
                    dve.tensor_copy(hs[u][:, 0, k], hid[u][:, k])
                    dve.drain()
                    dve.tensor_tensor(hs[u][:, 1, k], hid[u][:, k], hs[u][:, 0, k], ALU.subtract)\
                       .then_inc(s("hs_kept"), 1)

            def keep_output(t, u, n_store, e):
                dve.wait_ge(s("y_made"), FREE + t + 1)
                if n_store is not None:
                    dve.wait_ge(s(f"st_y{u}"), FREE + n_store)
                dve.scalar_tensor_tensor(
                    out=ysb[u], in0=PP[2][:, u * HALF:(u + 1) * HALF].rearrange("p (a c) -> p a c", a=2),
                    scalar=1.0 / WSCALE, in1=b2b[:, bass.ds(e, 1), :].broadcast_to((P, 2, C)),
                    op0=ALU.mult, op1=ALU.add).then_inc(s("y_kept"), 1)

            def expert(at):
                return dve.value_load(tile_e[0:1, at], min_val=0, max_val=E - 1)

            keep_turned(0, 0)
            split_hidden(0, 0)
            keep_turned(1, 1)
            with dve.Fori(0, (TILES - 1) // 2) as i:
                e0 = expert(bass.ds(i * 2, 1))
                e1 = expert(bass.ds(i * 2 + 1, 1))
                dve.wait_ge(s("y_made"), FREE + i * 2)
                split_hidden(i * 2 + 1, 1)
                keep_turned(i * 2 + 2, 0)
                keep_output(i * 2, 0, i * 16, e0)
                dve.wait_ge(s("y_made"), FREE + i * 2 + 1)
                split_hidden(i * 2 + 2, 0)
                keep_turned(i * 2 + 3, 1)
                keep_output(i * 2 + 1, 1, i * 16, e1)
            keep_output(TILES - 1, 0, 16 * (TILES // 2), expert(slice(TILES - 1, TILES)))

            with dve.Fori(0, B) as b:
                dve.tensor_copy(slot_now, slot[:, :, bass.ds(b * NT, NT)]).then_inc(s("idx_now"), 1)
                dve.tensor_copy(rs[:, 0], gate1[:, bass.ds(b * NT, NT)])
                dve.tensor_copy(rs[:, 1], gate2[:, bass.ds(b * NT, NT)])
                dve.drain()
                for f in range(2):
                    dve.wait_ge(s(f"ld_y{f}"), b * 128 + 128)
                    dve.wait_ge(s(f"ld_t{f}"), b * 16 + 16)
                    for k in range(2):
                        for t in range(4):
                            last = dve.scalar_tensor_tensor(
                                out=tf[f][:, t], in0=yg[f][:, k, t], scalar=rs[:, k, 4 * f + t:4 * f + t + 1],
                                in1=tf[f][:, t], op0=ALU.mult, op1=ALU.add)
                        if k == 0:
                            dve.drain()
                    last.then_inc(s("f_kept"), 1)
                dve.drain()


_INS = ["x", "L0_conv_wk", "L0_conv_bk", "L0_conv_wv", "L0_conv_bv", "L0_conv_wq", "L0_conv_bq",
        "L0_conv_wwg", "L0_conv_bn1_g", "L0_conv_bn1_b", "L0_conv_bn1_m", "L0_conv_bn1_v",
        "L0_conv_wout", "L0_conv_bout", "L0_conv_bn2_g", "L0_conv_bn2_b", "L0_conv_bn2_m",
        "L0_conv_bn2_v", "L1_attn_w_qkv", "L1_attn_w_out", "L1_attn_b_out", "L1_ffn_Wr",
        "L1_ffn_W1", "L1_ffn_b1", "L1_ffn_W2", "L1_ffn_b2"]
_OUTS = [((4, 256, 32, 32), "float32")]


def kernel(**inputs):
    import numpy as _np
    import concourse.bacc as _bacc
    from concourse import mybir as _mybir
    from concourse.bass_utils import run_bass_kernel_spmd as _run

    nc = _bacc.Bacc("TRN2", target_bir_lowering=False, num_devices=1)
    arrays, args = {}, []
    for name in _INS:
        a = _np.ascontiguousarray(inputs[name])
        arrays[f"in_{name}_dram"] = a
        args.append(nc.dram_tensor(f"in_{name}_dram", a.shape, _mybir.dt.from_np(a.dtype), kind="ExternalInput").ap())
    for i, (shape, dtype) in enumerate(_OUTS):
        dt = _mybir.dt.from_np(_np.dtype(dtype))
        args.append(nc.dram_tensor(f"out_{i}_dram", shape, dt, kind="ExternalOutput").ap())
    hybrid_block(nc, *args)
    r = _run(nc, [arrays], core_ids=[0])
    return r.results[0]["out_0_dram"]
```

```python
from contextlib import ExitStack

import concourse.bass as bass
from concourse import mybir

F32 = mybir.dt.float32
F16 = mybir.dt.float16
I32 = mybir.dt.int32
ALU = mybir.AluOpType
ACT = mybir.ActivationFunctionType
X_AXIS = mybir.AxisListType.X

P = 128
B, C, N = 4, 256, 1024
CC = C // P
NT = N // P
HALF = 512
IC = 128
HEADS, D = 8, 32
GH = 4
GROUPS = HEADS // GH
QK_ROWS = 3 * D
E, HID = 8, 1024
HC = HID // P
TT = 256
TILES = (2 * B * N) // TT + E - 1
REGION = B * N + TT
TABLE = TILES + 1
LOADS = 26
WSCALE = 64.0
MSCALE = 64.0
WE = 8192
BIG = 3.0e38
EPS = 1e-5


LOAD_GROUP = 16 * 10
MAX_AT = [[((st >= 4), int(st < 4 or st >= 12), (st - (4 if 4 <= st < 12 else 12)) % 16 * 2 + n)
           for n in range(2)] for st in range(16)]
ROW_AT = (4, 12)
PROJECT_AT, STATS_AT, VAR_AT, SD_AT, RSTD_AT = (0, 4, 6, 7), (8, 12), 14, 15, 16
NORM_AT, HIGH_AT, TURN_AT = (16, 16, 17, 17), (18, 19), (19, 20, 21, 22)
LOGIT_AT, PICK_AT, RANK_AT, GATE_AT = 23, (24, 26, 28, 29), 30, 31
FIRST_USES = 32 + 1
EXTRA_USES = 16
ROW_USES = FIRST_USES + EXTRA_USES
INVERT_AT = (1, 2, 3, 5)
GROUP_USES = 2 * (32 + 1)
TAIL_USES = 4 + 4 + 2

ROW = 2 * C + 4
FREE = 1
PLACES = ("tk_made st_res1 pv_made fT_made st_v st_res0 rT_kept_v listed " 
          "hs_kept st_out0 st_out1 st_out2 st_out3 f_kept qhi_kept qlo_kept vt_kept_a vt_kept_v idx_kept " 
          "nrm_kept sum_kept y_kept f_out st_q0 st_q1 y_made y_out")


def max_halves(st, early):
    if early and st < 4:
        return [(4 * st + n, k) for n in range(4) for k in range(2)]
    return [(n, k) for _, _, n in MAX_AT[st] for k in range(2)]


def hybrid_block(nc, x, wk, bk, wv, bv, wq, bq, wwg, bn1_g, bn1_b, bn1_m, bn1_v, wout, bout,
                 bn2_g, bn2_b, bn2_m, bn2_v, w_qkv, w_out, b_out, wr, w1, b1, w2, b2, out):
    ctx = ExitStack()

    def sem(name):
        return ctx.enter_context(nc.semaphore(name))

    def scratch(name, shape, dt):
        return nc.dram_tensor(name, shape, dt, kind="Internal").ap()

    q_hi_d, q_lo_d = scratch("q_hi_d", (B * C, N), F16), scratch("q_lo_d", (B * C, N), F16)
    k_hi_d, k_lo_d = scratch("k_hi_d", (B * C, N), F16), scratch("k_lo_d", (B * C, N), F16)
    v_d = scratch("v_d", (B * N, C), F32)
    res0_d = scratch("res0_d", (B * N, C), F32)
    res1_d = scratch("res1_d", (B * N, C), F32)
    list_d = scratch("list_d", (E * REGION, ROW), F16)
    y_d = scratch("y_d", (2 * B * N + TT, C), F32)
    late_d = scratch("late_d", (P, 2 * WE), F16)

    with ctx:
        def sb(name, shape, dt):
            return ctx.enter_context(nc.sbuf_tensor(name, shape, dt))

        WB = sb("WB", [P, E, WE], F16)
        WORK = sb("WORK", [P, 17664], F32)
        PP = [ctx.enter_context(nc.psum_tensor(f"PP{i}", [P, 2 * HALF], F32)) for i in range(4)]

        identf = sb("identf", [P, P], F32)
        ident16 = sb("ident16", [P, P], F16)
        below16 = sb("below16", [P, P], F16)
        ones16 = sb("ones16", [P, P], F16)
        onesf = sb("onesf", [P, D], F32)
        wr16 = sb("wr16", [P, CC, 2, E], F16)
        b1c = sb("b1c", [P, E, HC], F32)
        vec = sb("vec", [P, 32], F32)
        small = sb("small", [P, 8, 8], F32)
        bst = sb("bst", [P, NT, 6], F32)
        mv = sb("mv", [P, NT, 2], F32)
        nmax = sb("nmax", [P, NT], F32)
        rsum = sb("rsum", [P, NT], F32)
        rinv = sb("rinv", [P, NT], F32)
        mxp = sb("mxp", [P, 16, 2], F32)
        mx = sb("mx", [P, 2, 16], F32)
        nmr = sb("nmr", [16, P], F16)
        w8 = sb("w8", [P, E], F32)
        ebase = sb("ebase", [P, E], F32)
        toki = sb("toki", [P, B * NT, 2], I32)
        tokf = sb("tokf", [P, B * NT, 2], F32)
        tok16 = sb("tok16", [P, B * NT, 2], F16)
        placef = sb("placef", [P, 2, 2], F32)
        place = sb("place", [P, 2, 2], I32)
        gate1 = sb("gate1", [P, B * NT], F32)
        gate2 = sb("gate2", [P, B * NT], F32)
        idx = sb("idx", [P, 2, NT], I32)
        held16 = sb("held16", [P, E], F16)
        chosen = sb("chosen", [P, E], F32)[:, :]
        pick16 = sb("pick16", [P, NT, E], F16)
        rt = sb("rt", [P, 7, NT, E], F32)
        rs = sb("rs", [P, 6, NT], F32)

        def word_view(a, n):
            return WORK[:, a:a + n]

        o = [0]

        def take(n):
            o[0] += n
            assert o[0] <= 17664
            return word_view(o[0] - n, n)

        X = take(2048).rearrange("p (c n) -> p c n", c=CC)
        QV = take(2048)
        q_sb, v_sb = QV[:, 0:N], QV[:, N:2 * N]
        kT = take(1024)
        PA = take(3072)
        prob = [PA[:, i * N:(i + 1) * N] for i in range(3)]
        y1 = PA[:, 0:N]
        lnT = PA[:, 0:2048].bitcast(F16).rearrange("p (c s n) -> p c s n", c=CC, s=2)
        wqkv_raw = PA[:, 0:1536].rearrange("p (c n) -> p c n", c=CC)
        tok = take(2048).rearrange("p (t c) -> p t c", t=NT)
        VT = tok
        QS = take(2048)
        ln = QS.rearrange("p (t c) -> p t c", t=NT)
        qs = QS.bitcast(F16).rearrange("p (u s n) -> p u s n", u=2, s=2)
        stage = take(2048).rearrange("p (u n) -> p u n", u=2)
        kTs = take(384).rearrange("p (u o) -> p u o", u=3)
        wqkv16 = take(1536).bitcast(F16).rearrange("p (s c n) -> p s c n", s=2, c=CC)
        wqT = take(256).rearrange("p (c n) -> p c n", c=CC)
        wvT = take(256).rearrange("p (c n) -> p c n", c=CC)
        kwT = take(256).rearrange("p (c n) -> p c n", c=CC)
        woT = take(256).rearrange("p (c n) -> p c n", c=CC)
        kb = take(128)
        bob = take(256)
        wq_raw, wv_raw, wk_raw = tok[:, 0, :], tok[:, 1, :], tok[:, 2, :]
        wo_raw = tok[:, 3, :].rearrange("p (c n) -> p c n", c=CC)
        wwg_raw, wwgT, bkr = tok[:, 4, 0:128], tok[:, 4, 128:256], tok[:, 5, 0:128]
        b1_raw = tok[0:E * HC, 7, 0:P]
        wr_raw = tok[:, 6, 0:16].rearrange("p (c e) -> p c e", c=CC)

        o[0] = 0
        stacked = "p (h n) -> p h n"
        QP = take(4096).bitcast(F16).rearrange("p (u f h n) -> p u f h n", u=2, f=2, h=GH)
        VV = [take(1024).rearrange("p (j d) -> p j d", j=NT)]
        KP = [None, take(2048).bitcast(F16).rearrange(stacked, h=GH)]
        OS = take(2048).rearrange("p (g n) -> p g n", g=GROUPS)
        t1 = take(2048).rearrange("p (t c) -> p t c", t=NT)
        VV.append(take(1024).rearrange("p (j d) -> p j d", j=NT))
        KP[0] = take(2048).bitcast(F16).rearrange(stacked, h=GH)
        rin = take(512)
        wo_sb = take(512).rearrange("p (c n) -> p c n", c=CC)
        ROWS = take(NT * ROW // 2)
        whole_rows = ROWS.bitcast(F16).rearrange("p (t n) -> p t n", t=NT)
        rows = whole_rows[:, :, 0:2 * C].rearrange("p t (s c) -> p t s c", s=2)
        row_place = whole_rows[:, :, 2 * C:ROW]
        LATEW = WB[:, E - 2:E, :].rearrange("p e n -> p (e n)")
        PR = WB[:, E - 1].bitcast(F32).rearrange("p (u h n) -> p u h n", u=2, h=GH)
        ln32 = WB[:, E - 2, 0:4096].bitcast(F32).rearrange("p (t c) -> p t c", t=NT)
        lnr = WB[:, E - 2, 4096:8192].rearrange("p (t s n) -> p t s n", t=NT, s=4)

        o[0] = 0
        XS = [take(ROW) for _ in range(2)]
        whole_xs = [a.bitcast(F16).rearrange("p (a n) -> p a n", a=2) for a in XS]
        xs = [a[:, :, 0:2 * C].rearrange("p a (s c) -> p a s c", s=2) for a in whole_xs]
        xs_place = [a[:, :, 2 * C:ROW] for a in whole_xs]
        xT = [take(512).bitcast(F16).rearrange("p (s n) -> p s n", s=4) for _ in range(2)]
        hid = [take(2048).rearrange("p (k n) -> p k n", k=HC) for _ in range(2)]
        hs = [take(2048).bitcast(F16).rearrange("p (s k n) -> p s k n", s=2, k=HC) for _ in range(2)]
        ysb = [take(512).rearrange("p (a c) -> p a c", a=2) for _ in range(2)]
        b2b = take(2048).rearrange("p (e c) -> p e c", e=E)
        ZERO = take(ROW)
        zero = ZERO.bitcast(F16).rearrange("p (a n) -> p a n", a=2)
        zero_place = zero[:, :, 2 * C:ROW]
        TB = take(1408)
        cnt, lists = TB[:, 0:8], TB[:, 8:16]
        incl, start = TB[:, 16:24], TB[:, 24:32]
        thr = TB[:, 32:48]
        seq, seqc = TB[:, 48:88], TB[:, 88:128]
        te, tk = TB[:, 128:168], TB[:, 168:208]
        one8 = TB[:, 208:216]
        cmp = TB[:, 256:256 + TABLE * E].rearrange("p (s e) -> p s e", s=TABLE)
        tile_e = TB[:, 1152:1152 + TABLE].bitcast(I32)
        tile_row = TB[:, 1192:1192 + TABLE].bitcast(I32)
        zrow = TB[:, 1232:1240].bitcast(I32)
        zrowf = TB[:, 1240:1248]
        PHASE_C = o[0]
        o[0] = 0
        yg = [take(2048).rearrange("p (k t c) -> p k t c", k=2, t=4) for _ in range(4)]
        tf = [take(1024).rearrange("p (t c) -> p t c", t=4) for _ in range(2)]
        ob = [take(1024).rearrange("p (c n) -> p c n", c=CC) for _ in range(4)]
        assert 17664 - 2048 >= PHASE_C
        tf = [word_view(17664 - 1024 * (u + 1), 1024).rearrange("p (t c) -> p t c", t=4) for u in range(2)] + tf

        def parity(before):
            return before % 2 if isinstance(before, int) else ROW_USES - TAIL_USES

        def shared_bank(k):
            return PP[3][:, (k % 2) * HALF:(k % 2 + 1) * HALF]

        def hidden_bank(k):
            return PP[k // 2 % 2][:, (k % 2) * HALF:(k % 2) * HALF + TT]

        def turned_bank(u):
            return PP[3][:, u * HALF:(u + 1) * HALF].bitcast(F16)

        S = {}

        def s(name):
            if name not in S:
                S[name] = sem(name)
            return S[name]

        for name in ("ld_w ld_x0 ld_x1 x_used pool_const pe_prep dve_prep act_prep mv_prep "
                     "q_made v_made k_made q_kept v_kept k_kept sc_made max_kept exp_kept ks_kept "
                     "av_made y1_kept cv_made cv_kept x1_kept tk_made tk_kept_a tk_kept_v stat_kept "
                     "sd_kept ln_kept lnT_made lnT_kept_a lnT_kept_v qk_made qhi_kept qlo_kept vt_made "
                     "vt_kept_a vt_kept_v res0_kept st_res0 st_v st_q0 st_q1 "
                     "ld_stage0 ld_stage1 scaled split_hi split_lo st_last wts_split "
                     "ld_g0 ld_g1 sum_kept rin_kept rstd_kept ld_nm00 ld_nm01 ld_nm10 ld_nm11 st_made e_kept pv_made nrm_kept "
                     "c_made c_kept nm_kept nmT_made nmr_kept ld_wo ld_res0 pr_made stat1_kept "
                     "sd1_kept ln1_kept hi_kept rows_kept rT_made rT_kept_a rT_kept_v lg_made pick_kept "
                     "gexp_kept rk_made idx_kept st_list st_res1 phase_b cnt_made table_kept zero_kept "
                     "ld_last ld_b2 st_zero ld_xs0 ld_xs1 xT_made xT_kept h_made h_kept hs_kept "
                     "y_made y_kept st_y0 st_y1 places_kept y_out tile_on ld_y0 ld_y1 ld_y2 ld_y3 ld_t0 ld_t1 ld_t2 ld_t3 f_kept "
                     "fT_made f_out st_out0 st_out1 st_out2 st_out3 kone_kept scatter_on second_on listed t1_free").split():
            s(name)

        block = ctx.enter_context(nc.Block())

        BQ, BV, BK, G1, BB1, M1, V1, S1, BE1 = range(9)
        BO, G2, BB2, M2, V2, S2, BE2 = (10 + 2 * i for i in range(7))

        @block.sync
        def _(sp):
            for name in PLACES.split():
                sp.sem_inc(s(name), FREE)
            col = lambda a: a.rearrange("(p o) -> p o", o=1)
            n_w = 0
            for dst, src in ((wq_raw, wq), (wv_raw, wv), (wk_raw, wk),
                             (wo_raw, wout.rearrange("(c p) i -> p c i", p=P)), (wwg_raw, wwg),
                             (wqkv_raw, w_qkv.rearrange("(c p) n -> p c n", p=P)),
                             (wr_raw, wr.rearrange("(c p) e -> p c e", p=P)),
                             (bob, b_out.rearrange("(o c) -> o c", o=1).broadcast_to((P, C))),
                             (b1_raw, b1.rearrange("e (k p) -> (e k) p", p=P)),
                             (vec[:, BQ:BQ + 1], col(bq)), (vec[:, BV:BV + 1], col(bv)),
                             (vec[:, BK:BK + 1], col(bk)), (vec[:, G1:G1 + 1], col(bn1_g)),
                             (vec[:, BB1:BB1 + 1], col(bn1_b)), (vec[:, M1:M1 + 1], col(bn1_m)),
                             (vec[:, V1:V1 + 1], col(bn1_v)),
                             *((vec[:, at + c:at + c + 1], col(src[c * P:(c + 1) * P]))
                               for at, src in ((BO, bout), (G2, bn2_g), (BB2, bn2_b), (M2, bn2_m), (V2, bn2_v))
                               for c in range(CC))):
                sp.dma_start(dst, src).then_inc(s("ld_w"), 16)
                n_w += 1
            assert n_w == LOADS
            xv = x.rearrange("b (c p) h w -> b p c (h w)", p=P)
            qk_d = ((q_hi_d, q_lo_d), (k_hi_d, k_lo_d))

            def load_x(n, c):
                sp.dma_start(X[:, c], xv[bass.ds(n, 1), :, c, :].rearrange("o p n -> p (o n)"))\
                  .then_inc(s(f"ld_x{c}"), 16)

            def load_q(b, g, par):
                for r, src in enumerate((q_hi_d, q_hi_d, q_lo_d)):
                    part = src[bass.ds(b * C + g * P, P), :].rearrange("(h d) (f n) -> d h f n", d=D, f=2)
                    for f in range(2):
                        sp.dma_start(QP[r * D:(r + 1) * D, par, f], part[:, :, f, :])\
                          .then_inc(s(f"ld_g{par}"), 16)

            def load_k(b, g, par):
                for r, src in enumerate((k_hi_d, k_lo_d, k_hi_d)):
                    part = src[bass.ds(b * C + g * P, P), :].rearrange("(h d) n -> d h n", d=D)
                    sp.dma_start(KP[par][r * D:(r + 1) * D], part).then_inc(s(f"ld_g{par}"), 16)

            def load_v(b, g, par):
                sp.dma_start(VV[par], v_d[bass.ds(b * N, N), g * P:(g + 1) * P]
                             .rearrange("(j p) d -> p j d", p=P)).then_inc(s(f"ld_g{par}"), 16)

            def load_group(b, g, par):
                load_q(b, g, par)
                load_k(b, g, par)
                load_v(b, g, par)

            def tokens(b, last):
                if not last:
                    for c in range(CC):
                        sp.wait_ge(s("x_used"), b * 2 + (c + 1))
                        load_x(b + 1, c)
                else:
                    sp.wait_ge(s("x_used"), 2 * B)
                    for name, n in (("st_v", 16), ("st_q0", 64), ("st_q1", 64)):
                        sp.wait_ge(s(name), FREE + n)
                    load_q(0, 0, 0)
                    load_v(0, 0, 0)
                sp.wait_ge(s("res0_kept"), b + 1)
                sp.dma_start(res0_d[bass.ds(b * N, N), :].rearrange("(t p) c -> p t c", p=P), tok)\
                  .then_inc(s("st_res0"), 16)
                for u in range(4):
                    sp.wait_ge(s("qlo_kept"), FREE + b * 4 + (u + 1))
                    for k in range(2):
                        dst = qk_d[u // 2][k][bass.ds(b * C + (u % 2) * P, P), :]
                        sp.dma_start(dst, qs[:, u % 2, k, :]).then_inc(s(f"st_q{u % 2}"), 16)
                    if last and u == 2:
                        sp.wait_ge(s("split_lo"), 32)
                        load_k(0, 0, 0)
                sp.wait_ge(s("vt_kept_a"), FREE + b + 1)
                sp.wait_ge(s("vt_kept_v"), FREE + b + 1)
                sp.dma_start(v_d[bass.ds(b * N, N), :].rearrange("(t p) c -> p t c", p=P), VT)\
                  .then_inc(s("st_v"), 16)

            load_x(0, 0)
            load_x(0, 1)
            with sp.Fori(0, B - 1) as b:
                tokens(b, False)
            tokens(B - 1, True)
            sp.wait_ge(s("st_res0"), FREE + 16 * B)
            sp.wait_ge(s("st_q0"), FREE + 64 * B)
            sp.wait_ge(s("st_q1"), FREE + 64 * B)
            sp.wait_ge(s("st_v"), FREE + 16 * B)
            sp.wait_ge(s("vt_made"), 2 * B)
            sp.dma_start(wo_sb, w_out.rearrange("(c p) n -> p c n", p=P)).then_inc(s("ld_wo"), 16)

            def store_max(par, f, n):
                sp.wait_ge(s("nmr_kept"), n)
                sp.dma_start(QP[QK_ROWS:QK_ROWS + 1, par, f].rearrange("o h n -> o (h n)"),
                             nmr[:, :]).then_inc(s(f"ld_nm{par}{f}"), 16)

            def store_res1(tail, n):
                sp.wait_ge(s("ln1_kept"), n * 4)
                sp.dma_start(res1_d[bass.ds(tail * N, N), :].rearrange("(t p) c -> p t c", p=P), t1)\
                  .then_inc(s("st_res1"), 16)

            def attend(b, first):
                for g in range(GROUPS):
                    sp.wait_ge(s("pv_made"), FREE + b * 32 + g * 16)
                    if g == 0:
                        load_group(b, 1, 1)
                    else:
                        load_group((b + 1) % B, 0, 0)
                        if not first:
                            store_res1(b - 1, b)
                        sp.wait_ge(s("st_res1"), FREE + b * 16)
                        sp.sem_inc(s("t1_free"), 1)
                        sp.dma_start(t1, res0_d[bass.ds(b * N, N), :].rearrange("(t p) c -> p t c", p=P))\
                          .then_inc(s("ld_res0"), 16)
                    store_max(g, 1, b * 4 + (2 * g + 2))
                    store_max(1 - g, 0, b * 4 + (2 * g + 3))

            store_max(0, 0, 1)
            attend(0, True)
            with sp.Fori(1, B) as b:
                attend(b, False)
            sp.wait_ge(s("st_last"), 16)
            sp.wait_ge(s("listed"), FREE + B - 1)
            sp.wait_ge(s("pv_made"), FREE + 32 * B)
            sp.dma_start(WB[:, E - 1], late_d[:, WE:2 * WE]).then_inc(s("ld_last"), 16)
            sp.dma_start(b2b, b2.rearrange("(o e) c -> o e c", o=1).broadcast_to((P, E, C)))\
              .then_inc(s("ld_b2"), 16)
            store_res1(B - 1, B)
            sp.wait_ge(s("rows_kept"), 2 * B)
            sp.wait_ge(s("pick_kept"), B)
            sp.dma_start(WB[:, E - 2], late_d[:, 0:WE]).then_inc(s("ld_last"), 16)
            sp.wait_ge(s("st_res1"), FREE + 16 * B)
            sp.wait_ge(s("ld_nm00"), 16 * (B + 1))
            for f, g in ((1, 0), (0, 1), (1, 1)):
                sp.wait_ge(s(f"ld_nm{g}{f}"), 16 * B)

            sp.wait_ge(s("phase_b"), 1)
            sp.wait_ge(s("table_kept"), 1)
            sp.wait_ge(s("zero_kept"), 1)
            for e in range(E):
                r = sp.value_load(zrow[0:1, e:e + 1], min_val=0, max_val=E * REGION - TT)
                sp.dma_start(list_d[bass.ds(r, TT), :].rearrange("(a p) c -> p a c", p=P), zero)\
                  .then_inc(s("st_zero"), 16)
            sp.wait_ge(s("st_zero"), 16 * E)
            sp.wait_ge(s("st_list"), 16 * 2 * NT * B)

            def load_rows(t, u, n_before):
                r = sp.value_load(tile_row[0:1, t], min_val=0, max_val=E * REGION - TT)
                sp.dma_start(whole_xs[u], list_d[bass.ds(r, TT), :].rearrange("(a p) n -> p a n", p=P))\
                  .then_inc(s(f"ld_xs{u}"), 16)

            load_rows(slice(0, 1), 0, 0)
            load_rows(slice(1, 2), 1, 0)
            with sp.Fori(0, (TILES - 1) // 2) as i:
                for u in range(2):
                    sp.wait_ge(s("xT_made"), i * 2 + (u + 1))
                    sp.wait_ge(s("places_kept"), i * 2 + (u + 1))
                    load_rows(bass.ds(i * 2 + (u + 2), 1), u, None)

            ov = out.rearrange("b (c p) h w -> b p c (h w)", p=P)

            def load_half(h):
                u, at = h % 4, h * HALF
                if h >= 4:
                    sp.wait_ge(s("f_kept"), FREE + h - 3)
                    sp.wait_ge(s("fT_made"), FREE + h - 3)
                for k in range(2):
                    sp.dma_start(yg[u][:, k], y_d[k * B * N + at:k * B * N + at + HALF, :]
                                 .rearrange("(t p) c -> p t c", p=P)).then_inc(s(f"ld_y{u}"), 16)
                if h >= 2:
                    load_tokens(h)

            def load_tokens(h):
                u, at = h % 4, h * HALF
                sp.dma_start(tf[u], res1_d[at:at + HALF, :].rearrange("(t p) c -> p t c", p=P))\
                  .then_inc(s(f"ld_t{u}"), 16)

            load_tokens(0)
            load_tokens(1)
            sp.wait_ge(s("y_out"), FREE + TILES)
            for h in range(4):
                load_half(h)
            for h in range(2 * B):
                sp.wait_ge(s("f_out"), FREE + h + 1)
                sp.dma_start(ov[h // 2, :, :, (h % 2) * HALF:(h % 2 + 1) * HALF], ob[h % 4])\
                  .then_inc(s(f"st_out{h % 4}"), 16)
                if h + 4 < 2 * B:
                    load_half(h + 4)
            for u in range(4):
                sp.wait_ge(s(f"st_out{u}"), FREE + 16 * (2 * B // 4))

        @block.gpsimd
        def _(pool):
            def one_where(m, op, base):
                pool.affine_select(out=m[:, :], in_=m[:, :], compare_op=op, fill=1.0, base=base,
                                   pattern=[[-1, P]], channel_multiplier=1)
            for m in (identf, ident16, below16):
                pool.memset(m[:, :], 0.0)
            pool.memset(ones16[:, :], 1.0)
            pool.memset(onesf[:, :], 1.0)
            pool.drain()
            one_where(identf, ALU.not_equal, 0)
            one_where(ident16, ALU.not_equal, 0)
            one_where(below16, ALU.is_ge, 0)
            for e in range(E):
                pool.memset(w8[:, e:e + 1], float(E - e))
                pool.memset(ebase[:, e:e + 1], float(REGION * e))
            pool.iota(toki[:, :, 0], pattern=[[0, B * NT]], base=0, channel_multiplier=1)
            pool.iota(toki[:, :, 1], pattern=[[P, B * NT]], base=0, channel_multiplier=0)
            pool.drain()
            pool.sem_inc(s("pool_const"), 1)

            parts = []
            for e in [E - 2, E - 1] + list(range(E - 2)):
                for c in range(CC):
                    parts.append((e, w1[e].rearrange("(c p) n -> p c n", p=P)[:, c, :], c * HID, CC * HID))
                for c in range(2):
                    src = w2[e].rearrange("(k p) n -> p k n", p=P)[:, c * 4:c * 4 + 4, :]
                    parts.append((e, src, 2 * CC * HID + c * HID, HC * C))

            def load_part(i):
                dst = stage[:, i % 2, :]
                if parts[i][2] >= 2 * CC * HID:
                    dst = dst.rearrange("p (k n) -> p k n", k=4)
                pool.dma_start(dst, parts[i][1]).then_inc(s(f"ld_stage{i % 2}"), 16)

            load_part(0)
            load_part(1)
            for i, (e, _, at, gap) in enumerate(parts):
                hi, lo = WB[:, e, at:at + HID], WB[:, e, at + gap:at + gap + HID]
                pool.wait_ge(s("split_hi"), i + 1)
                pool.tensor_tensor(lo, stage[:, i % 2, :], hi, ALU.subtract).then_inc(s("split_lo"), 1)
                pool.wait_ge(s("split_lo"), i + 1)
                if i + 2 < len(parts):
                    load_part(i + 2)
                if i == 7:
                    pool.dma_start(late_d[:, :], LATEW).then_inc(s("st_last"), 16)

            for name, n in (("st_v", 16), ("st_q0", 64), ("st_q1", 64), ("st_res0", 16)):
                pool.wait_ge(s(name), FREE + n * B)
            pool.wait_ge(s("vt_made"), 2 * B)
            pool.wait_ge(s("split_lo"), 32)
            for par in range(2):
                pool.memset(KP[par][QK_ROWS:QK_ROWS + 1], MSCALE).then_inc(s("kone_kept"), 1)

            def normalise(g, f, n):
                out_at = OS[:, g, f * HALF:(f + 1) * HALF]
                pool.wait_ge(s("rin_kept"), n + 1)
                pool.tensor_tensor(out_at, out_at, rin, ALU.mult).then_inc(s("nrm_kept"), 1)

            def tail_low(n):
                for part in range(2):
                    here = slice(part * NT // 2, (part + 1) * NT // 2)
                    pool.wait_ge(s("hi_kept"), n * 2 + (part - 1))
                    pool.tensor_tensor(rows[:, here, 1, :], ln32[:, here], rows[:, here, 0, :], ALU.subtract)\
                        .then_inc(s("rows_kept"), 1)

            def scatter(n, k):
                if k == 0:
                    pool.wait_ge(s("idx_kept"), FREE + n)
                    pool.sem_inc(s("scatter_on"), 1)
                    pool.memset(row_place[:, :, 3:4], 0.0)
                else:
                    pool.wait_ge(s("st_list"), n * (16 * 2 * NT) - 16 * NT)
                    pool.sem_inc(s("second_on"), 1)
                pool.memset(row_place[:, :, 2:3], float(k * B * N))
                pool.drain()
                for t in range(NT):
                    pool.indirect_dma_start(
                        list_d[:, :], bass.IndirectOffsetOnAxis(ap=idx[:, k, t:t + 1], axis=0),
                        whole_rows[:, t], None).then_inc(s("st_list"), 16)
                if k:
                    pool.wait_ge(s("st_list"), n * (16 * 2 * NT))
                    pool.sem_inc(s("listed"), 1)

            def attend(b, tails):
                normalise(1, 1, b * 4 - 1)
                if tails != 1:
                    scatter(b - 1, 1)
                normalise(0, 0, b * 4)
                tail_low(b)
                normalise(0, 1, b * 4 + 1)
                normalise(1, 0, b * 4 + 2)
                scatter(b, 0)

            normalise(0, 0, 0)
            normalise(0, 1, 1)
            normalise(1, 0, 2)
            attend(1, 1)
            with pool.Fori(2, B) as b:
                attend(b, 2)
            normalise(1, 1, B * 4 - 1)
            scatter(B - 1, 1)
            for k in range(B * N // TT):
                pool.memset(thr[:, k:k + 1], float(TT * k))
            pool.iota(seq.bitcast(I32), pattern=[[1, TABLE]], base=0, channel_multiplier=0)
            pool.memset(one8, 1.0)
            pool.memset(ZERO, 0.0)
            pool.drain()
            pool.tensor_copy(zero_place[:, :, 0:1], tok16[:, 0:TT // P, 0:1])
            for a in range(TT // P):
                pool.memset(zero_place[:, a, 1:2], float(2 * B * N + a * P))
            pool.drain()
            pool.sem_inc(s("zero_kept"), 1)
            scatter(B, 0)
            scatter(B, 1)

            def store_output(t, u, n):
                pool.wait_ge(s("y_kept"), FREE + t + 1)
                pool.sem_inc(s("tile_on"), 1)
                for a in range(2):
                    pool.indirect_dma_start(
                        y_d[:, :], bass.IndirectOffsetOnAxis(ap=place[:, u, a:a + 1], axis=0),
                        ysb[u][:, a], None).then_inc(s(f"st_y{u}"), 16)
                pool.wait_ge(s(f"st_y{u}"), n)
                pool.sem_inc(s("y_out"), 1)

            with pool.Fori(0, (TILES - 1) // 2) as i:
                for u in range(2):
                    store_output(i * 2 + u, u, i * 32 + 32)
            store_output(TILES - 1, 0, 32 * ((TILES + 1) // 2))

        @block.scalar
        def _(act):
            act.wait_ge(s("dve_prep"), 1)
            act.activation(vec[:, 24:27], vec[:, 24:27], ACT.Sqrt).then_inc(s("act_prep"), 1)
            act.wait_ge(s("dve_prep"), 2)

            def keep_q(n):
                act.wait_ge(s("q_made"), n + 1)
                act.activation(q_sb, PP[0][:, :], ACT.Identity, bias=vec[:, BQ:BQ + 1]).then_inc(s("q_kept"), 1)

            def keep_v(n):
                act.wait_ge(s("v_made"), n + 1)
                act.activation(v_sb, PP[1][:, :], ACT.Identity, bias=vec[:, BV:BV + 1]).then_inc(s("v_kept"), 1)

            def split_weights(b, i):
                w = stage[:, i % 2, :]
                e = (b * 2 + (E - 2 + i // 4)) % E
                at = (i % 2) * HID + (0 if i % 4 < 2 else 2 * CC * HID)
                act.wait_ge(s(f"ld_stage{i % 2}"), 16 * (b * 4 + (i // 2 + 1)))
                hi = WB[:, bass.ds(e, 1), at:at + HID].rearrange("p o n -> p (o n)")
                act.activation(hi, w, ACT.Copy, scale=WSCALE)
                act.activation(w, w, ACT.Copy, scale=WSCALE).then_inc(s("split_hi"), 1)

            def tokens(b, last):
                for i in range(NT):
                    act.wait_ge(s("max_kept"), b * NT + (i + 1))
                    if i >= 3:
                        act.wait_ge(s("av_made"), b * NT + (i - 2))
                    act.activation(prob[i % 3], PP[i % 3][:, :], ACT.Exp, bias=nmax[:, i:i + 1],
                                   accum_out=rsum[:, i:i + 1]).then_inc(s("exp_kept"), 1)
                    if i % 2 == 0:
                        split_weights(b, i // 2)
                split_weights(b, 4)
                for c in range(CC):
                    act.wait_ge(s("cv_kept"), b * 2 + (c + 1))
                    act.activation(X[:, c], X[:, c], ACT.Relu, bias=vec[:, BE2 + c:BE2 + c + 1])\
                       .then_inc(s("x1_kept"), 1)
                act.wait_ge(s("tk_made"), FREE + b * 2 + 1)
                act.wait_ge(s("st_v"), FREE + b * 16)
                act.activation(tok[:, 0:4], PP[2][:, :].rearrange("p (t c) -> p t c", t=4), ACT.Copy)\
                   .then_inc(s("tk_kept_a"), 1)
                act.wait_ge(s("stat_kept"), b + 1)
                act.activation(small[:, 2], small[:, 1], ACT.Sqrt).then_inc(s("sd_kept"), 1)
                if not last:
                    keep_q(b + 1)
                    keep_v(b + 1)
                split_weights(b, 5)
                for c in range(CC):
                    act.wait_ge(s("lnT_made"), b * 2 + (c + 1))
                    act.activation(lnT[:, c, 0], PP[c][:, :], ACT.Copy).then_inc(s("lnT_kept_a"), 1)
                for u in range(4):
                    act.wait_ge(s("qk_made"), b * 4 + (u + 1))
                    if u >= 2:
                        act.wait_ge(s(f"st_q{u % 2}"), FREE + b * 64 + 32)
                    act.activation(qs[:, u % 2, 0], PP[(u + 2) % 4][:, :], ACT.Copy,
                                   scale=(C ** -0.5 if u < 2 else 1.0) / WSCALE).then_inc(s("qhi_kept"), 1)
                    if u < 2:
                        split_weights(b, 6 + u)
                act.wait_ge(s("vt_made"), b * 2 + 1)
                act.wait_ge(s("st_res0"), FREE + b * 16 + 16)
                act.activation(VT[:, 0:4], PP[2][:, :].rearrange("p (t c) -> p t c", t=4), ACT.Copy,
                               scale=1.0 / WSCALE)\
                   .then_inc(s("vt_kept_a"), 1)

            keep_q(0)
            keep_v(0)
            with act.Fori(0, B - 1) as b:
                tokens(b, False)
            tokens(B - 1, True)

            def tail_deviations(n):
                act.wait_ge(s("stat1_kept"), n)
                act.activation(small[:, 2], small[:, 1], ACT.Sqrt).then_inc(s("sd1_kept"), 1)

            def tail_norm(part, n):
                if part == 0:
                    act.wait_ge(s("rstd_kept"), n)
                for t in range(part * NT // 4, (part + 1) * NT // 4):
                    op = act.activation(ln32[:, t], t1[:, t], ACT.Identity,
                                        bias=small[:, 4, t:t + 1], scale=small[:, 3, t:t + 1])
                op.then_inc(s("ln1_kept"), 1)

            def tail_high(part, n):
                act.wait_ge(s("ln1_kept"), n * 4 + (2 * part - 2))
                if part == 0:
                    act.wait_ge(s("listed"), n)
                here = slice(part * NT // 2, (part + 1) * NT // 2)
                act.activation(rows[:, here, 0, :], ln32[:, here], ACT.Copy).then_inc(s("hi_kept"), 1)

            def keep_sums(g, f, n):
                act.wait_ge(s("pv_made"), n * 8 + (FREE + 8))
                act.wait_ge(s("nrm_kept"), FREE + n)
                act.activation(OS[:, g, f * HALF:(f + 1) * HALF], PP[2][:, 0:HALF], ACT.Copy)
                act.activation(rin, PP[2][:, HALF:2 * HALF], ACT.Copy).then_inc(s("sum_kept"), 1)

            def tail_gate(n):
                act.wait_ge(s("pick_kept"), n)
                act.activation(rs[:, 2], rs[:, 2], ACT.Exp, scale=1.0 / WSCALE).then_inc(s("gexp_kept"), 1)

            def attend(b, first):
                for g in range(GROUPS):
                    for st in range(16):
                        if not (first and g + st == 0):
                            act.wait_ge(s("pv_made"), b * 32 + (FREE + g * 16 + st - 1))
                        for pr in range(2):
                            act.wait_ge(s("st_made"), b * 64 + (g * 32 + st * 2 + pr + 1))
                            act.activation(PR[:, st % 2, 2 * pr:2 * pr + 2], PP[pr][:, :]
                                           .rearrange("p (h n) -> p h n", h=2), ACT.Exp).then_inc(s("e_kept"), 1)
                        if st % 8 == 0 and not (first and g + st == 0):
                            keep_sums(*divmod((g * 2 + st // 8 - 1) % 4, 2), b * 4 + (g * 2 + st // 8 - 1))
                        if not first and g * 16 + st == SD_AT:
                            tail_deviations(b)
                        for part in range(4):
                            if not first and g * 16 + st == NORM_AT[part]:
                                tail_norm(part, b)
                        if not first and g * 16 + st in HIGH_AT:
                            tail_high(HIGH_AT.index(g * 16 + st), b)
                        if not first and g * 16 + st == GATE_AT:
                            tail_gate(b)

            attend(0, True)
            with act.Fori(1, B) as b:
                attend(b, False)
            keep_sums(1, 1, 4 * B - 1)
            tail_deviations(B)
            tail_high(0, B)
            tail_high(1, B)
            tail_gate(B)

            act.wait_ge(s("table_kept"), 1)

            def gelus(t, u, at):
                e = act.value_load(tile_e[0:1, at], min_val=0, max_val=E - 1)
                for k in range(HC):
                    act.wait_ge(s("h_made"), t * HC + (k + 1))
                    act.activation(hid[u][:, k], hidden_bank(k), ACT.Gelu,
                                   bias=b1c[:, bass.ds(e, 1), k], scale=1.0 / WSCALE)\
                       .then_inc(s("h_kept"), 1)

            gelus(0, 0, slice(0, 1))
            with act.Fori(0, (TILES - 1) // 2) as i:
                for u in (1, 0):
                    act.wait_ge(s("hs_kept"), FREE + i * 8 + (0 if u else 4))
                    gelus(i * 2 + (1 if u else 2), u, bass.ds(i * 2 + (1 if u else 2), 1))

            with act.Fori(0, 2 * B // 4) as i:
                for u in range(4):
                    act.wait_ge(s("fT_made"), FREE + i * 4 + (u + 1))
                    act.wait_ge(s(f"st_out{u}"), FREE + i * 16)
                    act.activation(ob[u], PP[u][:, :].rearrange("p (c n) -> p c n", c=CC), ACT.Copy)\
                       .then_inc(s("f_out"), 1)

        @block.tensor
        def _(pe):
            def product(dst, pairs, sem_name=None):
                for n, (lhsT, rhs) in enumerate(pairs):
                    mm = pe.matmul(dst, lhsT, rhs, start=(n == 0), stop=(n == len(pairs) - 1))
                if sem_name:
                    mm.then_inc(s(sem_name), 1)

            pe.wait_ge(s("pool_const"), 1)
            pe.wait_ge(s("ld_w"), 16 * LOADS)
            for c in range(CC):
                cols = slice(c * P, (c + 1) * P)
                pe.transpose(PP[0][:, c * P:(c + 1) * P], wq_raw[:, cols], identf[:, :])
                pe.transpose(PP[0][:, 256 + c * P:256 + (c + 1) * P], wv_raw[:, cols], identf[:, :])
                pe.transpose(PP[0][:, 512 + c * P:512 + (c + 1) * P], wo_raw[:, c], identf[:, :])
            pe.transpose(PP[0][:, 896:896 + E * HC], b1_raw, identf[0:E * HC, 0:E * HC])
            pe.transpose(PP[0][:, 768:896], wwg_raw, identf[:, :]).then_inc(s("pe_prep"), 1)
            pe.wait_ge(s("dve_prep"), 1)
            for c in range(CC):
                product(PP[1][:, c * P:(c + 1) * P], [(wk_raw[:, c * P:(c + 1) * P], wwgT)])
            product(PP[1][:, 512:640], [(bkr, wwgT)], "pe_prep")
            pe.wait_ge(s("dve_prep"), 2)

            def halves(dst, w, src, sem_name):
                for h in range(2):
                    n = slice(h * HALF, (h + 1) * HALF)
                    product(dst[:, n], [(w(c), src[:, c, n]) for c in range(CC)],
                            sem_name if h else None)

            def project_x(n, first):
                for c in range(CC):
                    pe.wait_ge(s(f"ld_x{c}"), n * 16 + 16)
                    for dst, w, name in ((PP[0], wqT, "q_made"), (PP[1], wvT, "v_made")):
                        for h in range(2):
                            here = slice(h * HALF, (h + 1) * HALF)
                            mm = pe.matmul(dst[:, here], w[:, c], X[:, c, here],
                                           start=(c == 0), stop=(c == CC - 1))
                        if c == CC - 1:
                            mm.then_inc(s(name), 1)
                if not first:
                    pe.wait_ge(s("tk_kept_a"), n)
                for t in range(NT):
                    at = slice(t * P, (t + 1) * P)
                    product(PP[2][:, at], [(X[:, c, at], kwT[:, c]) for c in range(CC)],
                            "k_made" if t == NT - 1 else None)

            def tokens(b, last):
                def scores(i):
                    if i == 0:
                        pe.wait_ge(s("q_kept"), b + 1)
                        pe.wait_ge(s("v_kept"), b + 1)
                        pe.wait_ge(s("qhi_kept"), FREE + b * 4)
                        pe.wait_ge(s("qlo_kept"), FREE + b * 4)
                    elif i == 2:
                        pe.wait_ge(s("k_kept"), b + 1)
                        pe.wait_ge(s("vt_kept_a"), FREE + b)
                    elif i >= 3:
                        pe.wait_ge(s("exp_kept"), b * NT + (i - 2))
                    for h in range(2):
                        product(PP[i % 3][:, h * HALF:(h + 1) * HALF],
                                [(v_sb[:, i * P:(i + 1) * P], q_sb[:, h * HALF:(h + 1) * HALF])],
                                "sc_made" if h else None)

                def weigh(i):
                    pe.wait_ge(s("exp_kept"), b * NT + (i + 1))
                    pe.wait_ge(s("ks_kept"), b * NT + (i + 1))
                    if i == 0:
                        pe.wait_ge(s("vt_kept_v"), FREE + b)
                    for h in range(2):
                        mm = pe.matmul(PP[3][:, h * HALF:(h + 1) * HALF], kTs[:, i % 3],
                                       prob[i % 3][:, h * HALF:(h + 1) * HALF],
                                       start=(i == 0), stop=(i == NT - 1))
                    mm.then_inc(s("av_made"), 1)

                scores(0)
                scores(1)
                for i in range(NT):
                    if i + 2 < NT:
                        scores(i + 2)
                    weigh(i)
                for c in range(CC):
                    for h in range(2):
                        pe.wait_ge(s("y1_kept"), b * 2 + (h + 1))
                        product(PP[c][:, h * HALF:(h + 1) * HALF], [(woT[:, c], y1[:, h * HALF:(h + 1) * HALF])],
                                "cv_made" if h else None)
                for c in range(CC):
                    pe.wait_ge(s("x1_kept"), b * 2 + (c + 1))
                    for t in range(NT):
                        mm = pe.transpose(PP[2 + t // 4][:, (t % 4) * C + c * P:(t % 4) * C + (c + 1) * P],
                                          X[:, c, t * P:(t + 1) * P], identf[:, :])
                        if t % 4 == 3 and c == CC - 1:
                            mm.then_inc(s("tk_made"), 1)
                    pe.drain()
                    pe.sem_inc(s("x_used"), 1)
                if not last:
                    project_x(b + 1, False)
                    pe.wait_ge(s("q_kept"), b + 2)
                    pe.wait_ge(s("v_kept"), b + 2)
                for c in range(CC):
                    for t in range(NT):
                        pe.wait_ge(s("ln_kept"), b * NT + (t + 1)) if c == 0 else None
                        mm = pe.transpose(PP[c][:, t * P:(t + 1) * P], ln[:, t, c * P:(c + 1) * P], identf[:, :])
                    mm.then_inc(s("lnT_made"), 1)
                pe.wait_ge(s("lnT_kept_a"), b * 2 + 2)
                if not last:
                    pe.wait_ge(s("k_kept"), b + 2)
                for u in range(4):
                    for w, d in ((0, 0), (1, 0), (0, 1)):
                        if u == 0 and d:
                            pe.wait_ge(s("lnT_kept_v"), b * 2 + 2)
                        for c in range(CC):
                            for h in range(2):
                                here = slice(h * HALF, (h + 1) * HALF)
                                mm = pe.matmul(PP[(u + 2) % 4][:, here], wqkv16[:, w, c, u * P:(u + 1) * P],
                                               lnT[:, c, d, here], start=(w + d + c == 0),
                                               stop=(d == 1 and c == CC - 1))
                    mm.then_inc(s("qk_made"), 1)
                for t in range(NT):
                    if t % 4 == 0:
                        pe.wait_ge(s("qhi_kept"), FREE + b * 4 + (t // 4 + 1))
                        pe.wait_ge(s("qlo_kept"), FREE + b * 4 + (t // 4 + 1))
                    product(PP[2 + t // 4][:, (t % 4) * C:(t % 4 + 1) * C],
                            [(lnT[:, c, d, t * P:(t + 1) * P], wqkv16[:, w, c, 2 * C:3 * C])
                             for w, d in ((0, 0), (1, 0), (0, 1)) for c in range(CC)],
                            "vt_made" if t % 4 == 3 else None)

            project_x(0, True)
            with pe.Fori(0, B - 1) as b:
                tokens(b, False)
            tokens(B - 1, True)

            uses = [0]

            def next_bank(before):
                at = uses[0]
                uses[0] += 1
                if not isinstance(before, int) or before + at >= 2:
                    pe.wait_ge(s("c_kept"), before + (at - 1))
                return shared_bank(at + parity(before))

            def max_half(n, k, f, par, before):
                h, i = n // 4, n % 4
                pe.matmul(next_bank(before), QP[0:QK_ROWS, par, f, h, i * P:(i + 1) * P],
                          KP[par][0:QK_ROWS, h, k * HALF:(k + 1) * HALF],
                          start=True, stop=True).then_inc(s("c_made"), 1)

            def max_row(f, before, n):
                bank = next_bank(before)
                pe.wait_ge(s("nm_kept"), n)
                pe.transpose(bank[0:16, 0:P], mx[:, f], identf[:, :]).then_inc(s("c_made"), 1)

            def tail_project(c, before, n):
                bank = next_bank(before)
                pe.wait_ge(s("nrm_kept"), FREE + n * 4 - (1 if c < 2 else 0))
                for t in range(2):
                    tok_at = slice((2 * c + t) * P, (2 * c + t + 1) * P)
                    product(bank[:, t * C:(t + 1) * C], [(OS[:, k, tok_at], wo_sb[:, k]) for k in range(CC)],
                            "c_made" if t else None)

            def tail_turn(c, before, n):
                bank = next_bank(before).bitcast(F16)
                pe.wait_ge(s("rows_kept"), n * 2 - (1 if c < 2 else 0))
                for t in range(2):
                    for q in range(4):
                        mm = pe.transpose(bank[:, (4 * t + q) * P:(4 * t + q + 1) * P],
                                          rows[:, 2 * c + t, q // 2, (q % 2) * P:(q % 2 + 1) * P], ident16[:, :])
                mm.then_inc(s("c_made"), 1)

            def tail_logits(before):
                bank = next_bank(before)
                pe.wait_ge(s("c_kept"), before + (uses[0] - 1))
                for t in range(NT):
                    product(bank[:, t * 2 * E:(t + 1) * 2 * E],
                            [(lnr[:, t, q], wr16[:, q % 2].rearrange("p s e -> p (s e)")) for q in range(4)],
                            "c_made" if t == NT - 1 else None)

            def tail_ranks(before, n):
                bank = next_bank(before)
                pe.wait_ge(s("pick_kept"), n)
                pe.matmul(bank[:, 0:NT * E], below16[:, :], pick16[:, :, :].rearrange("p t e -> p (t e)"),
                          start=True, stop=False)
                for far in range(1, NT):
                    pe.matmul(bank[:, far * E:NT * E], ones16[:, :],
                              pick16[:, 0:NT - far, :].rearrange("p t e -> p (t e)"), start=False, stop=False)
                for t in range(NT):
                    mm = pe.matmul(bank[:, t * E:(t + 1) * E], ones16[:, :], held16[:, :],
                                   start=False, stop=(t == NT - 1))
                mm.then_inc(s("c_made"), 1)

            def attend(b, first):
                before = FIRST_USES if first else b * (2 * GROUP_USES + TAIL_USES) + (ROW_USES - TAIL_USES)
                uses[0] = 0

                def weigh_heads(g, st):
                    par, f, j = g % 2, st // 8, st % 8
                    pe.wait_ge(s("e_kept"), b * 64 + (g * 32 + st * 2 + 2))
                    if j == 0:
                        pe.wait_ge(s("sum_kept"), b * 4 + (FREE + g * 2 + f))
                    for h in range(GH):
                        pe.matmul(PP[2][h * D:(h + 1) * D, 0:HALF], VV[par][:, j, h * D:(h + 1) * D],
                                  PR[:, st % 2, h], start=(j == 0), stop=(j == 7))

                def sum_heads(st):
                    for h in range(GH):
                        mm = pe.matmul(PP[2][h * D:(h + 1) * D, HALF:2 * HALF], onesf[:, :],
                                       PR[:, st % 2, h], start=(st % 8 == 0), stop=(st % 8 == 7))
                    mm.then_inc(s("pv_made"), 1)

                for g in range(GROUPS):
                    for st in range(16):
                        f, j = st // 8, st % 8
                        if st == 0:
                            pe.wait_ge(s(f"ld_g{g}"), b * LOAD_GROUP + LOAD_GROUP)
                        if j == 0:
                            pe.wait_ge(s(f"ld_nm{g}{f}"), b * 16 + 16)
                        more, mf, _ = MAX_AT[st][0]
                        mg = (g + more) % 2
                        halves = max_halves(st, first and g == 0)

                        def max_quarter(q):
                            few = len(halves) // 4
                            for n, k in halves[q * few:(q + 1) * few]:
                                max_half(n, k, mf, mg, before)

                        for pr in range(2):
                            if not (first and g + st == 0):
                                pe.wait_ge(s("e_kept"), b * 64 + (g * 32 + st * 2 + pr - 1))
                            for h in (2 * pr, 2 * pr + 1):
                                mm = pe.matmul(PP[pr][:, (h % 2) * HALF:(h % 2 + 1) * HALF],
                                               KP[g][0:QK_ROWS + 1, h, j * P:(j + 1) * P],
                                               QP[0:QK_ROWS + 1, g, f, h, :], start=True, stop=True)
                            mm.then_inc(s("st_made"), 1)
                            if st == 4 and pr == 0:
                                pe.wait_ge(s(f"ld_g{1 - g}"), b * LOAD_GROUP + LOAD_GROUP * (g + 1))
                            max_quarter(pr)
                        weighs = st > 0 or g > 0 or not first
                        if weighs:
                            weigh_heads(g if st else g - 1, (st - 1) % 16)
                        max_quarter(2)
                        if st in ROW_AT:
                            max_row(1 - f, before, b * 4 + (2 * g + f + 2))
                        if weighs:
                            sum_heads((st - 1) % 16)
                        max_quarter(3)
                        at = g * 16 + st
                        if not first:
                            if at in PROJECT_AT:
                                tail_project(PROJECT_AT.index(at), before, b)
                            if at in TURN_AT:
                                tail_turn(TURN_AT.index(at), before, b)
                            if at == LOGIT_AT:
                                tail_logits(before)
                            if at == RANK_AT:
                                tail_ranks(before, b)
                if not first:
                    assert uses[0] == 2 * GROUP_USES + TAIL_USES

            pe.wait_ge(s("ld_g0"), LOAD_GROUP)
            for name, n in (("vt_kept_v", 1), ("vt_kept_a", 1), ("qlo_kept", 4)):
                pe.wait_ge(s(name), FREE + n * B)
            for n in range(32):
                max_half(n // 2, n % 2, 0, 0, 0)
            max_row(0, 0, 1)
            pe.wait_ge(s("kone_kept"), 2)
            attend(0, True)
            with pe.Fori(1, B) as b:
                attend(b, False)
            pe.wait_ge(s("e_kept"), B * 64)
            for lhsT, at in ((VV[1][:, 7], 0), (None, HALF)):
                for h in range(GH):
                    mm = pe.matmul(PP[2][h * D:(h + 1) * D, at:at + HALF],
                                   onesf[:, :] if lhsT is None else lhsT[:, h * D:(h + 1) * D],
                                   PR[:, 1, h], start=False, stop=True)
            mm.then_inc(s("pv_made"), 1)
            before = B * (2 * GROUP_USES + TAIL_USES) + (ROW_USES - TAIL_USES)
            uses[0] = 0
            for c in range(4):
                tail_project(c, before, B)
            for c in range(4):
                tail_turn(c, before, B)
            tail_logits(before)
            tail_ranks(before, B)

            pe.wait_ge(s("idx_kept"), FREE + B)
            product(PP[0][:, 0:E], [(ones16[:, :], held16[:, :])], "cnt_made")
            pe.wait_ge(s("table_kept"), 1)
            pe.wait_ge(s("ld_last"), 32)

            def expert(at):
                return pe.value_load(tile_e[0:1, at], min_val=0, max_val=E - 1)

            def weights(e, off, n):
                return WB[:, bass.ds(e, 1), off:off + n].rearrange("p o n -> p (o n)")

            def turn(t, u, n_load):
                pe.wait_ge(s(f"ld_xs{u}"), n_load)
                if not (isinstance(t, int) and t < 2):
                    pe.wait_ge(s("xT_kept"), t - 1)
                for q in range(4):
                    for a in range(2):
                        at = q * TT + a * P
                        mm = pe.transpose(turned_bank(u)[:, at:at + P],
                                          xs[u][:, a, q // 2, (q % 2) * P:(q % 2 + 1) * P], ident16[:, :])
                mm.then_inc(s("xT_made"), 1)

            MEET = ((0, 0), (0, 1), (1, 0))

            def first(t, u, e):
                pe.wait_ge(s("xT_kept"), t + 1)
                for k in range(HC):
                    if not (isinstance(t, int) and k < 4):
                        pe.wait_ge(s("h_kept"), t * HC + (k - 3))
                    product(hidden_bank(k),
                            [(weights(e, (w * CC + c) * HID + k * P, P), xT[u][:, d * CC + c])
                             for w, d in MEET for c in range(CC)], "h_made")

            def second(t, u, e):
                pe.wait_ge(s("hs_kept"), FREE + t * 4 + 4)
                for a in range(2):
                    product(PP[2][:, u * HALF + a * C:u * HALF + (a + 1) * C],
                            [(hs[u][:, d, k, a * P:(a + 1) * P], weights(e, 2 * CC * HID + (w * HC + k) * C, C))
                             for w, d in MEET for k in range(HC)], "y_made" if a else None)

            turn(0, 0, 16)
            first(0, 0, expert(slice(0, 1)))
            turn(1, 1, 16)
            with pe.Fori(0, (TILES - 1) // 2) as i:
                e0 = expert(bass.ds(i * 2, 1))
                e1 = expert(bass.ds(i * 2 + 1, 1))
                e2 = expert(bass.ds(i * 2 + 2, 1))
                first(i * 2 + 1, 1, e1)
                turn(i * 2 + 2, 0, i * 16 + 32)
                pe.wait_ge(s("y_kept"), FREE + i * 2)
                second(i * 2, 0, e0)
                first(i * 2 + 2, 0, e2)
                turn(i * 2 + 3, 1, i * 16 + 32)
                pe.wait_ge(s("y_kept"), FREE + i * 2)
                second(i * 2 + 1, 1, e1)
            pe.wait_ge(s("y_kept"), FREE + TILES - 2)
            second(TILES - 1, 0, expert(slice(TILES - 1, TILES)))

            with pe.Fori(0, 2 * B // 4) as i:
                for u in range(4):
                    pe.wait_ge(s("f_kept"), FREE + i * 4 + (u + 1))
                    if u == 0:
                        pe.wait_ge(s("f_out"), FREE + i * 4)
                    for c in range(CC):
                        for t in range(4):
                            mm = pe.transpose(PP[u][:, c * HALF + t * P:c * HALF + (t + 1) * P],
                                              tf[u][:, t, c * P:(c + 1) * P], identf[:, :])
                    mm.then_inc(s("fT_made"), 1)

        @block.vector
        def _(dve):
            def per_tile(a):
                return a.unsqueeze(2).broadcast_to((P, a.shape[1], E))

            def per_expert(a, n):
                return a.unsqueeze(1).broadcast_to((P, n, E))

            dve.wait_ge(s("pe_prep"), 1)
            dve.wait_ge(s("ld_w"), 16 * LOADS)
            for dst, at in ((wqT, 0), (wvT, 256), (woT, 512)):
                dve.tensor_copy(dst, PP[0][:, at:at + 256].rearrange("p (c n) -> p c n", c=CC))
            dve.tensor_copy(b1c[:, :, :], PP[0][:, 896:896 + E * HC].rearrange("p (e k) -> p e k", e=E))
            dve.tensor_copy(tokf[:, :, :], toki[:, :, :])
            dve.tensor_copy(wwgT, PP[0][:, 768:896])
            dve.drain()
            dve.tensor_copy(tok16[:, :, :], tokf[:, :, :])
            dve.tensor_scalar(bkr, identf[:, :], 0.0, vec[:, BK:BK + 1], ALU.mult, ALU.add)
            dve.tensor_scalar(vec[:, 24:25], vec[:, V1:V1 + 1], EPS, None, ALU.add)
            dve.tensor_scalar(vec[:, 25:27], vec[:, V2:V2 + 2], EPS, None, ALU.add)
            dve.tensor_scalar(wr16[:, :, 0, :], wr_raw, WSCALE, None, ALU.mult)
            dve.memset(held16[:, :], 0.0)
            dve.drain()
            dve.scalar_tensor_tensor(out=wr16[:, :, 1, :], in0=wr_raw, scalar=WSCALE, in1=wr16[:, :, 0, :],
                                     op0=ALU.mult, op1=ALU.subtract).then_inc(s("dve_prep"), 1)
            dve.wait_ge(s("act_prep"), 1)
            dve.reciprocal(vec[:, 27:30], vec[:, 24:27])
            dve.drain()
            dve.tensor_tensor(vec[:, S1:S1 + 1], vec[:, 27:28], vec[:, G1:G1 + 1], ALU.mult)
            dve.tensor_tensor(vec[:, S2:S2 + 2], vec[:, 28:30], vec[:, G2:G2 + 2], ALU.mult)
            dve.tensor_tensor(vec[:, BO:BO + 2], vec[:, BO:BO + 2], vec[:, M2:M2 + 2], ALU.subtract)
            dve.drain()
            dve.tensor_tensor(vec[:, M1:M1 + 1], vec[:, M1:M1 + 1], vec[:, S1:S1 + 1], ALU.mult)
            dve.tensor_tensor(vec[:, BO:BO + 2], vec[:, BO:BO + 2], vec[:, S2:S2 + 2], ALU.mult)
            dve.drain()
            dve.tensor_tensor(vec[:, BE1:BE1 + 1], vec[:, BB1:BB1 + 1], vec[:, M1:M1 + 1], ALU.subtract)
            dve.tensor_tensor(vec[:, BE2:BE2 + 2], vec[:, BO:BO + 2], vec[:, BB2:BB2 + 2], ALU.add)
            dve.wait_ge(s("pe_prep"), 2)
            dve.tensor_copy(kwT, PP[1][:, 0:256].rearrange("p (c n) -> p c n", c=CC))
            dve.tensor_copy(kb, PP[1][:, 512:640])
            dve.drain()
            dve.sem_inc(s("dve_prep"), 1)
            dve.tensor_scalar(wqkv16[:, 0], wqkv_raw, WSCALE, None, ALU.mult)
            dve.drain()
            dve.scalar_tensor_tensor(out=wqkv16[:, 1], in0=wqkv_raw, scalar=WSCALE, in1=wqkv16[:, 0],
                                     op0=ALU.mult, op1=ALU.subtract)

            def statistics(src, out_sem):
                for t in range(NT):
                    dve.bn_stats(bst[:, t], src[:, t])
                dve.drain()
                deviations(out_sem)

            def deviations(out_sem):
                for t in range(NT):
                    dve.bn_aggr(mv[:, t], bst[:, t])
                dve.drain()
                dve.tensor_scalar(small[:, 1], mv[:, :, 1], EPS, None, ALU.add).then_inc(s(out_sem), 1)

            def part_statistics(part):
                dve.drain()
                for t in range(part * NT // 2, (part + 1) * NT // 2):
                    dve.bn_stats(bst[:, t], t1[:, t])

            def keep_k(n):
                dve.wait_ge(s("k_made"), n + 1)
                dve.tensor_tensor(kT.rearrange("p (t o) -> p t o", t=NT), PP[2][:, :]
                                  .rearrange("p (t o) -> p t o", t=NT),
                                  kb.unsqueeze(1).broadcast_to((P, NT, P)), ALU.add).then_inc(s("k_kept"), 1)

            def tokens(b, last):
                def scale_keys(i):
                    dve.wait_ge(s("exp_kept"), b * NT + (i + 1))
                    dve.reciprocal(rinv[:, i:i + 1], rsum[:, i:i + 1])
                    dve.drain()
                    if i >= 3:
                        dve.wait_ge(s("av_made"), b * NT + (i - 2))
                    dve.tensor_scalar(kTs[:, i % 3], kT[:, i * P:(i + 1) * P], rinv[:, i:i + 1], None,
                                      ALU.mult).then_inc(s("ks_kept"), 1)

                for i in range(NT):
                    dve.wait_ge(s("sc_made"), b * NT + (i + 1))
                    dve.tensor_reduce(nmax[:, i:i + 1], PP[i % 3][:, :], X_AXIS, ALU.max, negate=True)\
                       .then_inc(s("max_kept"), 1)
                    if i:
                        scale_keys(i - 1)
                scale_keys(NT - 1)
                dve.wait_ge(s("av_made"), b * NT + NT)
                for h in range(2):
                    n = slice(h * HALF, (h + 1) * HALF)
                    dve.tensor_scalar(y1[:, n], PP[3][:, n], vec[:, S1:S1 + 1], vec[:, BE1:BE1 + 1],
                                      ALU.mult, ALU.add).then_inc(s("y1_kept"), 1)
                for c in range(CC):
                    dve.wait_ge(s("cv_made"), b * 2 + (c + 1))
                    dve.scalar_tensor_tensor(out=X[:, c], in0=PP[c][:, :], scalar=vec[:, S2 + c:S2 + c + 1],
                                             in1=X[:, c], op0=ALU.mult, op1=ALU.add).then_inc(s("cv_kept"), 1)
                dve.wait_ge(s("tk_made"), FREE + b * 2 + 2)
                dve.wait_ge(s("st_v"), FREE + b * 16)
                dve.tensor_copy(tok[:, 4:8], PP[3][:, :].rearrange("p (t c) -> p t c", t=4))\
                   .then_inc(s("tk_kept_v"), 1)
                dve.drain()
                dve.wait_ge(s("tk_kept_a"), b + 1)
                statistics(tok, "stat_kept")
                dve.wait_ge(s("sd_kept"), b + 1)
                dve.reciprocal(small[:, 3], small[:, 2])
                dve.drain()
                dve.wait_ge(s("st_q0"), FREE + b * 64)
                dve.wait_ge(s("st_q1"), FREE + b * 64)
                for t in range(NT):
                    dve.tensor_scalar(ln[:, t], tok[:, t], mv[:, t, 0:1], small[:, 3, t:t + 1],
                                      ALU.subtract, ALU.mult).then_inc(s("ln_kept"), 1)
                if not last:
                    keep_k(b + 1)
                for c in range(CC):
                    dve.wait_ge(s("lnT_kept_a"), b * 2 + (c + 1))
                    dve.tensor_tensor(lnT[:, c, 1], PP[c][:, :], lnT[:, c, 0], ALU.subtract)\
                       .then_inc(s("lnT_kept_v"), 1)
                dve.wait_ge(s("ln_kept"), b * NT + NT)
                dve.tensor_tensor(tok, tok, bob.unsqueeze(1).broadcast_to((P, NT, C)), ALU.add)\
                   .then_inc(s("res0_kept"), 1)
                for u in range(4):
                    dve.wait_ge(s("qhi_kept"), FREE + b * 4 + (u + 1))
                    dve.scalar_tensor_tensor(out=qs[:, u % 2, 1], in0=PP[(u + 2) % 4][:, :],
                                             scalar=(C ** -0.5 if u < 2 else 1.0) / WSCALE, in1=qs[:, u % 2, 0],
                                             op0=ALU.mult, op1=ALU.subtract).then_inc(s("qlo_kept"), 1)
                dve.wait_ge(s("vt_made"), b * 2 + 2)
                dve.wait_ge(s("st_res0"), FREE + b * 16 + 16)
                dve.tensor_scalar(VT[:, 4:8], PP[3][:, :].rearrange("p (t c) -> p t c", t=4),
                                  1.0 / WSCALE, None, ALU.mult)\
                   .then_inc(s("vt_kept_v"), 1)

            keep_k(0)
            with dve.Fori(0, B - 1) as b:
                tokens(b, False)
            tokens(B - 1, True)

            uses = [0]

            def bank_made(before):
                at = uses[0]
                uses[0] += 1
                dve.wait_ge(s("c_made"), before + (at + 1))
                return shared_bank(at + parity(before))

            def reduce_half(n, k, before):
                dve.tensor_reduce(mxp[:, n, k:k + 1], bank_made(before), X_AXIS, ALU.max)\
                   .then_inc(s("c_kept"), 1)

            def join_halves(f):
                dve.drain()
                dve.tensor_reduce(mx[:, f], mxp[:, :, :], X_AXIS, ALU.max, negate=True)
                dve.drain()
                dve.tensor_scalar(mx[:, f], mx[:, f], 1.0 / MSCALE, None, ALU.mult).then_inc(s("nm_kept"), 1)

            def keep_row(before, moved, n):
                bank = bank_made(before)
                if moved:
                    dve.wait_ge(s(moved), n)
                dve.tensor_copy(nmr[:, :], bank[0:16, 0:P]).then_inc(s("c_kept"), 1)
                dve.drain()
                dve.sem_inc(s("nmr_kept"), 1)

            logit, oh1, oh2, val, rest, rk, tmp = [rt[:, i] for i in range(7)]

            def tail_project(c, before, n):
                bank = bank_made(before)
                if c == 0:
                    dve.wait_ge(s("ld_res0"), n * 16)
                dve.tensor_tensor(t1[:, 2 * c:2 * c + 2], bank.rearrange("p (t c) -> p t c", t=2),
                                  t1[:, 2 * c:2 * c + 2], ALU.add).then_inc(s("c_kept"), 1)

            def tail_rstd(n):
                dve.wait_ge(s("sd1_kept"), n)
                dve.reciprocal(small[:, 3], small[:, 2])
                dve.drain()
                dve.scalar_tensor_tensor(out=small[:, 4], in0=mv[:, :, 0], scalar=-1.0, in1=small[:, 3],
                                         op0=ALU.mult, op1=ALU.mult).then_inc(s("rstd_kept"), 1)

            def tail_turn(c, before):
                dve.tensor_copy(lnr[:, 2 * c:2 * c + 2], bank_made(before).bitcast(F16)
                                .rearrange("p (t s n) -> p t s n", t=2, s=4)).then_inc(s("c_kept"), 1)

            def tail_logits(before):
                bank = bank_made(before)[:, 0:NT * 2 * E].rearrange("p (t s e) -> p t s e", t=NT, s=2)
                dve.tensor_copy(tmp, bank[:, :, 1])
                dve.drain()
                dve.tensor_tensor(logit, bank[:, :, 0], tmp, ALU.add).then_inc(s("c_kept"), 1)

            def largest(src, top):
                dve.drain()
                dve.tensor_reduce(top, src, X_AXIS, ALU.max)
                dve.drain()
                dve.tensor_tensor(val, src, per_tile(top), ALU.is_equal)
                dve.drain()
                dve.tensor_tensor(val, val, per_expert(w8[:, :], NT), ALU.mult)

            def mark(one_hot):
                dve.drain()
                dve.tensor_reduce(rs[:, 3], val, X_AXIS, ALU.max)
                dve.drain()
                dve.tensor_tensor(one_hot, per_expert(w8[:, :], NT), per_tile(rs[:, 3]), ALU.is_equal)
                dve.drain()

            def tail_pick(part):
                if part == 0:
                    largest(logit, rs[:, 0])
                elif part == 1:
                    mark(oh1)
                    dve.scalar_tensor_tensor(out=rest, in0=oh1, scalar=-BIG, in1=logit, op0=ALU.mult, op1=ALU.add)
                elif part == 2:
                    largest(rest, rs[:, 1])
                else:
                    mark(oh2)
                    dve.tensor_tensor(rs[:, 2], rs[:, 1], rs[:, 0], ALU.subtract)
                    dve.tensor_tensor(pick16[:, :, :], oh1, oh2, ALU.add)
                    dve.drain()
                    dve.sem_inc(s("pick_kept"), 1)

            def tail_places(before, tail, n):
                bank = bank_made(before)
                dve.tensor_copy(rk, bank[:, 0:NT * E].rearrange("p (t e) -> p t e", e=E)).then_inc(s("c_kept"), 1)
                dve.tensor_reduce(chosen, pick16[:, :, :].rearrange("p t e -> p e t"), X_AXIS, ALU.add)
                dve.drain()
                dve.tensor_tensor(val, rk, per_expert(ebase[:, :], NT), ALU.add)
                dve.tensor_tensor(held16[:, :], held16[:, :], chosen, ALU.add)
                dve.drain()
                dve.tensor_tensor(tmp, val, oh1, ALU.mult)
                dve.tensor_tensor(rest, val, oh2, ALU.mult)
                dve.drain()
                dve.tensor_reduce(rs[:, 0], tmp, X_AXIS, ALU.add)
                dve.tensor_reduce(rs[:, 1], rest, X_AXIS, ALU.add)
                dve.drain()
                dve.wait_ge(s("listed"), n)
                dve.tensor_copy(row_place[:, :, 0:2], tok16[:, bass.ds(tail * NT, NT), :])
                dve.tensor_copy(idx[:, :, :], rs[:, 0:2]).then_inc(s("idx_kept"), 1)

            def tail_gates(tail, n):
                here = bass.ds(tail * NT, NT)
                dve.wait_ge(s("gexp_kept"), n)
                dve.tensor_scalar(rs[:, 3], rs[:, 2], 1.0, None, ALU.add)
                dve.drain()
                dve.reciprocal(rs[:, 4], rs[:, 3])
                dve.drain()
                dve.tensor_copy(gate1[:, here], rs[:, 4])
                dve.tensor_tensor(gate2[:, here], rs[:, 4], rs[:, 2], ALU.mult)
                dve.drain()

            def invert_sums(part, n):
                if part == 0:
                    dve.wait_ge(s("sum_kept"), FREE + (n + 1))
                here = slice(part * P, (part + 1) * P)
                op = dve.reciprocal(rin[:, here], rin[:, here])
                if part == 3:
                    op.then_inc(s("rin_kept"), 1)

            def attend(b, first):
                before = FIRST_USES if first else b * (2 * GROUP_USES + TAIL_USES) + (ROW_USES - TAIL_USES)
                uses[0] = 0
                for g in range(GROUPS):
                    for st in range(16):
                        f, j = st // 8, st % 8
                        halves = max_halves(st, first and g == 0)
                        few = len(halves) // 4
                        for n, k in halves[:2 * few]:
                            reduce_half(n, k, before)
                        if j in INVERT_AT and (not first or g * 2 + f > 0):
                            invert_sums(INVERT_AT.index(j), b * 4 + (g * 2 + f - 1))
                        for n, k in halves[2 * few:3 * few]:
                            reduce_half(n, k, before)
                        if st in ROW_AT:
                            keep_row(before, f"ld_nm{g}{f}", b * 16 + 16)
                        for n, k in halves[3 * few:]:
                            reduce_half(n, k, before)
                        if j == 3:
                            join_halves(1 - f)
                        at = g * 16 + st
                        if not first:
                            if at in PROJECT_AT:
                                tail_project(PROJECT_AT.index(at), before, b)
                            if at in STATS_AT:
                                part_statistics(STATS_AT.index(at))
                            if at == VAR_AT:
                                dve.drain()
                                deviations("stat1_kept")
                            if at == RSTD_AT:
                                tail_rstd(b)
                            if at in TURN_AT:
                                tail_turn(TURN_AT.index(at), before)
                            if at == LOGIT_AT:
                                tail_logits(before)
                            if at in PICK_AT:
                                tail_pick(PICK_AT.index(at))
                            if at == RANK_AT:
                                tail_places(before, b - 1, b)
                            if at == GATE_AT:
                                tail_gates(b - 1, b)

            for n in range(32):
                reduce_half(n // 2, n % 2, 0)
            join_halves(0)
            keep_row(0, None, 0)
            attend(0, True)
            with dve.Fori(1, B) as b:
                attend(b, False)
            for part in range(4):
                invert_sums(part, 4 * B - 1)
            before = B * (2 * GROUP_USES + TAIL_USES) + (ROW_USES - TAIL_USES)
            uses[0] = 0
            for c in range(4):
                tail_project(c, before, B)
            part_statistics(0)
            part_statistics(1)
            dve.drain()
            deviations("stat1_kept")
            tail_rstd(B)
            dve.drain()
            for t in range(NT):
                op = dve.tensor_scalar(ln32[:, t], t1[:, t], mv[:, t, 0:1], small[:, 3, t:t + 1],
                                       ALU.subtract, ALU.mult)
                if t % 2:
                    op.then_inc(s("ln1_kept"), 1)
            for part in range(2):
                here = slice(part * NT // 2, (part + 1) * NT // 2)
                dve.wait_ge(s("hi_kept"), B * 2 + (part - 1))
                dve.tensor_tensor(rows[:, here, 1, :], ln32[:, here], rows[:, here, 0, :], ALU.subtract)\
                   .then_inc(s("rows_kept"), 1)
            for c in range(4):
                tail_turn(c, before)
            tail_logits(before)
            for part in range(4):
                tail_pick(part)
            tail_places(before, B - 1, B)
            tail_gates(B - 1, B)
            dve.wait_ge(s("idx_kept"), FREE + B)
            dve.sem_inc(s("phase_b"), 1)

            dve.wait_ge(s("zero_kept"), 1)
            dve.wait_ge(s("cnt_made"), 1)
            dve.wait_ge(s("ld_b2"), 16)
            dve.tensor_copy(cnt, PP[0][:, 0:E])
            dve.tensor_copy(seqc, seq.bitcast(I32))
            dve.drain()
            over = cmp[:, 0:B * N // TT]
            dve.tensor_tensor(over, per_expert(cnt, B * N // TT), per_tile(thr), ALU.is_gt)
            dve.tensor_tensor(zrowf, cnt, ebase[:, :], ALU.add)
            dve.drain()
            dve.tensor_reduce(lists, over.rearrange("p k e -> p e k"), X_AXIS, ALU.add)
            dve.tensor_copy(zrow, zrowf)
            dve.drain()
            dve.tensor_tensor_scan(incl, one8, lists, 0.0, ALU.mult, ALU.add)
            dve.drain()
            dve.tensor_tensor(start, incl, lists, ALU.subtract)
            dve.tensor_scalar(seq, incl[:, E - 1:E].broadcast_to((P, TABLE)), -1.0, None, ALU.add)
            dve.drain()
            dve.tensor_tensor(seqc, seqc, seq, ALU.min)
            dve.drain()
            dve.tensor_tensor(cmp, per_expert(incl, TABLE), per_tile(seqc), ALU.is_le)
            dve.drain()
            dve.tensor_reduce(te, cmp, X_AXIS, ALU.add)
            dve.drain()
            dve.tensor_tensor(cmp, cmp, per_expert(lists, TABLE), ALU.mult)
            dve.drain()
            dve.tensor_reduce(tk, cmp, X_AXIS, ALU.add)
            dve.drain()
            dve.tensor_tensor(tk, seqc, tk, ALU.subtract)
            dve.tensor_copy(tile_e, te)
            dve.drain()
            dve.tensor_scalar(tk, tk, float(TT), None, ALU.mult)
            dve.drain()
            dve.scalar_tensor_tensor(out=tk, in0=te, scalar=float(REGION), in1=tk, op0=ALU.mult, op1=ALU.add)
            dve.drain()
            dve.tensor_copy(tile_row, tk)
            dve.drain()
            dve.sem_inc(s("table_kept"), 1)
            def keep_turned(t, u):
                dve.wait_ge(s("xT_made"), t + 1)
                dve.tensor_copy(xT[u].rearrange("p s n -> p (s n)"), turned_bank(u)).then_inc(s("xT_kept"), 1)

            def split_hidden(t, u):
                for j in range(HC // 2):
                    dve.wait_ge(s("h_kept"), t * HC + (2 * j + 2))
                    k = slice(2 * j, 2 * j + 2)
                    dve.tensor_copy(hs[u][:, 0, k], hid[u][:, k])
                    dve.drain()
                    dve.tensor_tensor(hs[u][:, 1, k], hid[u][:, k], hs[u][:, 0, k], ALU.subtract)\
                       .then_inc(s("hs_kept"), 1)

            def keep_places(u):
                dve.tensor_reduce(placef[:, u], xs_place[u], X_AXIS, ALU.add)\
                   .then_inc(s("places_kept"), 1)

            def keep_output(t, u, e):
                dve.wait_ge(s("y_made"), FREE + t + 1)
                dve.wait_ge(s("y_out"), FREE + t)
                dve.tensor_copy(place[:, u], placef[:, u])
                dve.drain()
                dve.scalar_tensor_tensor(
                    out=ysb[u], in0=PP[2][:, u * HALF:(u + 1) * HALF].rearrange("p (a c) -> p a c", a=2),
                    scalar=1.0 / WSCALE, in1=b2b[:, bass.ds(e, 1), :].broadcast_to((P, 2, C)),
                    op0=ALU.mult, op1=ALU.add).then_inc(s("y_kept"), 1)

            def expert(at):
                return dve.value_load(tile_e[0:1, at], min_val=0, max_val=E - 1)

            keep_turned(0, 0)
            keep_places(0)
            split_hidden(0, 0)
            keep_turned(1, 1)
            keep_places(1)
            with dve.Fori(0, (TILES - 1) // 2) as i:
                e0 = expert(bass.ds(i * 2, 1))
                e1 = expert(bass.ds(i * 2 + 1, 1))
                dve.wait_ge(s("y_made"), FREE + i * 2)
                split_hidden(i * 2 + 1, 1)
                keep_turned(i * 2 + 2, 0)
                keep_output(i * 2, 0, e0)
                keep_places(0)
                dve.wait_ge(s("y_made"), FREE + i * 2 + 1)
                split_hidden(i * 2 + 2, 0)
                keep_turned(i * 2 + 3, 1)
                keep_output(i * 2 + 1, 1, e1)
                keep_places(1)
            keep_output(TILES - 1, 0, expert(slice(TILES - 1, TILES)))

            with dve.Fori(0, 2 * B // 4) as i:
                for u in range(4):
                    if u % 2 == 0:
                        here = bass.ds((i * 2 + u // 2) * NT, NT)
                        dve.tensor_copy(rs[:, 0], gate1[:, here])
                        dve.tensor_copy(rs[:, 1], gate2[:, here])
                        dve.drain()
                    dve.wait_ge(s(f"ld_y{u}"), i * 32 + 32)
                    dve.wait_ge(s(f"ld_t{u}"), i * 16 + 16)
                    for k in range(2):
                        for t in range(4):
                            g = (u % 2) * 4 + t
                            last = dve.scalar_tensor_tensor(
                                out=tf[u][:, t], in0=yg[u][:, k, t], scalar=rs[:, k, g:g + 1],
                                in1=tf[u][:, t], op0=ALU.mult, op1=ALU.add)
                        if k == 0:
                            dve.drain()
                    last.then_inc(s("f_kept"), 1)
                    dve.drain()


_INS = ["x", "L0_conv_wk", "L0_conv_bk", "L0_conv_wv", "L0_conv_bv", "L0_conv_wq", "L0_conv_bq",
        "L0_conv_wwg", "L0_conv_bn1_g", "L0_conv_bn1_b", "L0_conv_bn1_m", "L0_conv_bn1_v",
        "L0_conv_wout", "L0_conv_bout", "L0_conv_bn2_g", "L0_conv_bn2_b", "L0_conv_bn2_m",
        "L0_conv_bn2_v", "L1_attn_w_qkv", "L1_attn_w_out", "L1_attn_b_out", "L1_ffn_Wr",
        "L1_ffn_W1", "L1_ffn_b1", "L1_ffn_W2", "L1_ffn_b2"]
_OUTS = [((4, 256, 32, 32), "float32")]


def kernel(**inputs):
    import numpy as _np
    import concourse.bacc as _bacc
    from concourse import mybir as _mybir
    from concourse.bass_utils import run_bass_kernel_spmd as _run

    nc = _bacc.Bacc("TRN2", target_bir_lowering=False, num_devices=1)
    arrays, args = {}, []
    for name in _INS:
        a = _np.ascontiguousarray(inputs[name])
        arrays[f"in_{name}_dram"] = a
        args.append(nc.dram_tensor(f"in_{name}_dram", a.shape, _mybir.dt.from_np(a.dtype), kind="ExternalInput").ap())
    for i, (shape, dtype) in enumerate(_OUTS):
        dt = _mybir.dt.from_np(_np.dtype(dtype))
        args.append(nc.dram_tensor(f"out_{i}_dram", shape, dt, kind="ExternalOutput").ap())
    hybrid_block(nc, *args)
    r = _run(nc, [arrays], core_ids=[0])
    return r.results[0]["out_0_dram"]
```
